# Optimizing a Trainium2 kernel written in Bass

```python
import numpy as np
import jax
import jax.numpy as jnp

def _softmax(x, axis=-1):
    return jax.nn.softmax(x, axis=axis)

def _gelu(x):
    return jax.nn.gelu(x, approximate=True)

def _silu(x):
    return jax.nn.silu(x)

def _sigmoid(x):
    return jax.nn.sigmoid(x)

def _layernorm(x, axis=-1, eps=1e-05):
    m = jnp.mean(x, axis=axis, keepdims=True)
    v = jnp.var(x, axis=axis, keepdims=True)
    return (x - m) / jnp.sqrt(v + eps)

def _scatter_add(tgt, idx, src, axis=0):
    return tgt.at[idx].add(src)

def _segment_sum(src, seg, n):
    return jax.ops.segment_sum(src, seg, n)
kernel_name = 'mk_decoder_postln_d1_seqx_r4_447093'

def setup_inputs(seed: int=0):
    np.random.seed(seed)
    _w = jnp.asarray

    def _rec_inputs():
        import jax
        import jax.numpy as jnp
        _rk = jax.random.key(seed)
        x = 7.22e-05 + 1 * jax.random.normal(jax.random.fold_in(_rk, 1), (2, 1024, 256), jnp.float32)
        _lenS = 1024 - jax.random.randint(jax.random.fold_in(_rk, 7), (2,), 0, max(1, 1024 // 4) + 1, jnp.int32)
        _lenS2 = 64 - jax.random.randint(jax.random.fold_in(_rk, 8), (2,), 0, max(1, 64 // 4) + 1, jnp.int32)
        _ctx_1024P = jax.random.normal(jax.random.fold_in(_rk, 11), (2, 16, 256), jnp.float32)
        _ctx_1024c = jax.random.dirichlet(jax.random.fold_in(_rk, 511), 0.3 * jnp.ones((16,), jnp.float32), (2, 64))
        _ctx_1024t = jnp.einsum('bsk,bkd->bsd', _ctx_1024c, _ctx_1024P)
        _ctx_1024t = _ctx_1024t * jax.lax.rsqrt(jnp.mean(jnp.square(_ctx_1024t)) + 1e-12) * 0.953939
        ctx_1024 = -1.39393e-06 + 0.999914 * (_ctx_1024t + 0.3 * jax.random.normal(jax.random.fold_in(_rk, 611), (2, 64, 256), jnp.float32))
        return (x, ctx_1024)
    x, ctx_1024 = _rec_inputs()

    def _L0_attn_setup():
        import jax, jax.numpy as jnp
        import numpy as np
        B, L, D_MODEL = (4, 512, 256)
        EXPAND = 2
        D_INNER = EXPAND * D_MODEL
        D_STATE = 16
        D_CONV = 4
        DT_RANK = (D_MODEL + 15) // 16
        EPS = 1e-05

        def _rmsnorm(x, w):
            return x * jax.lax.rsqrt(jnp.mean(x * x, axis=-1, keepdims=True) + EPS) * w

        def _causal_depthwise_conv(x, w, b):
            xp = jnp.pad(x, ((0, 0), (0, 0), (D_CONV - 1, 0)))
            y = jax.lax.conv_general_dilated(xp, w[:, None, :], window_strides=(1,), padding='VALID', dimension_numbers=('NCH', 'OIH', 'NCH'), feature_group_count=D_INNER)
            return y + b[None, :, None]

        def _selective_scan(u, delta, A, Bm, Cm, D):

            def step(s, inp):
                d_t, B_t, C_t, u_t = inp
                dA = jnp.exp(d_t[..., None] * A)
                dBu = d_t[..., None] * B_t[:, None, :] * u_t[..., None]
                s = s * dA + dBu
                y = jnp.einsum('bds,bs->bd', s, C_t)
                return (s, y)
            s0 = jnp.zeros((u.shape[0], D_INNER, D_STATE), u.dtype)
            xs = (delta.swapaxes(0, 1), Bm.swapaxes(0, 1), Cm.swapaxes(0, 1), u.swapaxes(0, 1))
            _, ys = jax.lax.scan(step, s0, xs)
            return ys.swapaxes(0, 1) + u * D
        key = jax.random.key(seed)
        ks = jax.random.split(key, 10)
        s = 0.02
        return {'x': jax.random.normal(ks[0], (B, L, D_MODEL), jnp.float32), 'norm_w': jnp.ones((D_MODEL,), jnp.float32), 'in_proj_w': jax.random.normal(ks[1], (2 * D_INNER, D_MODEL), jnp.float32) * s, 'conv_w': jax.random.normal(ks[2], (D_INNER, D_CONV), jnp.float32) * s, 'conv_b': jnp.zeros((D_INNER,), jnp.float32), 'x_proj_w': jax.random.normal(ks[3], (DT_RANK + 2 * D_STATE, D_INNER), jnp.float32) * s, 'dt_proj_w': jax.random.normal(ks[4], (D_INNER, DT_RANK), jnp.float32) * s, 'dt_proj_b': jnp.log(jnp.expm1(jnp.full((D_INNER,), 0.01, jnp.float32))), 'A_log': jnp.log(jnp.broadcast_to(jnp.arange(1, D_STATE + 1, dtype=jnp.float32), (D_INNER, D_STATE))), 'D': jnp.ones((D_INNER,), jnp.float32), 'out_proj_w': jax.random.normal(ks[5], (D_MODEL, D_INNER), jnp.float32) * s}
    _L0_attn_all = _L0_attn_setup()
    _L0_attn_in = {k: v for k, v in _L0_attn_all.items() if k in ('norm_w', 'in_proj_w', 'conv_w', 'conv_b', 'x_proj_w', 'dt_proj_w', 'dt_proj_b', 'A_log', 'D', 'out_proj_w')}
    del _L0_attn_all

    def _L0_xattn_setup():
        import jax, jax.numpy as jnp
        import numpy as np
        DIM = 256
        NH = 8
        HD = DIM // NH
        E = 8
        EPS = 1e-05

        def rope_cos_sin(L, hd):
            inv_freq = 1.0 / 10000.0 ** (jnp.arange(0, hd, 2, dtype=jnp.float32) / hd)
            freqs = jnp.arange(L, dtype=jnp.float32)[:, None] * inv_freq[None, :]
            emb = jnp.concatenate([freqs, freqs], axis=-1)
            return (jnp.cos(emb), jnp.sin(emb))

        def rotate_half(x):
            x1 = x[..., 0::2]
            x2 = x[..., 1::2]
            return jnp.stack((-x2, x1), axis=-1).reshape(x.shape)

        def rope(t, cos, sin):
            return t * cos[None, None] + rotate_half(t) * sin[None, None]

        def heads(t):
            B, L, C = t.shape
            return t.reshape(B, L, NH, HD).transpose(0, 2, 1, 3)
        key = jax.random.key(seed)
        ks = jax.random.split(key, 32)
        std = 0.02
        d = {}
        d['x'] = jax.random.normal(ks[0], (16, 128, DIM), jnp.float32)
        d['h_a'] = jax.random.normal(ks[1], (16, 64, DIM), jnp.float32)
        d['h_t'] = jax.random.normal(ks[2], (16, 64, DIM), jnp.float32)
        names = ['qa', 'ka', 'va', 'qt', 'kt', 'vt', 'o', 'ffn']
        for i, n in enumerate(names):
            d['W_' + n] = jax.random.normal(ks[3 + 2 * i], (E, DIM, DIM), jnp.float32) * std
            d['b_' + n] = jax.random.normal(ks[4 + 2 * i], (E, DIM), jnp.float32) * std
        d['gamma'] = jnp.ones((E, DIM), jnp.float32)
        d['beta'] = jnp.zeros((E, DIM), jnp.float32)
        d['gating_factor'] = jnp.zeros((E,), jnp.float32)
        d['expert_idx'] = 3
        return d
    _L0_xattn_all = _L0_xattn_setup()
    _L0_xattn_in = {k: v for k, v in _L0_xattn_all.items() if k in ('W_qa', 'b_qa', 'W_ka', 'b_ka', 'W_va', 'b_va', 'W_qt', 'b_qt', 'W_kt', 'b_kt', 'W_vt', 'b_vt', 'W_o', 'b_o', 'W_ffn', 'b_ffn', 'gamma', 'beta', 'gating_factor')}
    del _L0_xattn_all

    def _L0_ffn_setup():
        import jax, jax.numpy as jnp
        import numpy as np
        from jax import lax
        D_MODEL = 256
        INTER = 256
        N_EXPERTS = 8
        TOP_K = 2
        ROUTE_SCALE = 1.0
        B, S = (2, 1024)
        key = jax.random.key(seed)
        ks = jax.random.split(key, 16)
        sc_d = 1.0 / np.sqrt(D_MODEL)
        sc_f = 1.0 / np.sqrt(INTER)
        inp = {'x': jax.random.normal(ks[0], (B, S, D_MODEL), dtype=jnp.float32), 'gate_w': jax.random.normal(ks[1], (N_EXPERTS, D_MODEL), dtype=jnp.float32) * sc_d, 'w1': jax.random.normal(ks[2], (N_EXPERTS, D_MODEL, INTER), dtype=jnp.float32) * sc_d, 'b1': jnp.zeros((N_EXPERTS, INTER), dtype=jnp.float32), 'w2': jax.random.normal(ks[3], (N_EXPERTS, INTER, D_MODEL), dtype=jnp.float32) * sc_f, 'b2': jnp.zeros((N_EXPERTS, D_MODEL), dtype=jnp.float32), 'w3': jax.random.normal(ks[4], (N_EXPERTS, D_MODEL, INTER), dtype=jnp.float32) * sc_d, 'b3': jnp.zeros((N_EXPERTS, INTER), dtype=jnp.float32), 'sw1': jax.random.normal(ks[5], (D_MODEL, INTER), dtype=jnp.float32) * sc_d, 'sb1': jnp.zeros((INTER,), dtype=jnp.float32), 'sw2': jax.random.normal(ks[6], (INTER, D_MODEL), dtype=jnp.float32) * sc_f, 'sb2': jnp.zeros((D_MODEL,), dtype=jnp.float32), 'sw3': jax.random.normal(ks[7], (D_MODEL, INTER), dtype=jnp.float32) * sc_d, 'sb3': jnp.zeros((INTER,), dtype=jnp.float32)}
        return inp
    _L0_ffn_all = _L0_ffn_setup()
    _L0_ffn_in = {k: v for k, v in _L0_ffn_all.items() if k in ('gate_w', 'w1', 'b1', 'w2', 'b2', 'w3', 'b3', 'sw1', 'sb1', 'sw2', 'sb2', 'sw3', 'sb3')}
    del _L0_ffn_all
    return {'x': x, 'ctx_1024': ctx_1024, 'L0_attn_norm_w': _L0_attn_in['norm_w'], 'L0_attn_in_proj_w': _L0_attn_in['in_proj_w'], 'L0_attn_conv_w': _L0_attn_in['conv_w'], 'L0_attn_conv_b': _L0_attn_in['conv_b'], 'L0_attn_x_proj_w': _L0_attn_in['x_proj_w'], 'L0_attn_dt_proj_w': _L0_attn_in['dt_proj_w'], 'L0_attn_dt_proj_b': _L0_attn_in['dt_proj_b'], 'L0_attn_A_log': _L0_attn_in['A_log'], 'L0_attn_D': _L0_attn_in['D'], 'L0_attn_out_proj_w': _L0_attn_in['out_proj_w'], 'L0_xattn_W_qa': _L0_xattn_in['W_qa'], 'L0_xattn_b_qa': _L0_xattn_in['b_qa'], 'L0_xattn_W_ka': _L0_xattn_in['W_ka'], 'L0_xattn_b_ka': _L0_xattn_in['b_ka'], 'L0_xattn_W_va': _L0_xattn_in['W_va'], 'L0_xattn_b_va': _L0_xattn_in['b_va'], 'L0_xattn_W_qt': _L0_xattn_in['W_qt'], 'L0_xattn_b_qt': _L0_xattn_in['b_qt'], 'L0_xattn_W_kt': _L0_xattn_in['W_kt'], 'L0_xattn_b_kt': _L0_xattn_in['b_kt'], 'L0_xattn_W_vt': _L0_xattn_in['W_vt'], 'L0_xattn_b_vt': _L0_xattn_in['b_vt'], 'L0_xattn_W_o': _L0_xattn_in['W_o'], 'L0_xattn_b_o': _L0_xattn_in['b_o'], 'L0_xattn_W_ffn': _L0_xattn_in['W_ffn'], 'L0_xattn_b_ffn': _L0_xattn_in['b_ffn'], 'L0_xattn_gamma': _L0_xattn_in['gamma'], 'L0_xattn_beta': _L0_xattn_in['beta'], 'L0_xattn_gating_factor': _L0_xattn_in['gating_factor'], 'L0_ffn_gate_w': _L0_ffn_in['gate_w'], 'L0_ffn_w1': _L0_ffn_in['w1'], 'L0_ffn_b1': _L0_ffn_in['b1'], 'L0_ffn_w2': _L0_ffn_in['w2'], 'L0_ffn_b2': _L0_ffn_in['b2'], 'L0_ffn_w3': _L0_ffn_in['w3'], 'L0_ffn_b3': _L0_ffn_in['b3'], 'L0_ffn_sw1': _L0_ffn_in['sw1'], 'L0_ffn_sb1': _L0_ffn_in['sb1'], 'L0_ffn_sw2': _L0_ffn_in['sw2'], 'L0_ffn_sb2': _L0_ffn_in['sb2'], 'L0_ffn_sw3': _L0_ffn_in['sw3'], 'L0_ffn_sb3': _L0_ffn_in['sb3']}

def reference(x, ctx_1024, L0_attn_norm_w, L0_attn_in_proj_w, L0_attn_conv_w, L0_attn_conv_b, L0_attn_x_proj_w, L0_attn_dt_proj_w, L0_attn_dt_proj_b, L0_attn_A_log, L0_attn_D, L0_attn_out_proj_w, L0_xattn_W_qa, L0_xattn_b_qa, L0_xattn_W_ka, L0_xattn_b_ka, L0_xattn_W_va, L0_xattn_b_va, L0_xattn_W_qt, L0_xattn_b_qt, L0_xattn_W_kt, L0_xattn_b_kt, L0_xattn_W_vt, L0_xattn_b_vt, L0_xattn_W_o, L0_xattn_b_o, L0_xattn_W_ffn, L0_xattn_b_ffn, L0_xattn_gamma, L0_xattn_beta, L0_xattn_gating_factor, L0_ffn_gate_w, L0_ffn_w1, L0_ffn_b1, L0_ffn_w2, L0_ffn_b2, L0_ffn_w3, L0_ffn_b3, L0_ffn_sw1, L0_ffn_sb1, L0_ffn_sw2, L0_ffn_sb2, L0_ffn_sw3, L0_ffn_sb3):
    import jax
    import jax.numpy as jnp

    def _L0_attn_ref(x, norm_w, in_proj_w, conv_w, conv_b, x_proj_w, dt_proj_w, dt_proj_b, A_log, D, out_proj_w):
        import jax, jax.numpy as jnp
        import numpy as np
        B, L, D_MODEL = (4, 512, 256)
        EXPAND = 2
        D_INNER = EXPAND * D_MODEL
        D_STATE = 16
        D_CONV = 4
        DT_RANK = (D_MODEL + 15) // 16
        EPS = 1e-05

        def _rmsnorm(x, w):
            return x * jax.lax.rsqrt(jnp.mean(x * x, axis=-1, keepdims=True) + EPS) * w

        def _causal_depthwise_conv(x, w, b):
            xp = jnp.pad(x, ((0, 0), (0, 0), (D_CONV - 1, 0)))
            y = jax.lax.conv_general_dilated(xp, w[:, None, :], window_strides=(1,), padding='VALID', dimension_numbers=('NCH', 'OIH', 'NCH'), feature_group_count=D_INNER)
            return y + b[None, :, None]

        def _selective_scan(u, delta, A, Bm, Cm, D):

            def step(s, inp):
                d_t, B_t, C_t, u_t = inp
                dA = jnp.exp(d_t[..., None] * A)
                dBu = d_t[..., None] * B_t[:, None, :] * u_t[..., None]
                s = s * dA + dBu
                y = jnp.einsum('bds,bs->bd', s, C_t)
                return (s, y)
            s0 = jnp.zeros((u.shape[0], D_INNER, D_STATE), u.dtype)
            xs = (delta.swapaxes(0, 1), Bm.swapaxes(0, 1), Cm.swapaxes(0, 1), u.swapaxes(0, 1))
            _, ys = jax.lax.scan(step, s0, xs)
            return ys.swapaxes(0, 1) + u * D
        h = _rmsnorm(x, norm_w)
        xz = jnp.einsum('bld,ed->ble', h, in_proj_w)
        xi, z = jnp.split(xz, 2, axis=-1)
        xi = _causal_depthwise_conv(xi.swapaxes(1, 2), conv_w, conv_b).swapaxes(1, 2)
        xi = jax.nn.silu(xi)
        x_dbl = jnp.einsum('bld,ed->ble', xi, x_proj_w)
        dt, Bm, Cm = jnp.split(x_dbl, [DT_RANK, DT_RANK + D_STATE], axis=-1)
        delta = jax.nn.softplus(jnp.einsum('blr,dr->bld', dt, dt_proj_w) + dt_proj_b)
        A = -jnp.exp(A_log)
        y = _selective_scan(xi, delta, A, Bm, Cm, D)
        y = y * jax.nn.silu(z)
        out = jnp.einsum('bld,ed->ble', y, out_proj_w)
        return out + x

    def _L0_xattn_ref(x, h_a, h_t, W_qa, b_qa, W_ka, b_ka, W_va, b_va, W_qt, b_qt, W_kt, b_kt, W_vt, b_vt, W_o, b_o, W_ffn, b_ffn, gamma, beta, gating_factor, expert_idx):
        import jax, jax.numpy as jnp
        import numpy as np
        DIM = 256
        NH = 8
        HD = DIM // NH
        E = 8
        EPS = 1e-05

        def rope_cos_sin(L, hd):
            inv_freq = 1.0 / 10000.0 ** (jnp.arange(0, hd, 2, dtype=jnp.float32) / hd)
            freqs = jnp.arange(L, dtype=jnp.float32)[:, None] * inv_freq[None, :]
            emb = jnp.concatenate([freqs, freqs], axis=-1)
            return (jnp.cos(emb), jnp.sin(emb))

        def rotate_half(x):
            x1 = x[..., 0::2]
            x2 = x[..., 1::2]
            return jnp.stack((-x2, x1), axis=-1).reshape(x.shape)

        def rope(t, cos, sin):
            return t * cos[None, None] + rotate_half(t) * sin[None, None]

        def heads(t):
            B, L, C = t.shape
            return t.reshape(B, L, NH, HD).transpose(0, 2, 1, 3)
        e = expert_idx

        def lin(t, W, b):
            return t @ W[e].T + b[e]
        B, T, C = x.shape
        Ka = h_a.shape[1]
        Kt = h_t.shape[1]
        q_a = heads(lin(x, W_qa, b_qa))
        q_t = heads(lin(x, W_qt, b_qt))
        k_a = heads(lin(h_a, W_ka, b_ka))
        v_a = heads(lin(h_a, W_va, b_va))
        k_t = heads(lin(h_t, W_kt, b_kt))
        v_t = heads(lin(h_t, W_vt, b_vt))
        cos_m, sin_m = rope_cos_sin(T, HD)
        q_a = rope(q_a, cos_m, sin_m)
        q_t = rope(q_t, cos_m, sin_m)
        cos_a, sin_a = rope_cos_sin(Ka, HD)
        k_a = rope(k_a, cos_a, sin_a)
        cos_t, sin_t = rope_cos_sin(Kt, HD)
        k_t = rope(k_t, cos_t, sin_t)
        ratio_g = jax.nn.sigmoid(gating_factor[e])
        s_a = jnp.einsum('bhtd,bhkd->bhtk', q_a, k_a)
        s_t = jnp.einsum('bhtd,bhkd->bhtk', q_t, k_t) * ratio_g
        scores = jnp.concatenate([s_a, s_t], axis=-1) / np.sqrt(HD)
        w = jax.nn.softmax(scores, axis=-1)
        v = jnp.concatenate([v_a, v_t], axis=2)
        out = jnp.einsum('bhtk,bhkd->bhtd', w, v)
        out = out.transpose(0, 2, 1, 3).reshape(B, T, C)
        out = lin(out, W_o, b_o)
        x = out + x
        mu = jnp.mean(x, axis=-1, keepdims=True)
        var = jnp.var(x, axis=-1, keepdims=True)
        xn = (x - mu) / jnp.sqrt(var + EPS) * gamma[e] + beta[e]
        x = jax.nn.relu(lin(xn, W_ffn, b_ffn))
        return x

    def _L0_ffn_ref(x, gate_w, w1, b1, w2, b2, w3, b3, sw1, sb1, sw2, sb2, sw3, sb3):
        import jax, jax.numpy as jnp
        import numpy as np
        from jax import lax
        D_MODEL = 256
        INTER = 256
        N_EXPERTS = 8
        TOP_K = 2
        ROUTE_SCALE = 1.0
        B, S = (2, 1024)
        Bx, Sx, D = x.shape
        xt = x.reshape(-1, D)
        scores = jax.nn.softmax((xt @ gate_w.T).astype(jnp.float32), axis=-1)
        top_vals, top_idx = lax.top_k(scores, TOP_K)
        weights = (top_vals * ROUTE_SCALE).astype(x.dtype)
        combine = jnp.sum(jax.nn.one_hot(top_idx, N_EXPERTS, dtype=x.dtype) * weights[..., None], axis=1)

        def body(acc, p):
            W1, B1, W2, B2, W3, B3, c = p
            h = jax.nn.silu(xt @ W1 + B1) * (xt @ W3 + B3)
            return (acc + c[:, None] * (h @ W2 + B2), None)
        y, _ = lax.scan(body, jnp.zeros_like(xt), (w1, b1, w2, b2, w3, b3, combine.T))
        z = jax.nn.silu(xt @ sw1 + sb1) * (xt @ sw3 + sb3) @ sw2 + sb2
        return (y + z).reshape(Bx, Sx, D)
    x = _layernorm(x + _L0_attn_ref(x, L0_attn_norm_w, L0_attn_in_proj_w, L0_attn_conv_w, L0_attn_conv_b, L0_attn_x_proj_w, L0_attn_dt_proj_w, L0_attn_dt_proj_b, L0_attn_A_log, L0_attn_D, L0_attn_out_proj_w), axis=-1)
    x = _layernorm(x + _L0_xattn_ref(x, ctx_1024, ctx_1024, L0_xattn_W_qa, L0_xattn_b_qa, L0_xattn_W_ka, L0_xattn_b_ka, L0_xattn_W_va, L0_xattn_b_va, L0_xattn_W_qt, L0_xattn_b_qt, L0_xattn_W_kt, L0_xattn_b_kt, L0_xattn_W_vt, L0_xattn_b_vt, L0_xattn_W_o, L0_xattn_b_o, L0_xattn_W_ffn, L0_xattn_b_ffn, L0_xattn_gamma, L0_xattn_beta, L0_xattn_gating_factor, 3), axis=-1)
    x = _layernorm(x + _L0_ffn_ref(x, L0_ffn_gate_w, L0_ffn_w1, L0_ffn_b1, L0_ffn_w2, L0_ffn_b2, L0_ffn_w3, L0_ffn_b3, L0_ffn_sw1, L0_ffn_sb1, L0_ffn_sw2, L0_ffn_sb2, L0_ffn_sw3, L0_ffn_sb3), axis=-1)
    return x

_drawn_inputs = setup_inputs


def setup_inputs(seed=0):
    import zlib

    import numpy as np

    out = dict(_drawn_inputs(seed))
    spreads = {'L0_attn_norm_w': (1.0, 0.6),
     'L0_attn_conv_b': (0.0, 0.8),
     'L0_attn_dt_proj_b': (-4.600166320800781, 0.6),
     'L0_attn_D': (1.0, 0.6),
     'L0_xattn_gamma': (1.0, 0.2),
     'L0_xattn_beta': (0.0, 0.1),
     'L0_xattn_gating_factor': (0.0, 0.8),
     'L0_ffn_b1': (0.0, 0.347),
     'L0_ffn_b2': (0.0, 0.1),
     'L0_ffn_b3': (0.0, 0.363),
     'L0_ffn_sb1': (0.0, 0.1),
     'L0_ffn_sb2': (0.0, 0.1),
     'L0_ffn_sb3': (0.0, 0.1)}
    factors = {'ctx_1024': 3.767,
     'L0_attn_in_proj_w': 8.0,
     'L0_attn_conv_w': 8.0,
     'L0_attn_x_proj_w': 8.0,
     'L0_attn_dt_proj_w': 8.0,
     'L0_attn_A_log': 8.0,
     'L0_attn_out_proj_w': 7.794,
     'L0_xattn_W_qa': 8.0,
     'L0_xattn_b_qa': 8.0,
     'L0_xattn_W_ka': 8.0,
     'L0_xattn_b_ka': 29.477,
     'L0_xattn_W_va': 4.424,
     'L0_xattn_b_va': 39.984,
     'L0_xattn_W_qt': 8.0,
     'L0_xattn_b_qt': 8.0,
     'L0_xattn_W_kt': 8.0,
     'L0_xattn_b_kt': 56.756,
     'L0_xattn_W_vt': 4.647,
     'L0_xattn_b_vt': 63.363,
     'L0_xattn_W_o': 3.339,
     'L0_xattn_b_o': 38.065,
     'L0_xattn_b_ffn': 2.734}
    for name, (base, spread) in spreads.items():
        noise = np.random.default_rng([zlib.crc32(name.encode()), seed]).standard_normal(out[name].shape)
        drawn = base * np.exp(spread * noise) if base else spread * noise
        out[name] = jnp.asarray(drawn.astype(out[name].dtype))
    for name, factor in factors.items():
        out[name] = (out[name] * factor).astype(out[name].dtype)
    return out
```

```python
from contextlib import ExitStack

import numpy as np

import concourse.bass as bass
from concourse import mybir

F32 = mybir.dt.float32
I32 = mybir.dt.int32
U32 = mybir.dt.uint32
ALU = mybir.AluOpType
ACT = mybir.ActivationFunctionType
AX = mybir.AxisListType

P = 128
SEQS, SEQ = 2, 1024
DM = 256
KD = DM // P
DI = 2 * DM
Q = DI // P
NS = 16
RANK = 16
TAPS = 4
TC = 512
NT = TC // P
CHUNKS = SEQS * SEQ // TC
CPS = SEQ // TC
HEADS, HD = 8, 32
HB = HEADS // 2
CTX = 64
KEYS = 2 * CTX
EXPERTS = 8
ALL = EXPERTS + 1
WRING, CRING = 2, 3
EPS = 1e-5
LINEAR = 30.0

VEC = {}
_at = 0
for _name, _n in (("norm_w", KD), ("conv_w", Q * TAPS), ("conv_b", Q), ("dt_b", Q), ("skip", Q), ("A_log", Q * NS),
                  ("bq", HB), ("bq_swap", HB), ("bk", HB), ("bk_swap", HB), ("gamma", KD), ("beta", KD),
                  ("b1", ALL * KD), ("b3", ALL * KD), ("gate", 1)):
    VEC[_name] = (_at, _at + _n)
    _at += _n
VECS = _at

T_X1T, T_Q, T_S, T_PT = 0, 1, 3, 4
T_O3, T_RES3, T_LNT, T_FFN, T_GATE, T_COMB, T_EXP = 11, 12, 13, 14, 15, 16, 17
T_OUT = T_EXP + 2 * ALL + 1
PRE_TICKS = 4


def schedule():
    steps = [("pre", 0), ("am", 0), ("pre", 1), ("am", 1), ("pre", 2), ("am", 2), ("pre", 3), ("am", 3)]
    t = PRE_TICKS
    for n in range(NS):
        for half in range(2):
            steps += [("scan", n, half), ("am", t)]
            t += 1
    steps.append(("scan_end",))
    steps.append(("post",))
    steps += [("am", k) for k in range(t, T_OUT + 1)]
    return steps


SCHEDULE = schedule()


class Signal:

    def __init__(self, sem, per):
        self.sem, self.per = sem, per

    def at(self, j, k):
        return self.sem, j * self.per + k


def is_first(j):
    return isinstance(j, int) and j == 0


def block_kernel(nc, x, w_in, w_out, w_xp, w_dt, w_q, w_qs, w_k, w_ks, w_v, w_o, w_f, w_gate, experts, b2, vecs, rows,
                 ctx_t, rope_q, rope_k, out):
    ctx = ExitStack()
    with ctx:
        def sb(name, shape, dt=F32):
            return ctx.enter_context(nc.sbuf_tensor(name, shape, dt))

        def signal(name, per):
            s = Signal(ctx.enter_context(nc.semaphore(name)), per)
            signals[name] = s
            return s

        signals = {}
        ps = ctx.enter_context(nc.psum_tensor("ps", [P, 8, 512], F32))

        win = sb("win", [P, KD, 2 * DI])
        wout = sb("wout", [P, Q, DM])
        wxp = sb("wxp", [P, Q, RANK + 2 * NS])
        wdt = sb("wdt", [RANK, DI])
        wq = sb("wq", [P, KD, 2 * DM])
        wqs = sb("wqs", [P, KD, 2 * DM])
        wo = sb("wo", [P, KD, DM])
        wf = sb("wf", [P, KD, DM])
        wgate = sb("wgate", [P, KD, EXPERTS])
        b2s = sb("b2s", [ALL, DM])
        vec = sb("vec", [P, VECS])
        row = sb("row", [1, 4, DM])
        kblk = sb("kblk", [P, SEQS, HB * 2 * KEYS])
        vx = sb("vx", [P, SEQS, HEADS * (HD + 1)])
        conv = sb("conv", [P, Q, TAPS, P])
        ident = sb("ident", [P, P])
        ones = sb("ones", [1, P])
        iota_i = sb("iota_i", [P, EXPERTS], I32)
        iota8 = sb("iota8", [P, EXPERTS])
        keep = sb("keep", [P, CHUNKS])
        power = sb("power", [P, NT])
        neg_a = sb("neg_a", [P, Q * NS])
        half_b1 = sb("half_b1", [P, ALL * KD])
        ratio = sb("ratio", [P, 4])

        xt = sb("xt", [P, NT, DM])
        u = sb("u", [P, Q, TC])
        sz = sb("sz", [P, Q, TC])
        delta = sb("delta", [P, Q, TC])
        v = sb("v", [P, Q, TC])
        bbc = sb("bbc", [P, 2, 2, TC])
        dbu = sb("dbu", [P, 2, Q, TC])
        hs = sb("hs", [P, 2, Q, TC + 4])
        yacc = sb("yacc", [P, NT, DI])
        hist = sb("hist", [P, Q, TAPS - 1])
        carry = sb("carry", [P, NS, Q])
        ctok = sb("ctok", [P, NT, NS])
        rows_t = sb("rows_t", [64, TC])
        dtr, brow = rows_t[0:RANK, :], rows_t[32:32 + NS, :]
        ssq = sb("ssq", [P, NT])
        ms = sb("ms", [P, NT])
        rms = sb("rms", [P, NT])
        xi = hs[:, 1, :, :]
        xn = yacc[:, 0:NT // 2, :].rearrange("p a (b d) -> p (a b) d", b=2)
        xnt = yacc[:, NT // 2:NT, :]

        x1 = sb("x1", [P, NT, DM])
        x1t = sb("x1t", [P, KD, TC])
        work = sb("work", [P, 4096 + 1024])
        qr = work[:, 0:2048].rearrange("p (b t) -> p b t", b=HB)
        qtmp = work[:, 2048:3072].rearrange("p (a t) -> p a t", a=2)
        prob = work[:, 3072:4096]
        probt = work[:, 4096:5120]
        th = work[:, 0:1024].rearrange("p (a t) -> p a t", a=2)
        ga = work[:, 1024:2048].rearrange("p (a t) -> p a t", a=2)
        gac = work[:, 2048:3072].rearrange("p (a t) -> p a t", a=2)
        gm = work[:, 3072:4096].rearrange("p (a t) -> p a t", a=2)
        hh = work[:, 4096:5120].rearrange("p (a t) -> p a t", a=2)
        rope = sb("rope", [P, 2, TC])
        mx = sb("mx", [P, HEADS])
        rec = sb("rec", [P, HEADS])
        on = sb("on", [P, DM])
        ont = sb("ont", [P, KD, P])
        xa = sb("xa", [P, NT, DM])
        x2 = sb("x2", [P, NT, DM])
        x2t = sb("x2t", [P, KD, TC])
        lg = sb("lg", [P, NT, EXPERTS])
        m8 = sb("m8", [P, NT, 8])
        i8 = sb("i8", [P, NT, 8], U32)
        i2 = sb("i2", [P, NT, 2])
        ls = sb("ls", [P, NT, EXPERTS])
        el = sb("el", [P, NT, EXPERTS])
        se = sb("se", [P, NT])
        re = sb("re", [P, NT])
        pr = sb("pr", [P, NT, EXPERTS])
        mk = sb("mk", [P, 2, NT, EXPERTS])
        mk2 = sb("mk2", [P, NT, EXPERTS])
        comb = sb("comb", [P, NT, ALL])
        combt = sb("combt", [ALL, TC])
        we = sb("we", [P, WRING, 3, KD * DM])
        cbc = sb("cbc", [P, CRING, TC])
        carrier = sb("carrier", [1, 8])
        stat, mv, ve, rstd = ({k: sb(f"{name}_{k}", [P, NT * n]) for k in ("x1", "xl", "x2", "xo")}
                              for name, n in (("stat", 6), ("mv", 2), ("ve", 1), ("rstd", 1)))

        ctxt = work[:, 0:KD * P].rearrange("p (k n) -> p k n", k=KD)
        ropek = work[:, 256:512].rearrange("p (a n) -> p a n", a=2)
        krot = work[:, 512:1536].rearrange("p (a b n) -> p a b n", a=2, b=HB)
        ksum = work[:, 1536:2048].rearrange("p (b n) -> p b n", b=HB)
        wk = work[:, 2048:3072].rearrange("p (k n) -> p k n", k=KD)
        wks = work[:, 3072:4096].rearrange("p (k n) -> p k n", k=KD)
        wv = work[:, 4096:5120].rearrange("p (k n) -> p k n", k=KD)

        brow_dram = nc.dram_tensor("brow_dram", (NS, TC), F32, kind="Internal").ap()
        comb_dram = nc.dram_tensor("comb_dram", (ALL, TC), F32, kind="Internal").ap()

        def col(name, i=0, n=1):
            a = VEC[name][0] + i
            return vec[:, a:a + n]

        one = lambda name: signal(name, 0)
        w_setup, w_mix, w_att = one("w_setup"), one("w_mix"), one("w_att")
        consts, ident_set, zeroed, iota_set = one("consts"), one("ident_set"), one("zeroed"), one("iota_set")
        setup_act, setup_dve, setup_pe = one("setup_act"), one("setup_dve"), one("setup_pe")
        kv_done, conv_set = one("kv_done"), one("conv_set")

        x_in = signal("x_in", 16)
        sq_done = signal("sq_done", 1)
        ms_done = signal("ms_done", 1)
        rms_done = signal("rms_done", 1)
        xn_done = signal("xn_done", 1)
        xnt_ps = signal("xnt_ps", KD)
        xnt_done = signal("xnt_done", KD)
        xz_ps = signal("xz_ps", 2 * Q)
        hist_in = signal("hist_in", 1)
        xi_done = signal("xi_done", Q)
        sz_done = signal("sz_done", Q)
        conv_ps = signal("conv_ps", Q)
        hist_out = signal("hist_out", 1)
        u_done = signal("u_done", Q)
        xp_ps = signal("xp_ps", 3)
        dtr_done = signal("dtr_done", 1)
        brow_done = signal("brow_done", 1)
        ctok_done = signal("ctok_done", 1)
        brow_out = signal("brow_out", 16)
        bbc_in = [signal(f"bbc_in{s}", 16 * NS // 4) for s in range(2)]
        dp_ps = signal("dp_ps", Q)
        ymin_done = signal("ymin_done", Q)
        exp_done = signal("exp_done", Q)
        ln_done = signal("ln_done", Q)
        delta_done = signal("delta_done", Q)
        v_done = signal("v_done", Q)
        carry_kept = signal("carry_kept", 1)
        carry_done = signal("carry_done", NS)
        da_done = signal("da_done", NS * Q)
        dbu_done = signal("dbu_done", NS)
        scan_done = signal("scan_done", NS * Q)
        ht_ps = signal("ht_ps", NS * NT)
        y_done = signal("y_done", NS * NT)
        yt_ps = signal("yt_ps", Q)
        yd_done = signal("yd_done", Q)
        yg_done = signal("yg_done", Q)
        out_ps = signal("out_ps", NT)
        res_done = signal("res_done", NT)
        x1_done = signal("x1_done", NT)

        norm = {k: {s: signal(f"{k}_{s}", n) for s, n in (("stats", NT), ("held", 1), ("aggr", NT), ("ve", 1), ("rstd", 1))}
                for k in ("x1", "xl", "x2", "xo")}

        x1t_ps = signal("x1t_ps", KD)
        x1t_done = signal("x1t_done", KD)
        rope_in = signal("rope_in", 16)
        q_ps = signal("q_ps", 2 * HB)
        rot_done = signal("rot_done", 2 * HB)
        q_done = signal("q_done", HB)
        s_ps = signal("s_ps", NT)
        mx_done = signal("mx_done", NT)
        sub_done = signal("sub_done", NT)
        p_done = signal("p_done", NT)
        pt_ps = signal("pt_ps", NT)
        pt_done = signal("pt_done", NT)
        av_ps = signal("av_ps", NT)
        rec_done = signal("rec_done", NT)
        on_done = signal("on_done", NT)
        ont_ps = signal("ont_ps", NT)
        ont_done = signal("ont_done", NT)
        ao_ps = signal("ao_ps", NT)
        xa_done = signal("xa_done", NT)
        xl_done = signal("xl_done", NT)
        xlt_ps = signal("xlt_ps", KD)
        xlt_done = signal("xlt_done", KD)
        f_ps = signal("f_ps", NT)
        f_done = signal("f_done", NT)
        x2_done = signal("x2_done", NT)
        x2t_ps = signal("x2t_ps", KD)
        x2t_done = signal("x2t_done", KD)
        lg_ps = signal("lg_ps", 1)
        lg_done = signal("lg_done", 1)
        m8_done = signal("m8_done", 2)
        i8_done = signal("i8_done", 1)
        ls_done = signal("ls_done", 1)
        el_done = signal("el_done", 1)
        top_done = signal("top_done", 7)
        comb_done = signal("comb_done", 1)
        combt_ps = signal("combt_ps", 1)
        combt_done = signal("combt_done", 1)
        comb_out = signal("comb_out", 16)
        cbc_in = [signal(f"cbc_in{s}", 16 * len(range(s, EXPERTS, CRING))) for s in range(CRING)]
        we_in = [signal(f"we_in{s}", 16 * len(range(s, ALL, WRING))) for s in range(WRING)]
        ab_ps = signal("ab_ps", 2 * ALL)
        th_done = signal("th_done", 2 * ALL)
        ga_done = signal("ga_done", 2 * ALL)
        gac_done = signal("gac_done", 2 * EXPERTS)
        gm_done = signal("gm_done", 2 * ALL)
        hh_done = signal("hh_done", 2 * ALL)
        o_ps = signal("o_ps", 2 * ALL)
        xo_done = signal("xo_done", NT)
        fin_done = signal("fin_done", NT)
        out_store = signal("out_store", 16)

        block = ctx.enter_context(nc.Block())

        def streams(eng, mixer, second):
            def body(i, first, last):
                for kind, *which in SCHEDULE:
                    if kind == "am":
                        if not first:
                            second(i - 1, which[0])
                    elif not last:
                        mixer(i, kind, *which)

            body(0, True, False)
            with eng.Fori(1, CHUNKS, 1) as i:
                body(i, False, False)
            body(CHUNKS, False, True)

        @block.sync
        def _(sp):
            for dst, src in ((ctxt, ctx_t), (wk, w_k), (wks, w_ks), (wv, w_v)):
                sp.dma_start(dst, src.rearrange("(k p) n -> p k n", p=P)).then_inc(w_setup.sem, 16)
            sp.dma_start(ropek, rope_k.rearrange("a p n -> p a n")).then_inc(w_setup.sem, 16)
            sp.dma_start(row[:, :, :].rearrange("o a n -> o (a n)"), rows).then_inc(w_setup.sem, 16)
            sp.dma_start(vec[:, :], vecs).then_inc(w_setup.sem, 16)
            sp.dma_start(win[:, :, :], w_in.rearrange("(k p) n -> p k n", p=P)).then_inc(w_mix.sem, 16)
            sp.dma_start(wxp[:, :, :], w_xp.rearrange("(k p) n -> p k n", p=P)).then_inc(w_mix.sem, 16)
            sp.dma_start(wdt[:, :], w_dt).then_inc(w_mix.sem, 16)
            sp.dma_start(wout[:, :, :], w_out.rearrange("(k p) n -> p k n", p=P)).then_inc(w_mix.sem, 16)
            for dst, src in ((wq, w_q), (wqs, w_qs), (wo, w_o), (wf, w_f), (wgate, w_gate)):
                sp.dma_start(dst[:, :, :], src.rearrange("(k p) n -> p k n", p=P)).then_inc(w_att.sem, 16)
            sp.dma_start(b2s[:, :], b2).then_inc(w_att.sem, 16)

            def load_bbc(j, pair):
                if pair >= 2:
                    sp.wait_ge(*dbu_done.at(j, 2 * pair - 2))
                sp.dma_start(bbc[:, pair % 2, :, :].rearrange("p a t -> p (a t)"),
                             brow_dram[2 * pair:2 * pair + 2, :].rearrange("a t -> (a t)").partition_broadcast(P)
                             ).then_inc(bbc_in[pair % 2].sem, 16)

            def mixer(j, kind, n=0, half=0):
                if kind == "pre" and n == 0:
                    sp.wait_ge(*res_done.at(j, 0))
                    sp.dma_start(xt[:, :, :], x[bass.ds(j, 1)].rearrange("a t p d -> p (a t) d")
                                 ).then_inc(x_in.sem, 16)
                if kind == "pre" and n == 3:
                    sp.wait_ge(*brow_done.at(j, 1))
                    sp.dma_start(brow_dram, brow).then_inc(brow_out.sem, 16)
                    sp.wait_ge(*brow_out.at(j, 16))
                    load_bbc(j, 0)
                    load_bbc(j, 1)
                if kind == "scan" and half == 1 and n % 2 == 1 and n // 2 + 2 < NS // 2:
                    load_bbc(j, n // 2 + 2)

            def load_expert(j, e):
                if e >= WRING:
                    sp.wait_ge(*o_ps.at(j, 2 * (e - WRING) + 2))
                else:
                    sp.wait_ge(*o_ps.at(j, 0))
                sp.dma_start(we[:, e % WRING, :, :].rearrange("p a n -> p (a n)"), experts[e]
                             ).then_inc(we_in[e % WRING].sem, 16)

            def load_comb(j, e):
                if e >= CRING:
                    sp.wait_ge(*gac_done.at(j, 2 * (e - CRING) + 2))
                sp.dma_start(cbc[:, e % CRING, :], comb_dram[e, :].partition_broadcast(P)
                             ).then_inc(cbc_in[e % CRING].sem, 16)

            def second(j, t):
                if t == 0:
                    sp.wait_ge(*rot_done.at(j, 0))
                    sp.dma_start(rope[:, :, :], rope_q[bass.ds(j, 1)].rearrange("c a p t -> p (c a) t")
                                 ).then_inc(rope_in.sem, 16)
                if t == T_LNT:
                    for e in range(WRING):
                        load_expert(j, e)
                if t == T_COMB:
                    sp.wait_ge(*combt_done.at(j, 1))
                    sp.dma_start(comb_dram, combt[0:ALL, :]).then_inc(comb_out.sem, 16)
                    sp.wait_ge(*comb_out.at(j, 16))
                    for e in range(CRING):
                        load_comb(j, e)
                for e in range(ALL):
                    if t == T_EXP + 2 * e + 2:
                        if e + WRING < ALL:
                            load_expert(j, e + WRING)
                        if e + CRING < EXPERTS:
                            load_comb(j, e + CRING)
                if t == T_OUT:
                    sp.wait_ge(*fin_done.at(j, NT))
                    sp.dma_start(out[bass.ds(j, 1)].rearrange("a t p d -> p (a t) d"), xa[:, :, :]
                                 ).then_inc(out_store.sem, 16)

            streams(sp, mixer, second)
            sp.wait_ge(*out_store.at(CHUNKS, 0))

        @block.gpsimd
        def _(pool):
            pool.memset(ident[:, :], 0.0).then_inc(zeroed.sem, 1)
            pool.memset(ones[:, :], 1.0).then_inc(consts.sem, 1)
            pool.memset(power[:, :], -0.5).then_inc(consts.sem, 1)
            for c in range(CHUNKS):
                pool.memset(keep[:, c:c + 1], 0.0 if c % CPS == 0 else 1.0).then_inc(consts.sem, 1)
            pool.memset(kblk[:, :, :], 0.0).then_inc(consts.sem, 1)
            pool.memset(vx[:, :, :], 1.0).then_inc(consts.sem, 1)
            pool.memset(carry[:, :, :], 0.0).then_inc(consts.sem, 1)
            pool.memset(hist[:, :, :], 0.0).then_inc(consts.sem, 1)
            pool.memset(comb[:, :, :], 1.0).then_inc(consts.sem, 1)
            pool.iota(iota_i[:, :], pattern=[[1, EXPERTS]], base=0, channel_multiplier=0).then_inc(iota_set.sem, 1)
            pool.wait_ge(zeroed.sem, 1)
            pool.affine_select(out=ident[:, :], in_=ident[:, :], compare_op=ALU.not_equal, fill=1.0,
                               base=0, pattern=[[-1, P]], channel_multiplier=1).then_inc(ident_set.sem, 1)

            def mixer(j, kind, n=0, half=0):
                if kind == "pre" and n == 0:
                    pool.wait_ge(*ms_done.at(j, 1))
                    if is_first(j):
                        pool.wait_ge(consts.sem, 7 + CHUNKS)
                    pool.tensor_tensor(rms[:, :], ms[:, :], power[:, :], ALU.pow).then_inc(rms_done.sem, 1)
                if kind == "scan" and half == 0:
                    pool.wait_ge(*bbc_in[n // 2 % 2].at(j, 16 * (n // 4 + 1)))
                    pool.wait_ge(*v_done.at(j, Q))
                    pool.wait_ge(*scan_done.at(j, max(0, Q * (n - 1))))
                    pool.tensor_tensor(dbu[:, n % 2, :, :], v[:, :, :],
                                       bbc[:, n // 2 % 2, n % 2, :].rearrange("p (o t) -> p o t", o=1)
                                       .to_broadcast([P, Q, TC]), ALU.mult).then_inc(dbu_done.sem, 1)
                if kind == "post":
                    rstd_of(j, "x1")

            def rstd_of(j, k):
                pool.wait_ge(*norm[k]["ve"].at(j, 1))
                pool.tensor_tensor(rstd[k][:, :], ve[k][:, :], power[:, :], ALU.pow
                                   ).then_inc(norm[k]["rstd"].sem, 1)

            def second(j, t):
                if t in (T_Q, T_Q + 1):
                    for b in range(2 * (t - T_Q), 2 * (t - T_Q) + 2):
                        pool.wait_ge(*rot_done.at(j, 2 * b + 2))
                        pool.tensor_tensor(qr[:, b, :], qr[:, b, :], qtmp[:, b % 2, :], ALU.add
                                           ).then_inc(q_done.sem, 1)
                if t == T_RES3:
                    rstd_of(j, "xl")
                if t == T_FFN:
                    rstd_of(j, "x2")
                e, ib = divmod(t - T_EXP, 2)
                if 0 <= e < EXPERTS:
                    pool.wait_ge(*ga_done.at(j, 2 * e + ib + 1))
                    pool.wait_ge(*cbc_in[e % CRING].at(j, 16 * (e // CRING + 1)))
                    pool.wait_ge(*gm_done.at(j, max(0, 2 * e + ib - 1)))
                    pool.tensor_tensor(gac[:, ib, :], ga[:, ib, :], cbc[:, e % CRING, :], ALU.mult
                                       ).then_inc(gac_done.sem, 1)
                if t == T_OUT:
                    rstd_of(j, "xo")

            streams(pool, mixer, second)

        @block.scalar
        def _(act):
            act.preload_act_table(ACT.Exp)
            act.wait_ge(w_setup.sem, 7 * 16)
            act.activation(neg_a[:, :], col("A_log", 0, Q * NS), ACT.Exp).then_inc(setup_act.sem, 1)
            act.activation(ratio[:, 0:1], col("gate"), ACT.Exp, scale=-1.0).then_inc(setup_act.sem, 1)

            def mixer(j, kind, n=0, half=0):
                if kind == "pre" and n == 0:
                    act.wait_ge(*x_in.at(j, 16))
                    act.wait_ge(*out_ps.at(j, 0))
                    for t in range(NT):
                        last = act.activation(xn[:, t, :], xt[:, t, :], ACT.Square, accum_out=ssq[:, t:t + 1])
                    last.then_inc(sq_done.sem, 1)
                if kind == "pre" and n == 1:
                    for k in range(KD):
                        act.wait_ge(*xnt_ps.at(j, k + 1))
                        act.activation(xnt[:, k, :], ps[:, k, :], ACT.Copy, scale=col("norm_w", k)
                                       ).then_inc(xnt_done.sem, 1)
                    for q in range(Q):
                        act.wait_ge(*xz_ps.at(j, Q + q + 1))
                        act.activation(sz[:, q, :], ps[:, (2 + q) % 4, :], ACT.Silu).then_inc(sz_done.sem, 1)
                if kind == "pre" and n == 2:
                    for q in range(Q):
                        act.wait_ge(*conv_ps.at(j, q + 1))
                        act.activation(u[:, q, :], ps[:, (2 + q) % 4, :], ACT.Silu, bias=col("conv_b", q)
                                       ).then_inc(u_done.sem, 1)
                    act.wait_ge(*xp_ps.at(j, 1))
                    act.activation(dtr, ps[0:RANK, 2, :], ACT.Copy).then_inc(dtr_done.sem, 1)
                    act.wait_ge(*xp_ps.at(j, 2))
                    act.wait_ge(*brow_out.at(j, 0))
                    act.activation(brow, ps[32:32 + NS, 3, :], ACT.Copy).then_inc(brow_done.sem, 1)
                if kind == "pre" and n == 3:
                    for q in range(Q):
                        act.wait_ge(*ymin_done.at(j, q + 1))
                        act.activation(delta[:, q, :], delta[:, q, :], ACT.Exp).then_inc(exp_done.sem, 1)
                    for q in range(Q):
                        act.wait_ge(*exp_done.at(j, q + 1))
                        act.activation(delta[:, q, :], delta[:, q, :], ACT.Ln, bias=1.0).then_inc(ln_done.sem, 1)
                if kind == "scan":
                    for q in range(2 * half, 2 * half + 2):
                        unit = n * Q + q
                        act.wait_ge(*delta_done.at(j, Q))
                        act.wait_ge(*scan_done.at(j, max(0, unit - 1)))
                        act.activation(ps[:, unit % 2, :], delta[:, q, :], ACT.Exp,
                                       scale=neg_a[:, q * NS + n:q * NS + n + 1]).then_inc(da_done.sem, 1)
                    if half == 1 and n >= 1:
                        save_carry(j, n - 1)
                if kind == "scan_end":
                    save_carry(j, NS - 1)

            def save_carry(j, n):
                act.wait_ge(*scan_done.at(j, Q * (n + 1)))
                act.activation(carry[:, n, :], hs[:, n % 2, :, TC - 1], ACT.Copy).then_inc(carry_done.sem, 1)

            def second(j, t):
                if t == T_X1T:
                    for k in range(KD):
                        act.wait_ge(*x1t_ps.at(j, k + 1))
                        act.activation(x1t[:, k, :], ps[:, 4 + k, :], ACT.Copy).then_inc(x1t_done.sem, 1)
                for tile in range(NT):
                    if t == T_S + 2 * tile:
                        if tile:
                            out_rows(j, tile - 1)
                        act.wait_ge(*sub_done.at(j, tile + 1))
                        act.activation(prob, prob, ACT.Exp, scale=HD ** -0.5).then_inc(p_done.sem, 1)
                    if t == T_PT + 2 * tile:
                        act.wait_ge(*pt_ps.at(j, tile + 1))
                        act.activation(probt.rearrange("p (a n) -> p a n", a=2), ps[:, 6:8, :], ACT.Copy
                                       ).then_inc(pt_done.sem, 1)
                if t == T_O3:
                    out_rows(j, NT - 1)
                if t == T_LNT:
                    for k in range(KD):
                        act.wait_ge(*xlt_ps.at(j, k + 1))
                        act.activation(x1t[:, k, :], ps[:, 4 + k, :], ACT.Identity, scale=col("gamma", k),
                                       bias=col("beta", k)).then_inc(xlt_done.sem, 1)
                if t == T_GATE:
                    for k in range(KD):
                        act.wait_ge(*x2t_ps.at(j, k + 1))
                        act.activation(x2t[:, k, :], ps[:, 4 + k, :], ACT.Copy).then_inc(x2t_done.sem, 1)
                    act.wait_ge(*ls_done.at(j, 1))
                    act.activation(el[:, :, :], ls[:, :, :], ACT.Exp).then_inc(el_done.sem, 1)
                if t == T_COMB:
                    act.wait_ge(*combt_ps.at(j, 1))
                    act.wait_ge(*comb_out.at(j, 0))
                    act.activation(combt[:, :], ps[0:ALL, 4, :], ACT.Copy).then_inc(combt_done.sem, 1)
                e, ib = divmod(t - T_EXP, 2)
                if 0 <= e < ALL:
                    c = 2 * e + ib
                    bias = half_b1[:, c:c + 1]
                    act.wait_ge(*ab_ps.at(j, c + 1))
                    act.wait_ge(*gm_done.at(j, max(0, c - 1)))
                    act.activation(ga[:, ib, :], ps[:, 4, :], ACT.Identity, scale=0.5, bias=bias
                                   ).then_inc(ga_done.sem, 1)
                    act.activation(th[:, ib, :], ps[:, 4, :], ACT.Tanh, scale=0.5, bias=bias
                                   ).then_inc(th_done.sem, 1)

            def out_rows(j, tile):
                act.wait_ge(*ont_ps.at(j, tile + 1))
                act.activation(ont[:, :, :], ps[:, 6, 0:DM].rearrange("p (k n) -> p k n", k=KD), ACT.Copy
                               ).then_inc(ont_done.sem, 1)

            streams(act, mixer, second)

        @block.tensor
        def _(pe):
            pe.wait_ge(w_setup.sem, 7 * 16)
            for s, w in enumerate((wk, wks)):
                for b in range(HB):
                    for k in range(KD):
                        last = pe.matmul(ps[:, 4 + s, b * P:(b + 1) * P], w[:, k, b * P:(b + 1) * P], ctxt[:, k, :],
                                         start=(k == 0), stop=(k == KD - 1))
            last.then_inc(setup_pe.sem, 1)
            pe.wait_ge(consts.sem, 7 + CHUNKS)
            for s in range(SEQS):
                for a in range(2):
                    o = ps[a * CTX:(a + 1) * CTX, 6, s * DM:(s + 1) * DM]
                    for k in range(KD):
                        pe.matmul(o, ctxt[:, k, s * CTX:(s + 1) * CTX], wv[:, k, a * DM:(a + 1) * DM],
                                  start=(k == 0), stop=False)
                    last = pe.matmul(o, ones[0:1, 0:CTX], row[0:1, a, :], start=False, stop=True)
            last.then_inc(setup_pe.sem, 1)

            def transposes(bank, src, tiles, sig):
                for t in range(tiles):
                    last = pe.transpose(ps[:, bank, t * P:(t + 1) * P], src(t), ident[:, :])
                last.then_inc(sig.sem, 1)

            def mixer(j, kind, n=0, half=0):
                if kind == "pre" and n == 1:
                    if is_first(j):
                        pe.wait_ge(ident_set.sem, 1)
                        pe.wait_ge(w_mix.sem, 4 * 16)
                        pe.wait_ge(conv_set.sem, 1)
                    pe.wait_ge(*xn_done.at(j, 1))
                    pe.wait_ge(*res_done.at(j, 0))
                    for k in range(KD):
                        transposes(k, lambda t: xn[:, t, k * P:(k + 1) * P], NT, xnt_ps)
                    pe.wait_ge(*xnt_done.at(j, KD))
                    for m in range(2 * Q):
                        if m >= Q:
                            pe.wait_ge(*xi_done.at(j, m - Q + 1))
                        for k in range(KD):
                            last = pe.matmul(ps[:, (2 + m) % 4, :], win[:, k, m * P:(m + 1) * P], xnt[:, k, :],
                                             start=(k == 0), stop=(k == KD - 1))
                        last.then_inc(xz_ps.sem, 1)
                if kind == "pre" and n == 2:
                    pe.wait_ge(*hist_in.at(j, 1))
                    for q in range(Q):
                        pe.wait_ge(*sz_done.at(j, q + 1))
                        for k in range(TAPS):
                            last = pe.matmul(ps[:, (2 + q) % 4, :], conv[:, q, k, :], xi[:, q, k:k + TC],
                                             start=(k == 0), stop=(k == TAPS - 1))
                        last.then_inc(conv_ps.sem, 1)
                    pe.wait_ge(*u_done.at(j, Q))
                    for s in range(2):
                        for q in range(Q):
                            last = pe.matmul(ps[32 * s:32 * s + NS, 2 + s, :], wxp[:, q, s * NS:(s + 1) * NS], u[:, q, :],
                                             start=(q == 0), stop=(q == Q - 1))
                        last.then_inc(xp_ps.sem, 1)
                    for t in range(NT):
                        for q in range(Q):
                            last = pe.matmul(ps[:, 0, t * NS:(t + 1) * NS], u[:, q, t * P:(t + 1) * P],
                                             wxp[:, q, 2 * NS:3 * NS], start=(q == 0), stop=(q == Q - 1))
                    last.then_inc(xp_ps.sem, 1)
                if kind == "pre" and n == 3:
                    pe.wait_ge(*dtr_done.at(j, 1))
                    pe.wait_ge(*brow_done.at(j, 1))
                    pe.wait_ge(*ctok_done.at(j, 1))
                    for q in range(Q):
                        pe.matmul(ps[:, (1 + q) % 4, :], wdt[:, q * P:(q + 1) * P], dtr,
                                  start=True, stop=True).then_inc(dp_ps.sem, 1)
                if kind == "scan" and n >= 1:
                    state_rows(j, n - 1, half)
                if kind == "scan_end":
                    state_rows(j, NS - 1, 0)
                    state_rows(j, NS - 1, 1)
                if kind == "post":
                    if is_first(j):
                        pe.wait_ge(w_att.sem, 6 * 16)
                        pe.wait_ge(kv_done.sem, 2)
                    pe.wait_ge(*y_done.at(j, NS * NT))
                    for q in range(Q):
                        transposes(q, lambda t: yacc[:, t, q * P:(q + 1) * P], NT, yt_ps)
                    pe.wait_ge(*yg_done.at(j, Q))
                    for t in range(NT):
                        for q in range(Q):
                            last = pe.matmul(ps[:, t // 2, t % 2 * DM:(t % 2 + 1) * DM], v[:, q, t * P:(t + 1) * P],
                                             wout[:, q, :], start=(q == 0), stop=(q == Q - 1))
                        last.then_inc(out_ps.sem, 1)

            def state_rows(j, n, half):
                for t in range(2 * half, 2 * half + 2):
                    pe.wait_ge(*scan_done.at(j, Q * (n + 1)))
                    pe.wait_ge(*y_done.at(j, max(0, n * NT + t - 1)))
                    transposes(2 + t % 2, lambda q: hs[:, n % 2, q, t * P:(t + 1) * P], Q, ht_ps)

            def second(j, t):
                if t == T_X1T:
                    pe.wait_ge(*x1_done.at(j, NT))
                    pe.wait_ge(*xo_done.at(j, 0))
                    pe.wait_ge(*hh_done.at(j, 0))
                    for k in range(KD):
                        transposes(4 + k, lambda t: x1[:, t, k * P:(k + 1) * P], NT, x1t_ps)
                if t in (T_Q, T_Q + 1):
                    pe.wait_ge(*x1t_done.at(j, KD))
                    for b in range(2 * (t - T_Q), 2 * (t - T_Q) + 2):
                        for s, w in enumerate((wq, wqs)):
                            o = 2 * b + s
                            if o >= 4:
                                pe.wait_ge(*rot_done.at(j, o - 3))
                            for k in range(KD):
                                last = pe.matmul(ps[:, 4 + (2 + o) % 4, :], w[:, k, b * P:(b + 1) * P], x1t[:, k, :],
                                                 start=(k == 0), stop=(k == KD - 1))
                            last.then_inc(q_ps.sem, 1)
                for tile in range(NT):
                    if t == T_S + 2 * tile:
                        pe.wait_ge(*q_done.at(j, HB))
                        pe.wait_ge(*rot_done.at(j, 2 * HB))
                        if tile:
                            pe.wait_ge(*on_done.at(j, tile))
                            pe.wait_ge(*xa_done.at(j, tile - 1))
                        for b in range(HB):
                            last = pe.matmul(ps[:, 4 + b // 2, b % 2 * 2 * KEYS:(b % 2 + 1) * 2 * KEYS],
                                             qr[:, b, tile * P:(tile + 1) * P],
                                             kblk[:, bass.ds(j // CPS, 1), b * 2 * KEYS:(b + 1) * 2 * KEYS]
                                             .rearrange("p a n -> p (a n)"), start=True, stop=True)
                        last.then_inc(s_ps.sem, 1)
                        if tile:
                            turn_out(j, tile - 1)
                    if t == T_PT + 2 * tile:
                        if tile:
                            out_proj(j, tile - 1)
                        pe.wait_ge(*p_done.at(j, tile + 1))
                        for h in range(HEADS):
                            last = pe.transpose(ps[:, 6 + h // 4, h % 4 * P:(h % 4 + 1) * P],
                                                prob[:, h * KEYS:(h + 1) * KEYS], ident[:, :])
                        last.then_inc(pt_ps.sem, 1)
                        pe.wait_ge(*pt_done.at(j, tile + 1))
                        for h in range(HEADS):
                            c = slice(h * (HD + 1), (h + 1) * (HD + 1))
                            last = pe.matmul(ps[:, 4, c], probt[:, h * P:(h + 1) * P],
                                             vx[:, bass.ds(j // CPS, 1), c].rearrange("p a n -> p (a n)"),
                                             start=True, stop=True)
                        last.then_inc(av_ps.sem, 1)
                if t == T_O3:
                    turn_out(j, NT - 1)
                if t == T_RES3:
                    out_proj(j, NT - 1)
                if t == T_LNT:
                    pe.wait_ge(*xl_done.at(j, NT))
                    for k in range(KD):
                        transposes(4 + k, lambda t: xa[:, t, k * P:(k + 1) * P], NT, xlt_ps)
                if t == T_FFN:
                    pe.wait_ge(*xlt_done.at(j, KD))
                    for tile in range(NT):
                        o = ps[:, 6 + tile // 2, tile % 2 * DM:(tile % 2 + 1) * DM]
                        for k in range(KD):
                            pe.matmul(o, x1t[:, k, tile * P:(tile + 1) * P], wf[:, k, :], start=(k == 0), stop=False)
                        pe.matmul(o, ones[0:1, :], row[0:1, 3, :], start=False, stop=True).then_inc(f_ps.sem, 1)
                if t == T_GATE:
                    pe.wait_ge(*x2_done.at(j, NT))
                    for k in range(KD):
                        transposes(4 + k, lambda t: x2[:, t, k * P:(k + 1) * P], NT, x2t_ps)
                    pe.wait_ge(*x2t_done.at(j, KD))
                    for tile in range(NT):
                        for k in range(KD):
                            last = pe.matmul(ps[:, 6, tile * EXPERTS:(tile + 1) * EXPERTS],
                                             x2t[:, k, tile * P:(tile + 1) * P], wgate[:, k, :],
                                             start=(k == 0), stop=(k == KD - 1))
                    last.then_inc(lg_ps.sem, 1)
                if t == T_COMB:
                    pe.wait_ge(*comb_done.at(j, 1))
                    for tile in range(NT):
                        last = pe.transpose(ps[0:ALL, 4, tile * P:(tile + 1) * P], comb[:, tile, :], ident[:, :])
                    last.then_inc(combt_ps.sem, 1)
                    pe.wait_ge(*combt_done.at(j, 1))
                    for tile in range(NT):
                        pe.matmul(out_cols(tile), combt[:, tile * P:(tile + 1) * P], b2s[:, :],
                                  start=(tile % 2 == 0), stop=False, skip_group_check=True)
                e, ib = divmod(t - T_EXP, 2)
                if 0 <= e < ALL:
                    c = 2 * e + ib
                    if ib == 0:
                        pe.wait_ge(*we_in[e % WRING].at(j, 16 * (e // WRING + 1)))
                    pe.wait_ge(*th_done.at(j, c))
                    for s in range(2):
                        if s == 1:
                            pe.wait_ge(*hh_done.at(j, c))
                        for k in range(KD):
                            last = pe.matmul(ps[:, 4 + s, :],
                                             we[:, e % WRING, s, k * DM + ib * P:k * DM + (ib + 1) * P],
                                             x2t[:, k, :], start=(k == 0), stop=(k == KD - 1))
                    last.then_inc(ab_ps.sem, 1)
                e, ib = divmod(t - T_EXP - 1, 2)
                if 0 <= e < ALL:
                    c = 2 * e + ib
                    pe.wait_ge(*hh_done.at(j, c + 1))
                    for tile in range(NT):
                        last = pe.matmul(out_cols(tile), hh[:, ib, tile * P:(tile + 1) * P],
                                         we[:, e % WRING, 2, ib * DM:(ib + 1) * DM],
                                         start=False, stop=(c == 2 * ALL - 1), skip_group_check=True)
                    last.then_inc(o_ps.sem, 1)

            def out_cols(tile):
                return ps[:, 6 + tile // 2, tile % 2 * DM:(tile % 2 + 1) * DM]

            def turn_out(j, tile):
                pe.wait_ge(*on_done.at(j, tile + 1))
                transposes(6, lambda k: on[:, k * P:(k + 1) * P], KD, ont_ps)

            def out_proj(j, tile):
                pe.wait_ge(*ont_done.at(j, tile + 1))
                pe.wait_ge(*sub_done.at(j, min(tile + 2, NT)))
                for k in range(KD):
                    pe.matmul(ps[:, 5, 0:DM], ont[:, k, :], wo[:, k, :], start=(k == 0), stop=False)
                pe.matmul(ps[:, 5, 0:DM], ones[0:1, :], row[0:1, 2, :], start=False, stop=True
                          ).then_inc(ao_ps.sem, 1)

            streams(pe, mixer, second)

        @block.vector
        def _(dve):
            dve.wait_ge(w_setup.sem, 7 * 16)
            dve.wait_ge(ident_set.sem, 1)
            for q in range(Q):
                for k in range(TAPS):
                    last = dve.tensor_scalar(conv[:, q, k, :], ident[:, :], col("conv_w", q * TAPS + k), None, ALU.mult)
            last.then_inc(conv_set.sem, 1)
            dve.wait_ge(iota_set.sem, 1)
            dve.tensor_copy(iota8[:, :], iota_i[:, :]).then_inc(setup_dve.sem, 1)
            dve.tensor_scalar(half_b1[:, :], col("b1", 0, ALL * KD), 0.5, None, ALU.mult).then_inc(setup_dve.sem, 1)
            dve.wait_ge(setup_act.sem, 2)
            dve.tensor_scalar(neg_a[:, :], neg_a[:, :], -1.0, None, ALU.mult).then_inc(setup_dve.sem, 1)
            dve.tensor_scalar(ratio[:, 1:2], ratio[:, 0:1], 1.0, None, ALU.add).then_inc(setup_dve.sem, 1)
            dve.wait_ge(setup_dve.sem, 4)
            dve.reciprocal(ratio[:, 2:3], ratio[:, 1:2]).then_inc(setup_dve.sem, 1)
            dve.wait_ge(setup_pe.sem, 1)
            for s, bias in enumerate(("bk", "bk_swap")):
                for b in range(HB):
                    last = dve.scalar_tensor_tensor(out=krot[:, s, b, :], in0=ps[:, 4 + s, b * P:(b + 1) * P],
                                                    scalar=col(bias, b), in1=ropek[:, s, :], op0=ALU.add, op1=ALU.mult)
            last.then_inc(setup_dve.sem, 1)
            dve.wait_ge(setup_dve.sem, 6)
            dve.tensor_tensor(ksum, krot[:, 0, :, :], krot[:, 1, :, :], ALU.add).then_inc(setup_dve.sem, 1)
            dve.wait_ge(setup_dve.sem, 7)
            dve.wait_ge(consts.sem, 7 + CHUNKS)
            for s in range(SEQS):
                for g in range(4):
                    r = slice(32 * g, 32 * g + 32)
                    o = kblk[r, s, :].rearrange("p (b n) -> p b n", b=HB)[:, :, g * CTX:(g + 1) * CTX]
                    i = ksum[r, :, s * CTX:(s + 1) * CTX]
                    if g % 2:
                        last = dve.tensor_scalar(o, i, ratio[r, 2:3], None, ALU.mult)
                    else:
                        last = dve.tensor_copy(o, i)
            last.then_inc(kv_done.sem, 1)
            dve.wait_ge(setup_pe.sem, 2)
            for s in range(SEQS):
                last = dve.tensor_copy(vx[:, s, :].rearrange("p (h d) -> p h d", h=HEADS)[:, :, 0:HD],
                                       ps[:, 6, s * DM:(s + 1) * DM].rearrange("p (h d) -> p h d", h=HEADS))
            last.then_inc(kv_done.sem, 1)

            def mixer(j, kind, n=0, half=0):
                if kind == "pre" and n == 0:
                    dve.wait_ge(*sq_done.at(j, 1))
                    dve.tensor_scalar(ms[:, :], ssq[:, :], 1.0 / DM, EPS, ALU.mult, ALU.add).then_inc(ms_done.sem, 1)
                    dve.wait_ge(*rms_done.at(j, 1))
                    for t in range(NT):
                        last = dve.tensor_scalar(xn[:, t, :], xt[:, t, :], rms[:, t:t + 1], None, ALU.mult)
                    last.then_inc(xn_done.sem, 1)
                    dve.wait_ge(*hist_out.at(j, 0))
                    dve.wait_ge(*ht_ps.at(j, 0))
                    dve.wait_ge(*carry_done.at(j, 0))
                    dve.tensor_scalar(xi[:, :, 0:TAPS - 1], hist[:, :, :], keep[:, bass.ds(j, 1)], None, ALU.mult
                                      ).then_inc(hist_in.sem, 1)
                    dve.tensor_scalar(carry[:, :, :], carry[:, :, :], keep[:, bass.ds(j, 1)], None, ALU.mult
                                      ).then_inc(carry_kept.sem, 1)
                if kind == "pre" and n == 1:
                    for q in range(Q):
                        dve.wait_ge(*xz_ps.at(j, q + 1))
                        dve.tensor_copy(xi[:, q, TAPS - 1:TAPS - 1 + TC], ps[:, (2 + q) % 4, :]).then_inc(xi_done.sem, 1)
                    dve.wait_ge(*xi_done.at(j, Q))
                    dve.wait_ge(*hist_in.at(j, 1))
                    dve.tensor_copy(hist[:, :, :], xi[:, :, TC:TC + TAPS - 1]).then_inc(hist_out.sem, 1)
                if kind == "pre" and n == 3:
                    dve.wait_ge(*xp_ps.at(j, 3))
                    dve.tensor_copy(ctok[:, :, :].rearrange("p t n -> p (t n)"), ps[:, 0, 0:NT * NS]
                                    ).then_inc(ctok_done.sem, 1)
                    for q in range(Q):
                        dve.wait_ge(*dp_ps.at(j, q + 1))
                        dve.tensor_scalar(delta[:, q, :], ps[:, (1 + q) % 4, :], col("dt_b", q), LINEAR,
                                          ALU.add, ALU.min).then_inc(ymin_done.sem, 1)
                    for q in range(Q):
                        dve.wait_ge(*ln_done.at(j, q + 1))
                        dve.scalar_tensor_tensor(out=delta[:, q, :], in0=ps[:, (1 + q) % 4, :], scalar=col("dt_b", q),
                                                 in1=delta[:, q, :], op0=ALU.add, op1=ALU.max
                                                 ).then_inc(delta_done.sem, 1)
                    for q in range(Q):
                        dve.wait_ge(*delta_done.at(j, q + 1))
                        dve.tensor_tensor(v[:, q, :], delta[:, q, :], u[:, q, :], ALU.mult).then_inc(v_done.sem, 1)
                if kind == "scan" and half == 0:
                    for q in range(Q):
                        unit = n * Q + q
                        if n == 0:
                            dve.wait_ge(*conv_ps.at(j, Q))
                            dve.wait_ge(*carry_kept.at(j, 1))
                        dve.wait_ge(*da_done.at(j, unit + 1))
                        dve.wait_ge(*dbu_done.at(j, n + 1))
                        if n >= 2:
                            dve.wait_ge(*ht_ps.at(j, (n - 1) * NT))
                            dve.wait_ge(*carry_done.at(j, n - 1))
                        dve.tensor_tensor_scan(hs[:, n % 2, q, 0:TC], ps[:, unit % 2, :], dbu[:, n % 2, q, :],
                                               carry[:, n, q:q + 1], ALU.mult, ALU.add).then_inc(scan_done.sem, 1)
                if kind == "scan" and half == 1 and n >= 1:
                    sum_states(j, n - 1)
                if kind == "scan_end":
                    sum_states(j, NS - 1)
                if kind == "post":
                    for q in range(Q):
                        dve.wait_ge(*yt_ps.at(j, q + 1))
                        dve.wait_ge(*dbu_done.at(j, NS))
                        dve.scalar_tensor_tensor(out=v[:, q, :], in0=u[:, q, :], scalar=col("skip", q),
                                                 in1=ps[:, q, :], op0=ALU.mult, op1=ALU.add).then_inc(yd_done.sem, 1)
                    for q in range(Q):
                        dve.wait_ge(*yd_done.at(j, q + 1))
                        dve.tensor_tensor(v[:, q, :], v[:, q, :], sz[:, q, :], ALU.mult).then_inc(yg_done.sem, 1)
                    for t in range(NT):
                        dve.wait_ge(*out_ps.at(j, t // 2 * 2 + 2))
                        dve.scalar_tensor_tensor(out=x1[:, t, :], in0=xt[:, t, :], scalar=2.0,
                                                 in1=ps[:, t // 2, t % 2 * DM:(t % 2 + 1) * DM],
                                                 op0=ALU.mult, op1=ALU.add).then_inc(res_done.sem, 1)
                    layer_norm(j, "x1", x1, x1, res_done, x1_done)

            def sum_states(j, n):
                for t in range(NT):
                    c = ctok[:, t, n:n + 1]
                    dve.wait_ge(*ht_ps.at(j, n * NT + t + 1))
                    if n == 0:
                        dve.wait_ge(*ctok_done.at(j, 1))
                        dve.wait_ge(*xz_ps.at(j, 2 * Q))
                        dve.tensor_scalar(yacc[:, t, :], ps[:, 2 + t % 2, :], c, None, ALU.mult).then_inc(y_done.sem, 1)
                    else:
                        dve.wait_ge(*y_done.at(j, (n - 1) * NT + t + 1))
                        dve.scalar_tensor_tensor(out=yacc[:, t, :], in0=ps[:, 2 + t % 2, :], scalar=c,
                                                 in1=yacc[:, t, :], op0=ALU.mult, op1=ALU.add).then_inc(y_done.sem, 1)

            def layer_norm(j, k, src, dst, before, after):
                st = stat[k][:, :].rearrange("p (t n) -> p t n", t=NT)
                mean = mv[k][:, :].rearrange("p (t n) -> p t n", t=NT)
                for t in range(NT):
                    dve.wait_ge(*before.at(j, t + 1))
                    dve.bn_stats(st[:, t, :], src[:, t, :]).then_inc(norm[k]["stats"].sem, 1)
                dve.wait_ge(*norm[k]["stats"].at(j, NT))
                spot = ("x1", "xl", "x2", "xo").index(k)
                dve.wait_ge(*norm[k]["held"].at(j, 0))
                dve.memset(carrier[0:1, spot:spot + 1], 0.0).then_inc(norm[k]["held"].sem, 1)
                for t in range(NT):
                    last = dve.bn_aggr(mean[:, t, :], st[:, t, :])
                last.then_inc(norm[k]["aggr"].sem, NT)
                dve.wait_ge(*norm[k]["aggr"].at(j, NT))
                dve.tensor_scalar(ve[k][:, :], mean[:, :, 1], EPS, None, ALU.add).then_inc(norm[k]["ve"].sem, 1)
                dve.wait_ge(*norm[k]["rstd"].at(j, 1))
                for t in range(NT):
                    dve.tensor_scalar(dst[:, t, :], src[:, t, :], mean[:, t, 0:1], rstd[k][:, t:t + 1],
                                      ALU.subtract, ALU.mult).then_inc(after.sem, 1)

            def residual(j, tile):
                dve.wait_ge(*ao_ps.at(j, tile + 1))
                if tile == 0:
                    dve.wait_ge(*out_store.at(j, 0))
                dve.tensor_tensor(xa[:, tile, :], ps[:, 5, 0:DM], x1[:, tile, :], ALU.add).then_inc(xa_done.sem, 1)

            def second(j, t):
                if t in (T_Q, T_Q + 1):
                    for b in range(2 * (t - T_Q), 2 * (t - T_Q) + 2):
                        for s, bias in enumerate(("bq", "bq_swap")):
                            o = 2 * b + s
                            dve.wait_ge(*q_ps.at(j, o + 1))
                            if o == 0:
                                dve.wait_ge(*rope_in.at(j, 16))
                                dve.wait_ge(*o_ps.at(j, 0))
                            if s == 1:
                                dve.wait_ge(*q_done.at(j, max(0, b - 1)))
                            dve.scalar_tensor_tensor(out=(qtmp[:, b % 2, :] if s else qr[:, b, :]),
                                                     in0=ps[:, 4 + (2 + o) % 4, :], scalar=col(bias, b),
                                                     in1=rope[:, s, :], op0=ALU.add, op1=ALU.mult
                                                     ).then_inc(rot_done.sem, 1)
                for tile in range(NT):
                    if t == T_S + 2 * tile:
                        s8 = ps[:, 4:6, :].rearrange("p a (h n) -> p (a h) n", n=KEYS)
                        dve.wait_ge(*s_ps.at(j, tile + 1))
                        dve.wait_ge(*sub_done.at(j, tile))
                        dve.tensor_reduce(mx[:, :], s8, AX.X, ALU.max).then_inc(mx_done.sem, 1)
                        dve.wait_ge(*mx_done.at(j, tile + 1))
                        dve.wait_ge(*pt_ps.at(j, tile))
                        dve.tensor_tensor(prob.rearrange("p (h n) -> p h n", h=HEADS), s8,
                                          mx[:, :].rearrange("p (h o) -> p h o", o=1).to_broadcast([P, HEADS, KEYS]),
                                          ALU.subtract).then_inc(sub_done.sem, 1)
                    if t == T_PT + 2 * tile:
                        if tile:
                            residual(j, tile - 1)
                        heads = ps[:, 4, 0:HEADS * (HD + 1)].rearrange("p (h d) -> p h d", h=HEADS)
                        dve.wait_ge(*av_ps.at(j, tile + 1))
                        dve.wait_ge(*on_done.at(j, tile))
                        dve.reciprocal(rec[:, :], heads[:, :, HD]).then_inc(rec_done.sem, 1)
                        dve.wait_ge(*rec_done.at(j, tile + 1))
                        dve.wait_ge(*ont_ps.at(j, tile))
                        dve.tensor_tensor(on[:, :].rearrange("p (h d) -> p h d", h=HEADS), heads[:, :, 0:HD],
                                          rec[:, :].rearrange("p (h o) -> p h o", o=1).to_broadcast([P, HEADS, HD]),
                                          ALU.mult).then_inc(on_done.sem, 1)
                if t == T_RES3:
                    residual(j, NT - 1)
                    layer_norm(j, "xl", xa, xa, xa_done, xl_done)
                if t == T_FFN:
                    for tile in range(NT):
                        dve.wait_ge(*f_ps.at(j, tile // 2 * 2 + 2))
                        dve.scalar_tensor_tensor(out=x2[:, tile, :], in0=ps[:, 6 + tile // 2, tile % 2 * DM:(tile % 2 + 1) * DM],
                                                 scalar=0.0, in1=x1[:, tile, :], op0=ALU.max, op1=ALU.add
                                                 ).then_inc(f_done.sem, 1)
                    layer_norm(j, "x2", x2, x2, f_done, x2_done)
                if t == T_GATE:
                    top_two(j)
                e, ib = divmod(t - T_EXP, 2)
                if 0 <= e < ALL:
                    c = 2 * e + ib
                    dve.wait_ge(*th_done.at(j, c + 1))
                    if e < EXPERTS:
                        dve.wait_ge(*gac_done.at(j, c + 1))
                    else:
                        dve.wait_ge(*ga_done.at(j, c + 1))
                    dve.wait_ge(*hh_done.at(j, max(0, c - 1)))
                    dve.scalar_tensor_tensor(out=gm[:, ib, :], in0=th[:, ib, :], scalar=1.0,
                                             in1=(gac if e < EXPERTS else ga)[:, ib, :],
                                             op0=ALU.add, op1=ALU.mult).then_inc(gm_done.sem, 1)
                    dve.wait_ge(*gm_done.at(j, c + 1))
                    dve.wait_ge(*ab_ps.at(j, c + 1))
                    dve.wait_ge(*o_ps.at(j, max(0, c - 1)))
                    dve.scalar_tensor_tensor(out=hh[:, ib, :], in0=ps[:, 5, :], scalar=col("b3", c),
                                             in1=gm[:, ib, :], op0=ALU.add, op1=ALU.mult).then_inc(hh_done.sem, 1)
                if t == T_OUT:
                    for tile in range(NT):
                        dve.wait_ge(*o_ps.at(j, 2 * ALL))
                        dve.tensor_tensor(xa[:, tile, :], ps[:, 6 + tile // 2, tile % 2 * DM:(tile % 2 + 1) * DM],
                                          x2[:, tile, :], ALU.add).then_inc(xo_done.sem, 1)
                    layer_norm(j, "xo", xa, xa, xo_done, fin_done)

            def top_two(j):
                wide = lambda a: a.to_broadcast([P, NT, EXPERTS])
                dve.wait_ge(*lg_ps.at(j, 1))
                dve.tensor_copy(lg[:, :, :].rearrange("p t e -> p (t e)"), ps[:, 6, 0:NT * EXPERTS]
                                ).then_inc(lg_done.sem, 1)
                dve.wait_ge(*lg_done.at(j, 1))
                dve.memset(carrier[0:1, 4:5], 0.0).then_inc(m8_done.sem, 1)
                for t in range(NT):
                    last = dve.max(m8[:, t, :], lg[:, t, :])
                last.then_inc(m8_done.sem, 1)
                dve.wait_ge(*m8_done.at(j, 2))
                dve.tensor_tensor(ls[:, :, :], lg[:, :, :], wide(m8[:, :, 0:1]), ALU.subtract).then_inc(ls_done.sem, 1)
                for t in range(NT):
                    last = dve.max_index(i8[:, t, :], m8[:, t, :], lg[:, t, :])
                last.then_inc(i8_done.sem, 1)
                dve.wait_ge(*i8_done.at(j, 1))
                dve.tensor_copy(i2[:, :, :], i8[:, :, 0:2]).then_inc(top_done.sem, 1)
                dve.wait_ge(*top_done.at(j, 1))
                for s in range(2):
                    last = dve.tensor_tensor(mk[:, s, :, :],
                                             iota8[:, :].rearrange("p (o e) -> p o e", o=1).to_broadcast([P, NT, EXPERTS]),
                                             wide(i2[:, :, s:s + 1]), ALU.is_equal)
                last.then_inc(top_done.sem, 1)
                dve.wait_ge(*top_done.at(j, 2))
                dve.tensor_tensor(mk2[:, :, :], mk[:, 0, :, :], mk[:, 1, :, :], ALU.add).then_inc(top_done.sem, 1)
                dve.wait_ge(*el_done.at(j, 1))
                dve.tensor_reduce(se[:, :], el[:, :, :], AX.X, ALU.add).then_inc(top_done.sem, 1)
                dve.wait_ge(*top_done.at(j, 4))
                dve.reciprocal(re[:, :], se[:, :]).then_inc(top_done.sem, 1)
                dve.wait_ge(*top_done.at(j, 5))
                dve.tensor_tensor(pr[:, :, :], el[:, :, :], wide(re[:, :].rearrange("p (t o) -> p t o", o=1)), ALU.mult
                                  ).then_inc(top_done.sem, 2)
                dve.wait_ge(*top_done.at(j, 7))
                dve.tensor_tensor(comb[:, :, 0:EXPERTS], pr[:, :, :], mk2[:, :, :], ALU.mult).then_inc(comb_done.sem, 1)

            streams(dve, mixer, second)
        return signals


def _swap(a):
    return a.reshape(*a.shape[:-1], -1, 2)[..., ::-1].reshape(a.shape)


def _pairs(a, t):
    n = a.shape[0]
    return np.concatenate([a.reshape(n, HEADS, HD), t.reshape(n, HEADS, HD)], axis=2).reshape(n, 2 * DM)


def _rope_tables(positions):
    inv = (1.0 / 10000.0 ** (np.arange(0, HD, 2, dtype=np.float32) / np.float32(HD))).astype(np.float32)
    freqs = positions.astype(np.float32)[:, None] * inv[None, :]
    emb = np.concatenate([freqs, freqs], axis=-1).T
    sign = np.where(np.arange(HD) % 2 == 0, -1.0, 1.0).astype(np.float32)[:, None]
    cos, sin = np.cos(emb).astype(np.float32), (np.sin(emb) * sign).astype(np.float32)
    return np.stack([np.tile(cos, (P // HD, 1)), np.tile(sin, (P // HD, 1))])


def _layout(I):
    A = {k: np.asarray(v) for k, v in I.items()}
    a = lambda k: A["L0_attn_" + k]
    c = lambda k: A["L0_xattn_" + k][3]
    f = lambda k: A["L0_ffn_" + k]
    by_row = lambda w: np.ascontiguousarray(w.reshape(-1, P, *w.shape[1:]).swapaxes(0, 1)).reshape(P, -1)
    pair_w = lambda m, n: _pairs(c(m).T, c(n).T)
    pair_b = lambda m, n: _pairs(c(m)[None], c(n)[None])[0]
    bq, bk = pair_b("b_qa", "b_qt"), pair_b("b_ka", "b_kt")
    parts = {
        "norm_w": by_row(a("norm_w")), "conv_w": by_row(a("conv_w")), "conv_b": by_row(a("conv_b")),
        "dt_b": by_row(a("dt_proj_b")), "skip": by_row(a("D")), "A_log": by_row(a("A_log")),
        "bq": by_row(bq), "bq_swap": by_row(_swap(bq)), "bk": by_row(bk), "bk_swap": by_row(_swap(bk)),
        "gamma": by_row(c("gamma")), "beta": by_row(c("beta")),
        "b1": by_row(np.concatenate([f("b1").reshape(-1), f("sb1")])),
        "b3": by_row(np.concatenate([f("b3").reshape(-1), f("sb3")])),
        "gate": np.broadcast_to(c("gating_factor").reshape(1, 1), (P, 1)),
    }
    wq, wk = pair_w("W_qa", "W_qt"), pair_w("W_ka", "W_kt")
    stack = lambda w, s: np.concatenate([f(w), f(s)[None]]).reshape(ALL, KD, P, DM).swapaxes(1, 2)
    experts = np.stack([stack("w1", "sw1"), stack("w3", "sw3"), stack("w2", "sw2")], axis=2).reshape(ALL, P, 3 * KD * DM)
    pos = np.arange(SEQ).reshape(CPS, TC)
    arrays = {
        "x": A["x"].reshape(CHUNKS, NT, P, DM),
        "w_in": a("in_proj_w").T, "w_out": a("out_proj_w").T, "w_xp": a("x_proj_w").T, "w_dt": a("dt_proj_w").T,
        "w_q": wq, "w_qs": _swap(wq), "w_k": wk, "w_ks": _swap(wk),
        "w_v": np.concatenate([c("W_va").T, c("W_vt").T], axis=1),
        "w_o": c("W_o").T, "w_f": c("W_ffn").T, "w_gate": f("gate_w").T,
        "experts": experts, "b2": np.concatenate([f("b2"), f("sb2")[None]]),
        "vecs": np.concatenate([parts[k] for k in VEC], axis=1),
        "rows": np.stack([c("b_va"), c("b_vt"), c("b_o"), c("b_ffn")]).reshape(1, -1),
        "ctx_t": A["ctx_1024"].reshape(SEQS * CTX, DM).T,
        "rope_q": np.stack([_rope_tables(pos[k % CPS]) for k in range(CHUNKS)]),
        "rope_k": _rope_tables(np.tile(np.arange(CTX), SEQS)),
    }
    return {k: np.ascontiguousarray(v) for k, v in arrays.items()}


def kernel(**inputs):
    import concourse.bacc as bacc
    from concourse.bass_utils import run_bass_kernel_spmd

    nc = bacc.Bacc("TRN2", target_bir_lowering=False, num_devices=1)
    arrays = _layout(inputs)
    args = [nc.dram_tensor(f"in_{n}", a.shape, mybir.dt.from_np(a.dtype), kind="ExternalInput").ap()
            for n, a in arrays.items()]
    out = nc.dram_tensor("out", (CHUNKS, NT, P, DM), F32, kind="ExternalOutput").ap()
    block_kernel(nc, *args, out)
    r = run_bass_kernel_spmd(nc, [{f"in_{n}": a for n, a in arrays.items()}], core_ids=[0])
    return r.results[0]["out"].reshape(SEQS, SEQ, DM)
```

```python
from contextlib import ExitStack

import numpy as np

import concourse.bass as bass
from concourse import mybir

F32 = mybir.dt.float32
I32 = mybir.dt.int32
U32 = mybir.dt.uint32
ALU = mybir.AluOpType
ACT = mybir.ActivationFunctionType
AX = mybir.AxisListType

P = 128
SEQS, SEQ = 2, 1024
DM = 256
KD = DM // P
DI = 2 * DM
Q = DI // P
NS = 16
RANK = 16
TAPS = 4
TC = 512
NT = TC // P
CHUNKS = SEQS * SEQ // TC
CPS = SEQ // TC
HEADS, HD = 8, 32
HB = HEADS // 2
CTX = 64
KEYS = 2 * CTX
EXPERTS = 8
ALL = EXPERTS + 1
WRING, CRING = 2, 2
EPS = 1e-5
LINEAR = 30.0

VEC = {}
_at = 0
for _name, _n in (("norm_w", KD), ("conv_w", Q * TAPS), ("conv_b", Q), ("dt_b", Q), ("skip", Q), ("A_log", Q * NS),
                  ("bq", HB), ("bq_swap", HB), ("bk", HB), ("bk_swap", HB), ("gamma", KD), ("beta", KD),
                  ("b1", ALL * KD), ("b3", ALL * KD), ("gate", 1)):
    VEC[_name] = (_at, _at + _n)
    _at += _n
VECS = _at

T_X1T, T_Q, T_S, T_PT = 0, 1, 3, 4
T_RES = T_PT + 2 * (NT - 1) + 4
T_LNT, T_FFN, T_X2, T_X2T, T_GATE, T_TOP = range(T_RES + 1, T_RES + 7)
T_EXP = T_TOP
T_OUT = T_EXP + 2 * ALL + 2
PRE_TICKS = 6
SCAN_TICKS = 2 * NS + 3


def schedule():
    tick = lambda t: [("early", t), ("late", t)]
    steps = [("post", 0), ("pre", 0), ("post", 1), ("pre", 1), ("post", 2), ("pre", 2), ("post", 3)]
    steps += tick(0) + [("pre", 3)] + tick(1) + [("pre", 4)] + tick(2) + [("pre", 5)] + tick(3) + tick(4) + tick(5)
    for s in range(max(SCAN_TICKS, T_OUT + 1 - PRE_TICKS)):
        steps += [("early", PRE_TICKS + s), ("scan", s), ("late", PRE_TICKS + s)]
    return steps


SCHEDULE = schedule()


class Signal:

    def __init__(self, sem, per):
        self.sem, self.per = sem, per

    def at(self, j, k):
        return self.sem, j * self.per + k + 1


def is_first(j):
    return isinstance(j, int) and j == 0


def block_kernel(nc, x, w_in, w_out, w_xp, w_dt, w_q, w_qs, w_k, w_ks, w_v, w_o, w_f, w_gate, experts, b2, vecs, rows,
                 ctx_t, rope_q, rope_k, out):
    ctx = ExitStack()
    with ctx:
        def sb(name, shape, dt=F32):
            return ctx.enter_context(nc.sbuf_tensor(name, shape, dt))

        def signal(name, per):
            s = Signal(ctx.enter_context(nc.semaphore(name)), per)
            signals[name] = s
            return s

        signals = {}
        ps = ctx.enter_context(nc.psum_tensor("ps", [P, 8, 512], F32))

        win = sb("win", [P, KD, 2 * DI])
        wout = sb("wout", [P, Q, DM])
        wxp = sb("wxp", [P, Q, RANK + 2 * NS])
        wdt = sb("wdt", [RANK, DI])
        wq = sb("wq", [P, KD, 2 * DM])
        wqs = sb("wqs", [P, KD, 2 * DM])
        wo = sb("wo", [P, KD, DM])
        wf = sb("wf", [P, KD, DM])
        wgate = sb("wgate", [P, KD, EXPERTS])
        b2s = sb("b2s", [ALL, DM])
        vec = sb("vec", [P, VECS])
        row = sb("row", [1, 4, DM])
        kblk = sb("kblk", [P, SEQS, HB * 2 * KEYS])
        vx = sb("vx", [P, SEQS, HEADS * (HD + 1)])
        conv = sb("conv", [P, Q, TAPS, P])
        ident = sb("ident", [P, P])
        ones = sb("ones", [1, P])
        iota_i = sb("iota_i", [P, EXPERTS], I32)
        iota8 = sb("iota8", [P, EXPERTS])
        keep = sb("keep", [P, CHUNKS])
        power = sb("power", [P, NT])
        neg_a = sb("neg_a", [P, Q * NS])
        half_b1 = sb("half_b1", [P, ALL * KD])
        ratio = sb("ratio", [P, 4])

        xt = sb("xt", [P, NT, DM])
        u = sb("u", [P, Q, TC])
        sz = sb("sz", [P, Q, TC])
        delta = sb("delta", [P, Q, TC])
        v = sb("v", [P, Q, TC])
        bbc = sb("bbc", [P, 2, 2, TC])
        dbu = sb("dbu", [P, 2, Q, TC])
        hs = sb("hs", [P, 2, Q, TC + 4])
        yacc = sb("yacc", [P, NT, DI])
        hist = sb("hist", [P, Q, TAPS - 1])
        carry = sb("carry", [P, NS, Q])
        ctok = sb("ctok", [P, NT, NS])
        rows_t = sb("rows_t", [64, TC])
        dtr, brow = rows_t[0:RANK, :], rows_t[32:32 + NS, :]
        ssq = sb("ssq", [P, NT])
        ms = sb("ms", [P, NT])
        rms = sb("rms", [P, NT])
        xi = hs[:, 1, :, :]
        xn = yacc[:, 0:NT // 2, :].rearrange("p a (b d) -> p (a b) d", b=2)
        xnt = yacc[:, NT // 2:NT, :]

        x1 = sb("x1", [P, NT, DM])
        x1t = sb("x1t", [P, KD, TC])
        work = sb("work", [P, 4096 + 1024])
        qr = work[:, 0:2048].rearrange("p (b t) -> p b t", b=HB)
        qtmp = work[:, 2048:3072].rearrange("p (a t) -> p a t", a=2)
        prob = work[:, 3072:4096]
        probt = work[:, 4096:5120]
        th = work[:, 0:1024].rearrange("p (a t) -> p a t", a=2)
        ga = work[:, 1024:2048].rearrange("p (a t) -> p a t", a=2)
        gac = work[:, 2048:3072].rearrange("p (a t) -> p a t", a=2)
        gm = work[:, 3072:4096].rearrange("p (a t) -> p a t", a=2)
        hh = work[:, 4096:5120].rearrange("p (a t) -> p a t", a=2)
        rope = sb("rope", [P, 2, TC])
        mx = sb("mx", [P, HEADS])
        rec = sb("rec", [P, HEADS])
        on = sb("on", [P, DM])
        ont = sb("ont", [P, KD, P])
        xa = sb("xa", [P, NT, DM])
        x2 = sb("x2", [P, NT, DM])
        x2t = sb("x2t", [P, KD, TC])
        lg = sb("lg", [P, NT, EXPERTS])
        m8 = sb("m8", [P, NT, 8])
        i8 = sb("i8", [P, NT, 8], U32)
        i2 = sb("i2", [P, NT, 2])
        ls = sb("ls", [P, NT, EXPERTS])
        el = sb("el", [P, NT, EXPERTS])
        se = sb("se", [P, NT])
        re = sb("re", [P, NT])
        pr = sb("pr", [P, NT, EXPERTS])
        mk = sb("mk", [P, 2, NT, EXPERTS])
        mk2 = sb("mk2", [P, NT, EXPERTS])
        comb = sb("comb", [P, NT, ALL])
        combt = sb("combt", [ALL, TC])
        we = sb("we", [P, WRING, 3, KD * DM])
        cbc = sb("cbc", [P, CRING, TC])
        carrier = sb("carrier", [1, 8])
        stat, mv, ve, rstd = ({k: sb(f"{name}_{k}", [P, NT * n]) for k in ("x1", "xl", "x2", "xo")}
                              for name, n in (("stat", 6), ("mv", 2), ("ve", 1), ("rstd", 1)))

        ctxt = work[:, 0:KD * P].rearrange("p (k n) -> p k n", k=KD)
        ropek = work[:, 256:512].rearrange("p (a n) -> p a n", a=2)
        krot = work[:, 512:1536].rearrange("p (a b n) -> p a b n", a=2, b=HB)
        ksum = work[:, 1536:2048].rearrange("p (b n) -> p b n", b=HB)
        wk = work[:, 2048:3072].rearrange("p (k n) -> p k n", k=KD)
        wks = work[:, 3072:4096].rearrange("p (k n) -> p k n", k=KD)
        wv = work[:, 4096:5120].rearrange("p (k n) -> p k n", k=KD)

        brow_dram = nc.dram_tensor("brow_dram", (NS, TC), F32, kind="Internal").ap()
        comb_dram = nc.dram_tensor("comb_dram", (ALL, TC), F32, kind="Internal").ap()

        def col(name, i=0, n=1):
            a = VEC[name][0] + i
            return vec[:, a:a + n]

        one = lambda name: signal(name, 0)
        w_setup, w_mix, w_att = one("w_setup"), one("w_mix"), one("w_att")
        consts, ident_set, zeroed, iota_set = one("consts"), one("ident_set"), one("zeroed"), one("iota_set")
        setup_act, setup_dve, setup_pe = one("setup_act"), one("setup_dve"), one("setup_pe")
        kv_done, conv_set = one("kv_done"), one("conv_set")

        x_in = signal("x_in", 16)
        xt_in = signal("xt_in", 16)
        sq_done = signal("sq_done", 1)
        ms_done = signal("ms_done", 1)
        rms_done = signal("rms_done", 1)
        xn_done = signal("xn_done", 1)
        xnt_ps = signal("xnt_ps", KD)
        xnt_done = signal("xnt_done", KD)
        xz_ps = signal("xz_ps", 2 * Q)
        hist_in = signal("hist_in", 1)
        xi_done = signal("xi_done", Q)
        sz_done = signal("sz_done", Q)
        conv_ps = signal("conv_ps", Q)
        hist_out = signal("hist_out", 1)
        u_done = signal("u_done", Q)
        xp_ps = signal("xp_ps", 3)
        dtr_done = signal("dtr_done", 1)
        brow_done = signal("brow_done", 1)
        ctok_done = signal("ctok_done", 1)
        brow_out = signal("brow_out", 16)
        bbc_in = [signal(f"bbc_in{s}", 16 * NS // 4) for s in range(2)]
        dp_ps = signal("dp_ps", Q)
        ymin_done = signal("ymin_done", Q)
        exp_done = signal("exp_done", Q)
        ln_done = signal("ln_done", Q)
        delta_done = signal("delta_done", Q)
        v_done = signal("v_done", Q)
        carry_kept = signal("carry_kept", 1)
        carry_done = signal("carry_done", NS)
        da_done = signal("da_done", NS * Q)
        dbu_done = signal("dbu_done", 2 * NS)
        scan_done = signal("scan_done", NS * Q)
        ht_ps = signal("ht_ps", NS * NT)
        y_done = signal("y_done", NS * NT)
        yt_ps = signal("yt_ps", Q)
        yd_done = signal("yd_done", Q)
        yg_done = signal("yg_done", Q)
        out_ps = signal("out_ps", NT)
        res_done = signal("res_done", NT)
        x1_done = signal("x1_done", NT)

        norm = {k: {s: signal(f"{k}_{s}", n) for s, n in (("stats", NT), ("held", 1), ("aggr", NT), ("ve", 1), ("rstd", 1))}
                for k in ("x1", "xl", "x2", "xo")}

        x1t_ps = signal("x1t_ps", KD)
        x1t_done = signal("x1t_done", KD)
        rope_in = signal("rope_in", 16)
        q_ps = signal("q_ps", 2 * HB)
        rot_done = signal("rot_done", 2 * HB)
        q_done = signal("q_done", HB)
        s_ps = signal("s_ps", NT)
        mx_done = signal("mx_done", NT)
        sub_done = signal("sub_done", NT)
        p_done = signal("p_done", NT)
        pt_ps = signal("pt_ps", NT)
        pt_done = signal("pt_done", NT)
        av_ps = signal("av_ps", NT)
        rec_done = signal("rec_done", NT)
        on_done = signal("on_done", NT)
        ont_ps = signal("ont_ps", NT)
        ont_done = signal("ont_done", NT)
        ao_ps = signal("ao_ps", NT)
        xa_done = signal("xa_done", NT)
        xl_done = signal("xl_done", NT)
        xlt_ps = signal("xlt_ps", KD)
        xlt_done = signal("xlt_done", KD)
        f_ps = signal("f_ps", NT)
        f_done = signal("f_done", NT)
        x2_done = signal("x2_done", NT)
        x2t_ps = signal("x2t_ps", KD)
        x2t_done = signal("x2t_done", KD)
        lg_ps = signal("lg_ps", 1)
        lg_done = signal("lg_done", 1)
        m8_done = signal("m8_done", 2)
        i8_done = signal("i8_done", 1)
        ls_done = signal("ls_done", 1)
        el_done = signal("el_done", 1)
        top_done = signal("top_done", 7)
        comb_done = signal("comb_done", 1)
        combt_ps = signal("combt_ps", 1)
        combt_done = signal("combt_done", 1)
        comb_out = signal("comb_out", 16)
        cbc_in = [signal(f"cbc_in{s}", 16 * len(range(s, EXPERTS, CRING))) for s in range(CRING)]
        we_in = [signal(f"we_in{s}", 16 * len(range(s, ALL, WRING))) for s in range(WRING)]
        w2_in = [signal(f"w2_in{s}", 16 * len(range(s, ALL, WRING))) for s in range(WRING)]
        a_ps = signal("a_ps", 2 * ALL)
        b_ps = signal("b_ps", 2 * ALL)
        th_done = signal("th_done", 2 * ALL)
        ga_done = signal("ga_done", 2 * ALL)
        gac_done = signal("gac_done", 2 * EXPERTS)
        gm_done = signal("gm_done", 2 * ALL)
        hh_done = signal("hh_done", 2 * ALL)
        o_ps = signal("o_ps", 2 * ALL)
        xo_done = signal("xo_done", NT)
        fin_done = signal("fin_done", NT)
        out_store = signal("out_store", 16)

        block = ctx.enter_context(nc.Block())

        def streams(eng, mixer, second):
            def body(i, first, last):
                for kind, step in SCHEDULE:
                    if kind in ("early", "late"):
                        if not first:
                            second(i - 1, step, kind == "early")
                    elif kind == "post":
                        if not first:
                            mixer(i - 1, kind, step)
                    elif not last:
                        mixer(i, kind, step)

            body(0, True, False)
            with eng.Fori(1, CHUNKS, 1) as i:
                body(i, False, False)
            body(CHUNKS, False, True)

        @block.sync
        def _(sp):
            for dst, src in ((ctxt, ctx_t), (wk, w_k), (wks, w_ks), (wv, w_v)):
                sp.dma_start(dst, src.rearrange("(k p) n -> p k n", p=P)).then_inc(w_setup.sem, 16)
            sp.dma_start(ropek, rope_k.rearrange("a p n -> p a n")).then_inc(w_setup.sem, 16)
            sp.dma_start(row[:, :, :].rearrange("o a n -> o (a n)"), rows).then_inc(w_setup.sem, 16)
            sp.dma_start(vec[:, :], vecs).then_inc(w_setup.sem, 16)
            sp.dma_start(win[:, :, :], w_in.rearrange("(k p) n -> p k n", p=P)).then_inc(w_mix.sem, 16)
            sp.dma_start(wxp[:, :, :], w_xp.rearrange("(k p) n -> p k n", p=P)).then_inc(w_mix.sem, 16)
            sp.dma_start(wdt[:, :], w_dt).then_inc(w_mix.sem, 16)
            sp.dma_start(wout[:, :, :], w_out.rearrange("(k p) n -> p k n", p=P)).then_inc(w_mix.sem, 16)
            for dst, src in ((wq, w_q), (wqs, w_qs), (wo, w_o), (wf, w_f), (wgate, w_gate)):
                sp.dma_start(dst[:, :, :], src.rearrange("(k p) n -> p k n", p=P)).then_inc(w_att.sem, 16)
            sp.dma_start(b2s[:, :], b2).then_inc(w_att.sem, 16)

            def load_bbc(j, pair):
                if pair >= 2:
                    sp.wait_ge(*dbu_done.at(j, 2 * (2 * pair - 2)))
                sp.dma_start(bbc[:, pair % 2, :, :].rearrange("p a t -> p (a t)"),
                             brow_dram[2 * pair:2 * pair + 2, :].rearrange("a t -> (a t)").partition_broadcast(P)
                             ).then_inc(bbc_in[pair % 2].sem, 16)

            def mixer(j, kind, n):
                if kind == "pre" and n == 0:
                    sp.wait_ge(*yt_ps.at(j, 0))
                    sp.dma_start(xn, x[bass.ds(j, 1)].rearrange("a t p d -> p (a t) d")
                                 ).then_inc(x_in.sem, 16)
                if kind == "pre" and n == 2:
                    sp.wait_ge(*res_done.at(j, 0))
                    sp.dma_start(xt[:, :, :], x[bass.ds(j, 1)].rearrange("a t p d -> p (a t) d")
                                 ).then_inc(xt_in.sem, 16)
                if kind == "pre" and n == 4:
                    sp.wait_ge(*brow_done.at(j, 1))
                    sp.dma_start(brow_dram, brow).then_inc(brow_out.sem, 16)
                    sp.wait_ge(*brow_out.at(j, 16))
                    load_bbc(j, 0)
                    load_bbc(j, 1)
                if kind == "scan" and n % 4 == 3 and (n + 5) // 4 < NS // 2:
                    load_bbc(j, (n + 5) // 4)

            def load_gates(j, e):
                if e >= WRING:
                    sp.wait_ge(*b_ps.at(j, 2 * (e - WRING) + 2))
                else:
                    sp.wait_ge(*b_ps.at(j, 0))
                sp.dma_start(we[:, e % WRING, 0:2, :].rearrange("p a n -> p (a n)"), experts[e, :, 0:2 * KD * DM]
                             ).then_inc(we_in[e % WRING].sem, 16)

            def load_second(j, e):
                if e >= WRING:
                    sp.wait_ge(*o_ps.at(j, 2 * (e - WRING) + 2))
                else:
                    sp.wait_ge(*o_ps.at(j, 0))
                sp.dma_start(we[:, e % WRING, 2, :], experts[e, :, 2 * KD * DM:3 * KD * DM]
                             ).then_inc(w2_in[e % WRING].sem, 16)

            def load_comb(j, e):
                if e >= CRING:
                    sp.wait_ge(*gac_done.at(j, 2 * (e - CRING) + 2))
                sp.dma_start(cbc[:, e % CRING, :], comb_dram[e, :].partition_broadcast(P)
                             ).then_inc(cbc_in[e % CRING].sem, 16)

            def second(j, t, early):
                if early:
                    return
                if t == 0:
                    sp.wait_ge(*rot_done.at(j, 0))
                    sp.dma_start(rope[:, :, :], rope_q[bass.ds(j, 1)].rearrange("c a p t -> p (c a) t")
                                 ).then_inc(rope_in.sem, 16)
                if t == T_LNT:
                    for e in range(WRING):
                        load_gates(j, e)
                        load_second(j, e)
                if t == T_TOP:
                    sp.wait_ge(*combt_done.at(j, 1))
                    sp.dma_start(comb_dram, combt[0:ALL, :]).then_inc(comb_out.sem, 16)
                    sp.wait_ge(*comb_out.at(j, 16))
                    for e in range(CRING):
                        load_comb(j, e)
                e, part = divmod(t - T_EXP - 2, 2)
                if 0 <= e < ALL and part == 0:
                    if e + WRING < ALL:
                        load_gates(j, e + WRING)
                    if e + CRING < EXPERTS:
                        load_comb(j, e + CRING)
                if 0 <= e < ALL and part == 1 and e + WRING < ALL:
                    load_second(j, e + WRING)
                if t == T_OUT:
                    sp.wait_ge(*fin_done.at(j, NT))
                    sp.dma_start(out[bass.ds(j, 1)].rearrange("a t p d -> p (a t) d"), xa[:, :, :]
                                 ).then_inc(out_store.sem, 16)

            streams(sp, mixer, second)
            sp.wait_ge(*out_store.at(CHUNKS, 0))

        @block.gpsimd
        def _(pool):
            for s in signals.values():
                if s.per:
                    pool.sem_inc(s.sem, 1)
            pool.memset(ident[:, :], 0.0).then_inc(zeroed.sem, 1)
            pool.memset(ones[:, :], 1.0).then_inc(consts.sem, 1)
            pool.memset(power[:, :], -0.5).then_inc(consts.sem, 1)
            for c in range(CHUNKS):
                pool.memset(keep[:, c:c + 1], 0.0 if c % CPS == 0 else 1.0).then_inc(consts.sem, 1)
            pool.memset(kblk[:, :, :], 0.0).then_inc(consts.sem, 1)
            pool.memset(vx[:, :, :], 1.0).then_inc(consts.sem, 1)
            pool.memset(carry[:, :, :], 0.0).then_inc(consts.sem, 1)
            pool.memset(hist[:, :, :], 0.0).then_inc(consts.sem, 1)
            pool.memset(comb[:, :, :], 1.0).then_inc(consts.sem, 1)
            pool.iota(iota_i[:, :], pattern=[[1, EXPERTS]], base=0, channel_multiplier=0).then_inc(iota_set.sem, 1)
            pool.wait_ge(zeroed.sem, 1)
            pool.affine_select(out=ident[:, :], in_=ident[:, :], compare_op=ALU.not_equal, fill=1.0,
                               base=0, pattern=[[-1, P]], channel_multiplier=1).then_inc(ident_set.sem, 1)

            def mixer(j, kind, n):
                if kind == "pre" and n == 0:
                    pool.wait_ge(*ms_done.at(j, 1))
                    if is_first(j):
                        pool.wait_ge(consts.sem, 7 + CHUNKS)
                    pool.tensor_tensor(rms[:, :], ms[:, :], power[:, :], ALU.pow).then_inc(rms_done.sem, 1)
                if kind == "scan":
                    if n == 0:
                        inputs(j, 0)
                    if n + 1 < 2 * NS:
                        inputs(j, n + 1)
                if kind == "post" and n == 2:
                    rstd_of(j, "x1")

            def inputs(j, i):
                n, h = divmod(i, 2)
                pool.wait_ge(*bbc_in[n // 2 % 2].at(j, 16 * (n // 4 + 1)))
                if i == 0:
                    pool.wait_ge(*v_done.at(j, Q))
                pool.wait_ge(*scan_done.at(j, max(0, 2 * i - 6)))
                pool.tensor_tensor(dbu[:, n % 2, 2 * h:2 * h + 2, :], v[:, 2 * h:2 * h + 2, :],
                                   bbc[:, n // 2 % 2, n % 2, :].rearrange("p (o t) -> p o t", o=1)
                                   .to_broadcast([P, 2, TC]), ALU.mult).then_inc(dbu_done.sem, 1)

            def rstd_of(j, k):
                pool.wait_ge(*norm[k]["ve"].at(j, 1))
                pool.tensor_tensor(rstd[k][:, :], ve[k][:, :], power[:, :], ALU.pow
                                   ).then_inc(norm[k]["rstd"].sem, 1)

            def second(j, t, early):
                if early:
                    if t in (T_RES, T_X2):
                        rstd_of(j, "xl" if t == T_RES else "x2")
                    return
                if t in (T_Q, T_Q + 1):
                    for b in range(2 * (t - T_Q), 2 * (t - T_Q) + 2):
                        pool.wait_ge(*rot_done.at(j, 2 * b + 2))
                        pool.tensor_tensor(qr[:, b, :], qr[:, b, :], qtmp[:, b % 2, :], ALU.add
                                           ).then_inc(q_done.sem, 1)
                c = t - T_EXP - 1
                if 0 <= c < 2 * EXPERTS:
                    e, ib = divmod(c, 2)
                    pool.wait_ge(*ga_done.at(j, c + 1))
                    pool.wait_ge(*cbc_in[e % CRING].at(j, 16 * (e // CRING + 1)))
                    pool.wait_ge(*gm_done.at(j, max(0, c - 1)))
                    pool.tensor_tensor(gac[:, ib, :], ga[:, ib, :], cbc[:, e % CRING, :], ALU.mult
                                       ).then_inc(gac_done.sem, 1)
                if t == T_OUT:
                    rstd_of(j, "xo")

            streams(pool, mixer, second)

        @block.scalar
        def _(act):
            act.preload_act_table(ACT.Exp)
            act.wait_ge(w_setup.sem, 7 * 16)
            act.activation(neg_a[:, :], col("A_log", 0, Q * NS), ACT.Exp).then_inc(setup_act.sem, 1)
            act.activation(ratio[:, 0:1], col("gate"), ACT.Exp, scale=-1.0).then_inc(setup_act.sem, 1)

            def mixer(j, kind, n):
                if kind == "pre" and n == 0:
                    act.wait_ge(*x_in.at(j, 16))
                    for t in range(NT):
                        last = act.activation(xnt[:, t // 2, t % 2 * DM:(t % 2 + 1) * DM], xn[:, t, :], ACT.Square,
                                              accum_out=ssq[:, t:t + 1])
                    last.then_inc(sq_done.sem, 1)
                if kind == "pre" and n == 1:
                    for k in range(KD):
                        act.wait_ge(*xnt_ps.at(j, k + 1))
                        act.activation(xnt[:, k, :], ps[:, k, :], ACT.Copy, scale=col("norm_w", k)
                                       ).then_inc(xnt_done.sem, 1)
                if kind == "pre" and n == 2:
                    act.wait_ge(*yg_done.at(j, 0))
                    for q in range(Q):
                        act.wait_ge(*xz_ps.at(j, Q + q + 1))
                        act.activation(sz[:, q, :], ps[:, q, :], ACT.Silu).then_inc(sz_done.sem, 1)
                if kind == "pre" and n == 3:
                    for q in range(Q):
                        act.wait_ge(*conv_ps.at(j, q + 1))
                        act.activation(u[:, q, :], ps[:, q, :], ACT.Silu, bias=col("conv_b", q)
                                       ).then_inc(u_done.sem, 1)
                if kind == "pre" and n == 4:
                    act.wait_ge(*xp_ps.at(j, 1))
                    act.activation(dtr, ps[0:RANK, 2, :], ACT.Copy).then_inc(dtr_done.sem, 1)
                    act.wait_ge(*xp_ps.at(j, 2))
                    act.wait_ge(*brow_out.at(j, 0))
                    act.activation(brow, ps[32:32 + NS, 3, :], ACT.Copy).then_inc(brow_done.sem, 1)
                if kind == "pre" and n == 5:
                    for q in range(Q):
                        act.wait_ge(*ymin_done.at(j, q + 1))
                        act.activation(delta[:, q, :], delta[:, q, :], ACT.Exp).then_inc(exp_done.sem, 1)
                    for q in range(Q):
                        act.wait_ge(*exp_done.at(j, q + 1))
                        act.activation(delta[:, q, :], delta[:, q, :], ACT.Ln, bias=1.0).then_inc(ln_done.sem, 1)
                if kind == "scan":
                    for unit in range(2 * n + 2 if n else 0, min(2 * n + 4, NS * Q)):
                        if unit == 0:
                            act.wait_ge(*delta_done.at(j, Q))
                        m, q = divmod(unit, Q)
                        act.wait_ge(*scan_done.at(j, max(0, unit - 1)))
                        act.activation(ps[:, unit % 2, :], delta[:, q, :], ACT.Exp,
                                       scale=neg_a[:, q * NS + m:q * NS + m + 1]).then_inc(da_done.sem, 1)
                    m = n // 2 - 1
                    if n % 2 == 0 and 0 <= m < NS:
                        act.wait_ge(*scan_done.at(j, Q * (m + 1)))
                        act.activation(carry[:, m, :], hs[:, m % 2, :, TC - 1], ACT.Copy).then_inc(carry_done.sem, 1)

            def second(j, t, early):
                if not early:
                    if t == T_X1T:
                        for k in range(KD):
                            act.wait_ge(*x1t_ps.at(j, k + 1))
                            act.activation(x1t[:, k, :], ps[:, 4 + k, :], ACT.Copy).then_inc(x1t_done.sem, 1)
                    if t == T_TOP:
                        act.wait_ge(*ls_done.at(j, 1))
                        act.activation(el[:, :, :], ls[:, :, :], ACT.Exp).then_inc(el_done.sem, 1)
                        act.wait_ge(*combt_ps.at(j, 1))
                        act.wait_ge(*comb_out.at(j, 0))
                        act.activation(combt[:, :], ps[0:ALL, 7, :], ACT.Copy).then_inc(combt_done.sem, 1)
                    return
                for tile in range(NT):
                    if t == T_PT + 2 * tile:
                        act.wait_ge(*sub_done.at(j, tile + 1))
                        act.activation(prob, prob, ACT.Exp, scale=HD ** -0.5).then_inc(p_done.sem, 1)
                    if t == T_PT + 2 * tile + 1:
                        act.wait_ge(*pt_ps.at(j, tile + 1))
                        act.wait_ge(*av_ps.at(j, tile))
                        act.activation(probt.rearrange("p (a n) -> p a n", a=2), ps[:, 6:8, :], ACT.Copy
                                       ).then_inc(pt_done.sem, 1)
                    if t == T_PT + 2 * tile + 3:
                        act.wait_ge(*ont_ps.at(j, tile + 1))
                        act.wait_ge(*ao_ps.at(j, tile))
                        act.activation(ont[:, :, :], ps[:, 5, 0:DM].rearrange("p (k n) -> p k n", k=KD), ACT.Copy
                                       ).then_inc(ont_done.sem, 1)
                if t == T_FFN:
                    for k in range(KD):
                        act.wait_ge(*xlt_ps.at(j, k + 1))
                        act.activation(x1t[:, k, :], ps[:, 4 + k, :], ACT.Identity, scale=col("gamma", k),
                                       bias=col("beta", k)).then_inc(xlt_done.sem, 1)
                if t == T_GATE:
                    for k in range(KD):
                        act.wait_ge(*x2t_ps.at(j, k + 1))
                        act.activation(x2t[:, k, :], ps[:, 4 + k, :], ACT.Copy).then_inc(x2t_done.sem, 1)
                c = t - T_EXP
                if 0 <= c < 2 * ALL:
                    ib = c % 2
                    bias = half_b1[:, c:c + 1]
                    act.wait_ge(*a_ps.at(j, c + 1))
                    act.wait_ge(*gm_done.at(j, max(0, c - 1)))
                    act.activation(ga[:, ib, :], ps[:, 4, :], ACT.Identity, scale=0.5, bias=bias
                                   ).then_inc(ga_done.sem, 1)
                    act.activation(th[:, ib, :], ps[:, 4, :], ACT.Tanh, scale=0.5, bias=bias
                                   ).then_inc(th_done.sem, 1)

            streams(act, mixer, second)

        @block.tensor
        def _(pe):
            pe.wait_ge(w_setup.sem, 7 * 16)
            for s, w in enumerate((wk, wks)):
                for b in range(HB):
                    for k in range(KD):
                        last = pe.matmul(ps[:, 4 + s, b * P:(b + 1) * P], w[:, k, b * P:(b + 1) * P], ctxt[:, k, :],
                                         start=(k == 0), stop=(k == KD - 1))
            last.then_inc(setup_pe.sem, 1)
            pe.wait_ge(consts.sem, 7 + CHUNKS)
            for s in range(SEQS):
                for a in range(2):
                    o = ps[a * CTX:(a + 1) * CTX, 6, s * DM:(s + 1) * DM]
                    for k in range(KD):
                        pe.matmul(o, ctxt[:, k, s * CTX:(s + 1) * CTX], wv[:, k, a * DM:(a + 1) * DM],
                                  start=(k == 0), stop=False)
                    last = pe.matmul(o, ones[0:1, 0:CTX], row[0:1, a, :], start=False, stop=True)
            last.then_inc(setup_pe.sem, 1)

            def transposes(bank, src, tiles, sig):
                for t in range(tiles):
                    last = pe.transpose(ps[:, bank, t * P:(t + 1) * P], src(t), ident[:, :])
                last.then_inc(sig.sem, 1)

            def mixer(j, kind, n):
                if kind == "pre" and n == 1:
                    if is_first(j):
                        pe.wait_ge(ident_set.sem, 1)
                        pe.wait_ge(w_mix.sem, 4 * 16)
                        pe.wait_ge(conv_set.sem, 1)
                    pe.wait_ge(*xn_done.at(j, 1))
                    for k in range(KD):
                        transposes(k, lambda t: xn[:, t, k * P:(k + 1) * P], NT, xnt_ps)
                if kind == "pre" and n == 2:
                    pe.wait_ge(*xnt_done.at(j, KD))
                    for m in range(2 * Q):
                        if m == 2:
                            pe.wait_ge(*res_done.at(j, 0))
                        if m >= Q:
                            pe.wait_ge(*xi_done.at(j, m - Q + 1))
                        for k in range(KD):
                            last = pe.matmul(ps[:, m % 4, :], win[:, k, m * P:(m + 1) * P], xnt[:, k, :],
                                             start=(k == 0), stop=(k == KD - 1))
                        last.then_inc(xz_ps.sem, 1)
                if kind == "pre" and n == 3:
                    pe.wait_ge(*hist_in.at(j, 1))
                    for q in range(Q):
                        pe.wait_ge(*sz_done.at(j, q + 1))
                        for k in range(TAPS):
                            last = pe.matmul(ps[:, q, :], conv[:, q, k, :], xi[:, q, k:k + TC],
                                             start=(k == 0), stop=(k == TAPS - 1))
                        last.then_inc(conv_ps.sem, 1)
                if kind == "pre" and n == 4:
                    pe.wait_ge(*u_done.at(j, Q))
                    for s in range(2):
                        for q in range(Q):
                            last = pe.matmul(ps[32 * s:32 * s + NS, 2 + s, :], wxp[:, q, s * NS:(s + 1) * NS], u[:, q, :],
                                             start=(q == 0), stop=(q == Q - 1))
                        last.then_inc(xp_ps.sem, 1)
                    for t in range(NT):
                        for q in range(Q):
                            last = pe.matmul(ps[:, 0, t * NS:(t + 1) * NS], u[:, q, t * P:(t + 1) * P],
                                             wxp[:, q, 2 * NS:3 * NS], start=(q == 0), stop=(q == Q - 1))
                    last.then_inc(xp_ps.sem, 1)
                if kind == "pre" and n == 5:
                    if is_first(j):
                        pe.wait_ge(w_att.sem, 6 * 16)
                        pe.wait_ge(kv_done.sem, 2)
                    pe.wait_ge(*dtr_done.at(j, 1))
                    pe.wait_ge(*brow_done.at(j, 1))
                    pe.wait_ge(*ctok_done.at(j, 1))
                    for q in range(Q):
                        pe.matmul(ps[:, (1 + q) % 4, :], wdt[:, q * P:(q + 1) * P], dtr,
                                  start=True, stop=True).then_inc(dp_ps.sem, 1)
                if kind == "scan" and 2 <= n < 2 * NS + 2:
                    state_rows(j, *divmod(n - 2, 2))
                if kind == "post" and n == 0:
                    for t in range(NT):
                        pe.wait_ge(*y_done.at(j, (NS - 1) * NT + t + 1))
                    for q in range(Q):
                        transposes(q, lambda t: yacc[:, t, q * P:(q + 1) * P], NT, yt_ps)
                if kind == "post" and n == 1:
                    for t in range(NT):
                        for q in range(Q):
                            if t == 0:
                                pe.wait_ge(*yg_done.at(j, q + 1))
                            last = pe.matmul(ps[:, 2 + t // 2, t % 2 * DM:(t % 2 + 1) * DM], v[:, q, t * P:(t + 1) * P],
                                             wout[:, q, :], start=(q == 0), stop=(q == Q - 1))
                        last.then_inc(out_ps.sem, 1)

            def state_rows(j, n, half):
                for t in range(2 * half, 2 * half + 2):
                    pe.wait_ge(*scan_done.at(j, Q * (n + 1)))
                    pe.wait_ge(*y_done.at(j, max(0, n * NT + t - 1)))
                    transposes(2 + t % 2, lambda q: hs[:, n % 2, q, t * P:(t + 1) * P], Q, ht_ps)

            def second(j, t, early):
                (second_early if early else second_late)(j, t)

            def second_early(j, t):
                if t == T_X1T:
                    pe.wait_ge(*x1_done.at(j, NT))
                    pe.wait_ge(*xo_done.at(j, 0))
                    pe.wait_ge(*hh_done.at(j, 0))
                    for k in range(KD):
                        transposes(4 + k, lambda t: x1[:, t, k * P:(k + 1) * P], NT, x1t_ps)
                if t in (T_Q, T_Q + 1):
                    pe.wait_ge(*x1t_done.at(j, KD))
                    for b in range(2 * (t - T_Q), 2 * (t - T_Q) + 2):
                        for s, w in enumerate((wq, wqs)):
                            o = 2 * b + s
                            if o >= 4:
                                pe.wait_ge(*rot_done.at(j, o - 3))
                            for k in range(KD):
                                last = pe.matmul(ps[:, 4 + (2 + o) % 4, :], w[:, k, b * P:(b + 1) * P], x1t[:, k, :],
                                                 start=(k == 0), stop=(k == KD - 1))
                            last.then_inc(q_ps.sem, 1)
                for tile in range(NT):
                    if t == T_S + 2 * tile:
                        pe.wait_ge(*q_done.at(j, HB))
                        if tile:
                            pe.wait_ge(*sub_done.at(j, tile))
                        if tile >= 2:
                            pe.wait_ge(*ont_done.at(j, tile - 1))
                        for b in range(HB):
                            last = pe.matmul(ps[:, 4 + b // 2, b % 2 * 2 * KEYS:(b % 2 + 1) * 2 * KEYS],
                                             qr[:, b, tile * P:(tile + 1) * P],
                                             kblk[:, bass.ds(j // CPS, 1), b * 2 * KEYS:(b + 1) * 2 * KEYS]
                                             .rearrange("p a n -> p (a n)"), start=True, stop=True)
                        last.then_inc(s_ps.sem, 1)
                c = t - T_EXP
                if 0 <= c < 2 * ALL:
                    e, ib = divmod(c, 2)
                    if ib == 0:
                        pe.wait_ge(*we_in[e % WRING].at(j, 16 * (e // WRING + 1)))
                    pe.wait_ge(*th_done.at(j, c))
                    gate_rows(j, e, ib, 0, a_ps)
                if 0 <= c - 1 < 2 * ALL:
                    pe.wait_ge(*hh_done.at(j, c - 1))
                    gate_rows(j, *divmod(c - 1, 2), 1, b_ps)

            def gate_rows(j, e, ib, s, sig):
                for k in range(KD):
                    last = pe.matmul(ps[:, 4 + s, :], we[:, e % WRING, s, k * DM + ib * P:k * DM + (ib + 1) * P],
                                     x2t[:, k, :], start=(k == 0), stop=(k == KD - 1))
                last.then_inc(sig.sem, 1)

            def second_late(j, t):
                for tile in range(NT):
                    if t == T_PT + 2 * tile:
                        pe.wait_ge(*p_done.at(j, tile + 1))
                        pe.wait_ge(*rot_done.at(j, 2 * HB))
                        pe.wait_ge(*on_done.at(j, tile))
                        if tile >= 2:
                            pe.wait_ge(*xa_done.at(j, tile - 1))
                        for h in range(HEADS):
                            last = pe.transpose(ps[:, 6 + h // 4, h % 4 * P:(h % 4 + 1) * P],
                                                prob[:, h * KEYS:(h + 1) * KEYS], ident[:, :])
                        last.then_inc(pt_ps.sem, 1)
                    if t == T_PT + 2 * tile + 1:
                        pe.wait_ge(*pt_done.at(j, tile + 1))
                        for h in range(HEADS):
                            c = slice(h * (HD + 1), (h + 1) * (HD + 1))
                            last = pe.matmul(ps[:, 6, c], probt[:, h * P:(h + 1) * P],
                                             vx[:, bass.ds(j // CPS, 1), c].rearrange("p a n -> p (a n)"),
                                             start=True, stop=True)
                        last.then_inc(av_ps.sem, 1)
                    if t == T_PT + 2 * tile + 2:
                        pe.wait_ge(*on_done.at(j, tile + 1))
                        pe.wait_ge(*sub_done.at(j, min(tile + 2, NT)))
                        transposes(5, lambda k: on[:, k * P:(k + 1) * P], KD, ont_ps)
                    if t == T_PT + 2 * tile + 3:
                        pe.wait_ge(*ont_done.at(j, tile + 1))
                        pe.wait_ge(*pt_done.at(j, min(tile + 2, NT)))
                        for k in range(KD):
                            pe.matmul(ps[:, 7, 0:DM], ont[:, k, :], wo[:, k, :], start=(k == 0), stop=False)
                        pe.matmul(ps[:, 7, 0:DM], ones[0:1, :], row[0:1, 2, :], start=False, stop=True
                                  ).then_inc(ao_ps.sem, 1)
                if t == T_LNT:
                    pe.wait_ge(*xl_done.at(j, NT))
                    for k in range(KD):
                        transposes(4 + k, lambda t: xa[:, t, k * P:(k + 1) * P], NT, xlt_ps)
                if t == T_FFN:
                    pe.wait_ge(*xlt_done.at(j, KD))
                    for tile in range(NT):
                        o = ps[:, 6 + tile // 2, tile % 2 * DM:(tile % 2 + 1) * DM]
                        for k in range(KD):
                            pe.matmul(o, x1t[:, k, tile * P:(tile + 1) * P], wf[:, k, :], start=(k == 0), stop=False)
                        pe.matmul(o, ones[0:1, :], row[0:1, 3, :], start=False, stop=True).then_inc(f_ps.sem, 1)
                if t == T_X2T:
                    pe.wait_ge(*x2_done.at(j, NT))
                    for k in range(KD):
                        transposes(4 + k, lambda t: x2[:, t, k * P:(k + 1) * P], NT, x2t_ps)
                if t == T_GATE:
                    pe.wait_ge(*x2t_done.at(j, KD))
                    for tile in range(NT):
                        for k in range(KD):
                            last = pe.matmul(ps[:, 6, tile * EXPERTS:(tile + 1) * EXPERTS],
                                             x2t[:, k, tile * P:(tile + 1) * P], wgate[:, k, :],
                                             start=(k == 0), stop=(k == KD - 1))
                    last.then_inc(lg_ps.sem, 1)
                if t == T_TOP:
                    pe.wait_ge(*comb_done.at(j, 1))
                    for tile in range(NT):
                        last = pe.transpose(ps[0:ALL, 7, tile * P:(tile + 1) * P], comb[:, tile, :], ident[:, :])
                    last.then_inc(combt_ps.sem, 1)
                if t == T_TOP + 1:
                    pe.wait_ge(*combt_done.at(j, 1))
                    for tile in range(NT):
                        pe.matmul(out_cols(tile), combt[:, tile * P:(tile + 1) * P], b2s[:, :],
                                  start=(tile % 2 == 0), stop=False, skip_group_check=True)
                c = t - T_EXP - 2
                if 0 <= c < 2 * ALL:
                    e, ib = divmod(c, 2)
                    if ib == 0:
                        pe.wait_ge(*w2_in[e % WRING].at(j, 16 * (e // WRING + 1)))
                    pe.wait_ge(*hh_done.at(j, c + 1))
                    for tile in range(NT):
                        last = pe.matmul(out_cols(tile), hh[:, ib, tile * P:(tile + 1) * P],
                                         we[:, e % WRING, 2, ib * DM:(ib + 1) * DM],
                                         start=False, stop=(c == 2 * ALL - 1), skip_group_check=True)
                    last.then_inc(o_ps.sem, 1)

            def out_cols(tile):
                return ps[:, 6 + tile // 2, tile % 2 * DM:(tile % 2 + 1) * DM]

            streams(pe, mixer, second)

        @block.vector
        def _(dve):
            dve.wait_ge(w_setup.sem, 7 * 16)
            dve.wait_ge(ident_set.sem, 1)
            for q in range(Q):
                for k in range(TAPS):
                    last = dve.tensor_scalar(conv[:, q, k, :], ident[:, :], col("conv_w", q * TAPS + k), None, ALU.mult)
            last.then_inc(conv_set.sem, 1)
            dve.wait_ge(iota_set.sem, 1)
            dve.tensor_copy(iota8[:, :], iota_i[:, :]).then_inc(setup_dve.sem, 1)
            dve.tensor_scalar(half_b1[:, :], col("b1", 0, ALL * KD), 0.5, None, ALU.mult).then_inc(setup_dve.sem, 1)
            dve.wait_ge(setup_act.sem, 2)
            dve.tensor_scalar(neg_a[:, :], neg_a[:, :], -1.0, None, ALU.mult).then_inc(setup_dve.sem, 1)
            dve.tensor_scalar(ratio[:, 1:2], ratio[:, 0:1], 1.0, None, ALU.add).then_inc(setup_dve.sem, 1)
            dve.wait_ge(setup_dve.sem, 4)
            dve.reciprocal(ratio[:, 2:3], ratio[:, 1:2]).then_inc(setup_dve.sem, 1)
            dve.wait_ge(setup_pe.sem, 1)
            for s, bias in enumerate(("bk", "bk_swap")):
                for b in range(HB):
                    last = dve.scalar_tensor_tensor(out=krot[:, s, b, :], in0=ps[:, 4 + s, b * P:(b + 1) * P],
                                                    scalar=col(bias, b), in1=ropek[:, s, :], op0=ALU.add, op1=ALU.mult)
            last.then_inc(setup_dve.sem, 1)
            dve.wait_ge(setup_dve.sem, 6)
            dve.tensor_tensor(ksum, krot[:, 0, :, :], krot[:, 1, :, :], ALU.add).then_inc(setup_dve.sem, 1)
            dve.wait_ge(setup_dve.sem, 7)
            dve.wait_ge(consts.sem, 7 + CHUNKS)
            for s in range(SEQS):
                for g in range(4):
                    r = slice(32 * g, 32 * g + 32)
                    o = kblk[r, s, :].rearrange("p (b n) -> p b n", b=HB)[:, :, g * CTX:(g + 1) * CTX]
                    i = ksum[r, :, s * CTX:(s + 1) * CTX]
                    if g % 2:
                        last = dve.tensor_scalar(o, i, ratio[r, 2:3], None, ALU.mult)
                    else:
                        last = dve.tensor_copy(o, i)
            last.then_inc(kv_done.sem, 1)
            dve.wait_ge(setup_pe.sem, 2)
            for s in range(SEQS):
                last = dve.tensor_copy(vx[:, s, :].rearrange("p (h d) -> p h d", h=HEADS)[:, :, 0:HD],
                                       ps[:, 6, s * DM:(s + 1) * DM].rearrange("p (h d) -> p h d", h=HEADS))
            last.then_inc(kv_done.sem, 1)

            def mixer(j, kind, n):
                if kind == "pre" and n == 0:
                    dve.wait_ge(*sq_done.at(j, 1))
                    dve.tensor_scalar(ms[:, :], ssq[:, :], 1.0 / DM, EPS, ALU.mult, ALU.add).then_inc(ms_done.sem, 1)
                    dve.wait_ge(*hist_out.at(j, 0))
                    dve.wait_ge(*ht_ps.at(j, 0))
                    dve.wait_ge(*carry_done.at(j, 0))
                    dve.tensor_scalar(xi[:, :, 0:TAPS - 1], hist[:, :, :], keep[:, bass.ds(j, 1)], None, ALU.mult
                                      ).then_inc(hist_in.sem, 1)
                    dve.tensor_scalar(carry[:, :, :], carry[:, :, :], keep[:, bass.ds(j, 1)], None, ALU.mult
                                      ).then_inc(carry_kept.sem, 1)
                if kind == "pre" and n == 1:
                    dve.wait_ge(*rms_done.at(j, 1))
                    for t in range(NT):
                        last = dve.tensor_scalar(xn[:, t, :], xn[:, t, :], rms[:, t:t + 1], None, ALU.mult)
                    last.then_inc(xn_done.sem, 1)
                if kind == "pre" and n == 2:
                    for q in range(Q):
                        dve.wait_ge(*xz_ps.at(j, q + 1))
                        dve.tensor_copy(xi[:, q, TAPS - 1:TAPS - 1 + TC], ps[:, q, :]).then_inc(xi_done.sem, 1)
                    dve.wait_ge(*xi_done.at(j, Q))
                    dve.wait_ge(*hist_in.at(j, 1))
                    dve.tensor_copy(hist[:, :, :], xi[:, :, TC:TC + TAPS - 1]).then_inc(hist_out.sem, 1)
                if kind == "pre" and n == 4:
                    dve.wait_ge(*xp_ps.at(j, 3))
                    dve.tensor_copy(ctok[:, :, :].rearrange("p t n -> p (t n)"), ps[:, 0, 0:NT * NS]
                                    ).then_inc(ctok_done.sem, 1)
                if kind == "pre" and n == 5:
                    for q in range(Q):
                        dve.wait_ge(*dp_ps.at(j, q + 1))
                        dve.tensor_scalar(delta[:, q, :], ps[:, (1 + q) % 4, :], col("dt_b", q), LINEAR,
                                          ALU.add, ALU.min).then_inc(ymin_done.sem, 1)
                    for q in range(Q):
                        dve.wait_ge(*ln_done.at(j, q + 1))
                        dve.scalar_tensor_tensor(out=delta[:, q, :], in0=ps[:, (1 + q) % 4, :], scalar=col("dt_b", q),
                                                 in1=delta[:, q, :], op0=ALU.add, op1=ALU.max
                                                 ).then_inc(delta_done.sem, 1)
                    for q in range(Q):
                        dve.wait_ge(*delta_done.at(j, q + 1))
                        dve.tensor_tensor(v[:, q, :], delta[:, q, :], u[:, q, :], ALU.mult).then_inc(v_done.sem, 1)
                if kind == "scan":
                    if 3 <= n < 2 * NS + 3:
                        sum_states(j, *divmod(n - 3, 2))
                    for unit in range(2 * n, min(2 * n + 2, NS * Q)):
                        m, q = divmod(unit, Q)
                        if unit == 0:
                            dve.wait_ge(*conv_ps.at(j, Q))
                            dve.wait_ge(*carry_kept.at(j, 1))
                        dve.wait_ge(*da_done.at(j, unit + 1))
                        dve.wait_ge(*dbu_done.at(j, n + 1))
                        if m >= 2 and q == 0:
                            dve.wait_ge(*ht_ps.at(j, (m - 1) * NT))
                            dve.wait_ge(*carry_done.at(j, m - 1))
                        dve.tensor_tensor_scan(hs[:, m % 2, q, 0:TC], ps[:, unit % 2, :], dbu[:, m % 2, q, :],
                                               carry[:, m, q:q + 1], ALU.mult, ALU.add).then_inc(scan_done.sem, 1)
                if kind == "post" and n == 0:
                    for q in range(Q):
                        dve.wait_ge(*yt_ps.at(j, q + 1))
                        dve.wait_ge(*dbu_done.at(j, 2 * NS))
                        dve.scalar_tensor_tensor(out=v[:, q, :], in0=u[:, q, :], scalar=col("skip", q),
                                                 in1=ps[:, q, :], op0=ALU.mult, op1=ALU.add).then_inc(yd_done.sem, 1)
                    for q in range(Q):
                        dve.wait_ge(*yd_done.at(j, q + 1))
                        dve.tensor_tensor(v[:, q, :], v[:, q, :], sz[:, q, :], ALU.mult).then_inc(yg_done.sem, 1)
                if kind == "post" and n == 2:
                    for t in range(NT):
                        dve.wait_ge(*out_ps.at(j, t // 2 * 2 + 2))
                        if t == 0:
                            dve.wait_ge(*xt_in.at(j, 16))
                        dve.scalar_tensor_tensor(out=x1[:, t, :], in0=xt[:, t, :], scalar=2.0,
                                                 in1=ps[:, 2 + t // 2, t % 2 * DM:(t % 2 + 1) * DM],
                                                 op0=ALU.mult, op1=ALU.add).then_inc(res_done.sem, 1)
                    for t in range(NT):
                        row_stats(j, "x1", x1, t, res_done)
                    deviations(j, "x1")
                if kind == "post" and n == 3:
                    normalise(j, "x1", x1, x1, x1_done)

            def sum_states(j, n, half):
                for t in range(2 * half, 2 * half + 2):
                    c = ctok[:, t, n:n + 1]
                    dve.wait_ge(*ht_ps.at(j, n * NT + t + 1))
                    if n == 0:
                        dve.wait_ge(*ctok_done.at(j, 1))
                        dve.wait_ge(*xz_ps.at(j, 2 * Q))
                        dve.tensor_scalar(yacc[:, t, :], ps[:, 2 + t % 2, :], c, None, ALU.mult).then_inc(y_done.sem, 1)
                    else:
                        dve.wait_ge(*y_done.at(j, (n - 1) * NT + t + 1))
                        dve.scalar_tensor_tensor(out=yacc[:, t, :], in0=ps[:, 2 + t % 2, :], scalar=c,
                                                 in1=yacc[:, t, :], op0=ALU.mult, op1=ALU.add).then_inc(y_done.sem, 1)

            def row_stats(j, k, src, t, before):
                dve.wait_ge(*before.at(j, t + 1))
                dve.bn_stats(stat[k][:, 6 * t:6 * t + 6], src[:, t, :]).then_inc(norm[k]["stats"].sem, 1)

            def deviations(j, k):
                st = stat[k][:, :].rearrange("p (t n) -> p t n", t=NT)
                mean = mv[k][:, :].rearrange("p (t n) -> p t n", t=NT)
                dve.wait_ge(*norm[k]["stats"].at(j, NT))
                spot = ("x1", "xl", "x2", "xo").index(k)
                dve.wait_ge(*norm[k]["held"].at(j, 0))
                dve.memset(carrier[0:1, spot:spot + 1], 0.0).then_inc(norm[k]["held"].sem, 1)
                for t in range(NT):
                    last = dve.bn_aggr(mean[:, t, :], st[:, t, :])
                last.then_inc(norm[k]["aggr"].sem, NT)
                dve.wait_ge(*norm[k]["aggr"].at(j, NT))
                dve.tensor_scalar(ve[k][:, :], mean[:, :, 1], EPS, None, ALU.add).then_inc(norm[k]["ve"].sem, 1)

            def normalise(j, k, src, dst, after):
                mean = mv[k][:, :].rearrange("p (t n) -> p t n", t=NT)
                dve.wait_ge(*norm[k]["rstd"].at(j, 1))
                for t in range(NT):
                    dve.tensor_scalar(dst[:, t, :], src[:, t, :], mean[:, t, 0:1], rstd[k][:, t:t + 1],
                                      ALU.subtract, ALU.mult).then_inc(after.sem, 1)

            def second(j, t, early):
                (second_early if early else second_late)(j, t)

            def second_early(j, t):
                for tile in range(NT):
                    if t == T_PT + 2 * tile + 2:
                        heads = ps[:, 6, 0:HEADS * (HD + 1)].rearrange("p (h d) -> p h d", h=HEADS)
                        dve.wait_ge(*av_ps.at(j, tile + 1))
                        dve.wait_ge(*on_done.at(j, tile))
                        dve.reciprocal(rec[:, :], heads[:, :, HD]).then_inc(rec_done.sem, 1)
                        dve.wait_ge(*rec_done.at(j, tile + 1))
                        dve.wait_ge(*ont_ps.at(j, tile))
                        dve.tensor_tensor(on[:, :].rearrange("p (h d) -> p h d", h=HEADS), heads[:, :, 0:HD],
                                          rec[:, :].rearrange("p (h o) -> p h o", o=1).to_broadcast([P, HEADS, HD]),
                                          ALU.mult).then_inc(on_done.sem, 1)
                    if t == T_PT + 2 * tile + 4:
                        dve.wait_ge(*ao_ps.at(j, tile + 1))
                        if tile == 0:
                            dve.wait_ge(*out_store.at(j, 0))
                        dve.tensor_tensor(xa[:, tile, :], ps[:, 7, 0:DM], x1[:, tile, :], ALU.add
                                          ).then_inc(xa_done.sem, 1)
                        row_stats(j, "xl", xa, tile, xa_done)
                if t == T_RES:
                    deviations(j, "xl")
                if t == T_LNT:
                    normalise(j, "xl", xa, xa, xl_done)
                if t == T_X2:
                    for tile in range(NT):
                        dve.wait_ge(*f_ps.at(j, tile // 2 * 2 + 2))
                        dve.scalar_tensor_tensor(out=x2[:, tile, :], in0=ps[:, 6 + tile // 2, tile % 2 * DM:(tile % 2 + 1) * DM],
                                                 scalar=0.0, in1=x1[:, tile, :], op0=ALU.max, op1=ALU.add
                                                 ).then_inc(f_done.sem, 1)
                    for tile in range(NT):
                        row_stats(j, "x2", x2, tile, f_done)
                    deviations(j, "x2")
                if t == T_X2T:
                    normalise(j, "x2", x2, x2, x2_done)

            def second_late(j, t):
                if t in (T_Q, T_Q + 1):
                    for b in range(2 * (t - T_Q), 2 * (t - T_Q) + 2):
                        for s, bias in enumerate(("bq", "bq_swap")):
                            o = 2 * b + s
                            dve.wait_ge(*q_ps.at(j, o + 1))
                            if o == 0:
                                dve.wait_ge(*rope_in.at(j, 16))
                                dve.wait_ge(*o_ps.at(j, 0))
                            if s == 1:
                                dve.wait_ge(*q_done.at(j, max(0, b - 1)))
                            dve.scalar_tensor_tensor(out=(qtmp[:, b % 2, :] if s else qr[:, b, :]),
                                                     in0=ps[:, 4 + (2 + o) % 4, :], scalar=col(bias, b),
                                                     in1=rope[:, s, :], op0=ALU.add, op1=ALU.mult
                                                     ).then_inc(rot_done.sem, 1)
                for tile in range(NT):
                    if t == T_S + 2 * tile:
                        s8 = ps[:, 4:6, :].rearrange("p a (h n) -> p (a h) n", n=KEYS)
                        dve.wait_ge(*s_ps.at(j, tile + 1))
                        dve.wait_ge(*sub_done.at(j, tile))
                        dve.tensor_reduce(mx[:, :], s8, AX.X, ALU.max).then_inc(mx_done.sem, 1)
                        dve.wait_ge(*mx_done.at(j, tile + 1))
                        dve.wait_ge(*pt_ps.at(j, tile))
                        dve.tensor_tensor(prob.rearrange("p (h n) -> p h n", h=HEADS), s8,
                                          mx[:, :].rearrange("p (h o) -> p h o", o=1).to_broadcast([P, HEADS, KEYS]),
                                          ALU.subtract).then_inc(sub_done.sem, 1)
                if t == T_TOP:
                    top_two(j)
                c = t - T_EXP - 1
                if 0 <= c < 2 * ALL:
                    ib = c % 2
                    gated = gac_done if c < 2 * EXPERTS else ga_done
                    dve.wait_ge(*th_done.at(j, c + 1))
                    dve.wait_ge(*gated.at(j, c + 1))
                    dve.wait_ge(*hh_done.at(j, max(0, c - 1)))
                    dve.scalar_tensor_tensor(out=gm[:, ib, :], in0=th[:, ib, :], scalar=1.0,
                                             in1=(gac if c < 2 * EXPERTS else ga)[:, ib, :],
                                             op0=ALU.add, op1=ALU.mult).then_inc(gm_done.sem, 1)
                    dve.wait_ge(*gm_done.at(j, c + 1))
                    dve.wait_ge(*b_ps.at(j, c + 1))
                    dve.wait_ge(*o_ps.at(j, max(0, c - 1)))
                    dve.scalar_tensor_tensor(out=hh[:, ib, :], in0=ps[:, 5, :], scalar=col("b3", c),
                                             in1=gm[:, ib, :], op0=ALU.add, op1=ALU.mult).then_inc(hh_done.sem, 1)
                if t == T_OUT:
                    for tile in range(NT):
                        dve.wait_ge(*o_ps.at(j, 2 * ALL))
                        dve.tensor_tensor(xa[:, tile, :], ps[:, 6 + tile // 2, tile % 2 * DM:(tile % 2 + 1) * DM],
                                          x2[:, tile, :], ALU.add).then_inc(xo_done.sem, 1)
                    for tile in range(NT):
                        row_stats(j, "xo", xa, tile, xo_done)
                    deviations(j, "xo")
                    normalise(j, "xo", xa, xa, fin_done)

            def top_two(j):
                wide = lambda a: a.to_broadcast([P, NT, EXPERTS])
                dve.wait_ge(*lg_ps.at(j, 1))
                dve.tensor_copy(lg[:, :, :].rearrange("p t e -> p (t e)"), ps[:, 6, 0:NT * EXPERTS]
                                ).then_inc(lg_done.sem, 1)
                dve.wait_ge(*lg_done.at(j, 1))
                dve.memset(carrier[0:1, 4:5], 0.0).then_inc(m8_done.sem, 1)
                for t in range(NT):
                    last = dve.max(m8[:, t, :], lg[:, t, :])
                last.then_inc(m8_done.sem, 1)
                dve.wait_ge(*m8_done.at(j, 2))
                dve.tensor_tensor(ls[:, :, :], lg[:, :, :], wide(m8[:, :, 0:1]), ALU.subtract).then_inc(ls_done.sem, 1)
                for t in range(NT):
                    last = dve.max_index(i8[:, t, :], m8[:, t, :], lg[:, t, :])
                last.then_inc(i8_done.sem, 1)
                dve.wait_ge(*i8_done.at(j, 1))
                dve.tensor_copy(i2[:, :, :], i8[:, :, 0:2]).then_inc(top_done.sem, 1)
                dve.wait_ge(*top_done.at(j, 1))
                for s in range(2):
                    last = dve.tensor_tensor(mk[:, s, :, :],
                                             iota8[:, :].rearrange("p (o e) -> p o e", o=1).to_broadcast([P, NT, EXPERTS]),
                                             wide(i2[:, :, s:s + 1]), ALU.is_equal)
                last.then_inc(top_done.sem, 1)
                dve.wait_ge(*top_done.at(j, 2))
                dve.tensor_tensor(mk2[:, :, :], mk[:, 0, :, :], mk[:, 1, :, :], ALU.add).then_inc(top_done.sem, 1)
                dve.wait_ge(*el_done.at(j, 1))
                dve.tensor_reduce(se[:, :], el[:, :, :], AX.X, ALU.add).then_inc(top_done.sem, 1)
                dve.wait_ge(*top_done.at(j, 4))
                dve.reciprocal(re[:, :], se[:, :]).then_inc(top_done.sem, 1)
                dve.wait_ge(*top_done.at(j, 5))
                dve.tensor_tensor(pr[:, :, :], el[:, :, :], wide(re[:, :].rearrange("p (t o) -> p t o", o=1)), ALU.mult
                                  ).then_inc(top_done.sem, 2)
                dve.wait_ge(*top_done.at(j, 7))
                dve.tensor_tensor(comb[:, :, 0:EXPERTS], pr[:, :, :], mk2[:, :, :], ALU.mult).then_inc(comb_done.sem, 1)

            streams(dve, mixer, second)
        return signals


def _swap(a):
    return a.reshape(*a.shape[:-1], -1, 2)[..., ::-1].reshape(a.shape)


def _pairs(a, t):
    n = a.shape[0]
    return np.concatenate([a.reshape(n, HEADS, HD), t.reshape(n, HEADS, HD)], axis=2).reshape(n, 2 * DM)


def _rope_tables(positions):
    inv = (1.0 / 10000.0 ** (np.arange(0, HD, 2, dtype=np.float32) / np.float32(HD))).astype(np.float32)
    freqs = positions.astype(np.float32)[:, None] * inv[None, :]
    emb = np.concatenate([freqs, freqs], axis=-1).T
    sign = np.where(np.arange(HD) % 2 == 0, -1.0, 1.0).astype(np.float32)[:, None]
    cos, sin = np.cos(emb).astype(np.float32), (np.sin(emb) * sign).astype(np.float32)
    return np.stack([np.tile(cos, (P // HD, 1)), np.tile(sin, (P // HD, 1))])


def _layout(I):
    A = {k: np.asarray(v) for k, v in I.items()}
    a = lambda k: A["L0_attn_" + k]
    c = lambda k: A["L0_xattn_" + k][3]
    f = lambda k: A["L0_ffn_" + k]
    by_row = lambda w: np.ascontiguousarray(w.reshape(-1, P, *w.shape[1:]).swapaxes(0, 1)).reshape(P, -1)
    pair_w = lambda m, n: _pairs(c(m).T, c(n).T)
    pair_b = lambda m, n: _pairs(c(m)[None], c(n)[None])[0]
    bq, bk = pair_b("b_qa", "b_qt"), pair_b("b_ka", "b_kt")
    parts = {
        "norm_w": by_row(a("norm_w")), "conv_w": by_row(a("conv_w")), "conv_b": by_row(a("conv_b")),
        "dt_b": by_row(a("dt_proj_b")), "skip": by_row(a("D")), "A_log": by_row(a("A_log")),
        "bq": by_row(bq), "bq_swap": by_row(_swap(bq)), "bk": by_row(bk), "bk_swap": by_row(_swap(bk)),
        "gamma": by_row(c("gamma")), "beta": by_row(c("beta")),
        "b1": by_row(np.concatenate([f("b1").reshape(-1), f("sb1")])),
        "b3": by_row(np.concatenate([f("b3").reshape(-1), f("sb3")])),
        "gate": np.broadcast_to(c("gating_factor").reshape(1, 1), (P, 1)),
    }
    wq, wk = pair_w("W_qa", "W_qt"), pair_w("W_ka", "W_kt")
    stack = lambda w, s: np.concatenate([f(w), f(s)[None]]).reshape(ALL, KD, P, DM).swapaxes(1, 2)
    experts = np.stack([stack("w1", "sw1"), stack("w3", "sw3"), stack("w2", "sw2")], axis=2).reshape(ALL, P, 3 * KD * DM)
    pos = np.arange(SEQ).reshape(CPS, TC)
    arrays = {
        "x": A["x"].reshape(CHUNKS, NT, P, DM),
        "w_in": a("in_proj_w").T, "w_out": a("out_proj_w").T, "w_xp": a("x_proj_w").T, "w_dt": a("dt_proj_w").T,
        "w_q": wq, "w_qs": _swap(wq), "w_k": wk, "w_ks": _swap(wk),
        "w_v": np.concatenate([c("W_va").T, c("W_vt").T], axis=1),
        "w_o": c("W_o").T, "w_f": c("W_ffn").T, "w_gate": f("gate_w").T,
        "experts": experts, "b2": np.concatenate([f("b2"), f("sb2")[None]]),
        "vecs": np.concatenate([parts[k] for k in VEC], axis=1),
        "rows": np.stack([c("b_va"), c("b_vt"), c("b_o"), c("b_ffn")]).reshape(1, -1),
        "ctx_t": A["ctx_1024"].reshape(SEQS * CTX, DM).T,
        "rope_q": np.stack([_rope_tables(pos[k % CPS]) for k in range(CHUNKS)]),
        "rope_k": _rope_tables(np.tile(np.arange(CTX), SEQS)),
    }
    return {k: np.ascontiguousarray(v) for k, v in arrays.items()}


def kernel(**inputs):
    import concourse.bacc as bacc
    from concourse.bass_utils import run_bass_kernel_spmd

    nc = bacc.Bacc("TRN2", target_bir_lowering=False, num_devices=1)
    arrays = _layout(inputs)
    args = [nc.dram_tensor(f"in_{n}", a.shape, mybir.dt.from_np(a.dtype), kind="ExternalInput").ap()
            for n, a in arrays.items()]
    out = nc.dram_tensor("out", (CHUNKS, NT, P, DM), F32, kind="ExternalOutput").ap()
    block_kernel(nc, *args, out)
    r = run_bass_kernel_spmd(nc, [{f"in_{n}": a for n, a in arrays.items()}], core_ids=[0])
    return r.results[0]["out"].reshape(SEQS, SEQ, DM)
```

```python
from contextlib import ExitStack

import numpy as np

import concourse.bass as bass
from concourse import mybir

F32 = mybir.dt.float32
F32R = mybir.dt.float32r
I32 = mybir.dt.int32
U32 = mybir.dt.uint32
ALU = mybir.AluOpType
ACT = mybir.ActivationFunctionType
AX = mybir.AxisListType

P = 128
SEQS, SEQ = 2, 1024
DM = 256
KD = DM // P
DI = 2 * DM
Q = DI // P
NS = 16
RANK = 16
TAPS = 4
TC = 512
NT = TC // P
CHUNKS = SEQS * SEQ // TC
CPS = SEQ // TC
HEADS, HD = 8, 32
HB = HEADS // 2
CTX = 64
KEYS = 2 * CTX
EXPERTS = 8
ALL = EXPERTS + 1
WRING, CRING = 2, 2
HRING = 3
DRING = 3
EPS = 1e-5
LINEAR = 30.0

VEC = {}
_at = 0
for _name, _n in (("norm_w", KD), ("conv_w", Q * TAPS), ("conv_b", Q), ("dt_b", Q), ("skip", Q), ("A_log", Q * NS),
                  ("bq", HB), ("bk", HB), ("bk_swap", HB), ("gamma", KD), ("beta", KD),
                  ("b1", ALL * KD), ("b3", ALL * KD), ("gate", 1)):
    VEC[_name] = (_at, _at + _n)
    _at += _n
VECS = _at

T_X1T, T_Q, T_ROT, T_S, T_PT = 0, 1, 2, 3, 4
T_RES = T_PT + 2 * (NT - 1) + 4
T_LNT, T_FFN, T_X2, T_X2T, T_GATE, T_TOP = range(T_RES + 1, T_RES + 7)
T_EXP = T_TOP
T_OUT = T_EXP + 2 * ALL + 2
PRE_TICKS = 2
SCAN_TICKS = 2 * NS + 3


def schedule():
    tick = lambda t: [("early", t), ("mid", t), ("late", t)]
    steps = [("setup", 0), ("pre", 1), ("post", 3), ("post", 4), ("pre", 2), ("post", 5), ("pre", 3)] + tick(0)
    steps += [("pre", 4), ("pre", 5), ("early", 1), ("pre", 6), ("late", 1), ("setup", 1)]
    for t in range(2, PRE_TICKS):
        steps += tick(t)
    for s in range(SCAN_TICKS):
        t = PRE_TICKS + s
        steps += [("early", t), ("sum", s), ("mid", t), ("scan", s), ("late", t)]
        if SCAN_TICKS - 12 <= s < SCAN_TICKS - 8:
            steps.append(("fetch", s - SCAN_TICKS + 12))
    for k, t in enumerate(range(PRE_TICKS + SCAN_TICKS, T_OUT + 1)):
        steps += [("post", k)] if k < 3 else []
        steps += tick(t)
    return steps


SCHEDULE = schedule()


class Signal:

    def __init__(self, sem, per):
        self.sem, self.per = sem, per

    def at(self, j, k):
        return self.sem, j * self.per + k + 1


def is_first(j):
    return isinstance(j, int) and j == 0


def block_kernel(nc, x, w_in, w_out, w_xp, w_dt, w_q, w_k, w_ks, w_v, w_o, w_f, w_gate, w13, w2, b2, vecs, rows,
                 ctx_t, rope_q, rope_k, out):
    ctx = ExitStack()
    with ctx:
        def sb(name, shape, dt=F32):
            return ctx.enter_context(nc.sbuf_tensor(name, shape, dt))

        def signal(name, per):
            s = Signal(ctx.enter_context(nc.semaphore(name)), per)
            signals[name] = s
            return s

        signals = {}
        ps = ctx.enter_context(nc.psum_tensor("ps", [P, 8, 512], F32))

        win = sb("win", [P, KD, 2 * DI])
        wout = sb("wout", [P, Q, DM])
        wxp = sb("wxp", [P, Q, P])
        wdt = sb("wdt", [RANK, DI])
        wq = sb("wq", [P, KD, 2 * DM])
        wo = sb("wo", [P, KD, DM])
        wf = sb("wf", [P, KD, DM])
        wgate = sb("wgate", [P, KD, EXPERTS])
        wgate_parts = sb("wgate_parts", [P, KD, 2 * EXPERTS])
        b2s = sb("b2s", [ALL, DM])
        vec = sb("vec", [P, VECS])
        row = sb("row", [1, 2, DM])
        kblk = sb("kblk", [P, SEQS, HB * 2 * KEYS])
        vx = sb("vx", [P, SEQS, HEADS * (HD + 1)])
        ident = sb("ident", [P, P])
        ones = sb("ones", [1, P])
        iota_i = sb("iota_i", [P, EXPERTS], I32)
        iota8 = sb("iota8", [P, EXPERTS])
        keep = sb("keep", [P, CHUNKS])
        power = sb("power", [P, NT])
        neg_a = sb("neg_a", [P, Q * NS])
        half_b1 = sb("half_b1", [P, ALL * KD])
        ratio = sb("ratio", [P, 4])

        xt = sb("xt", [P, NT, DM])
        xn = sb("xn", [P, NT, DM])
        u = sb("u", [P, Q, TC])
        sz = sb("sz", [P, Q, TC])
        delta = sb("delta", [P, Q, TC])
        v = sb("v", [P, Q, TC])
        bbc = sb("bbc", [P, 2, 2, TC])
        dbu = sb("dbu", [P, DRING, 2, TC])
        hs = sb("hs", [P, 2, Q, TC + 4])
        yacc = sb("yacc", [P, NT, DI])
        hist = sb("hist", [P, Q, TAPS - 1])
        carry = sb("carry", [P, NS, Q])
        ctok = sb("ctok", [P, NT, NS])
        rows_t = sb("rows_t", [P, TC])
        dtr, brow = rows_t[0:RANK, :], rows_t[32:32 + NS, :]
        ssq = sb("ssq", [P, NT])
        ms = sb("ms", [P, NT])
        rms = sb("rms", [P, NT])
        xi = hs[:, 1, :, :]
        xnt = yacc[:, NT // 2:NT, :]

        x1 = sb("x1", [P, NT, DM])
        x1t = sb("x1t", [P, KD, TC])
        work = sb("work", [P, 4096 + 1024])
        qr = work[:, 0:2048].rearrange("p (b t) -> p b t", b=HB)
        qs = work[:, 2048:4096].rearrange("p (b t) -> p b t", b=HB)
        prob = work[:, 3072:4096]
        probt = work[:, 4096:5120]
        th = work[:, 0:1024].rearrange("p (a t) -> p a t", a=2)
        ga = work[:, 1024:2048].rearrange("p (a t) -> p a t", a=2)
        gac = work[:, 2048:3072].rearrange("p (a t) -> p a t", a=2)
        gm = work[:, 3072:4096].rearrange("p (a t) -> p a t", a=2)
        hh = work[:, 4096:5120].rearrange("p (a t) -> p a t", a=2)
        rope = sb("rope", [P, 2, TC])
        mx = sb("mx", [P, HEADS])
        top = sb("top", [P, HEADS])
        rec = sb("rec", [P, HEADS])
        on = sb("on", [P, DM])
        ont = sb("ont", [P, KD, P])
        xa = sb("xa", [P, NT, DM])
        x2 = sb("x2", [P, NT, DM])
        x2_hi = sb("x2_hi", [P, KD, TC])
        x2_lo = sb("x2_lo", [P, KD, TC])
        lg = sb("lg", [P, NT, EXPERTS])
        lg_low = sb("lg_low", [P, NT, EXPERTS])
        m8 = sb("m8", [P, NT, 8])
        i8 = sb("i8", [P, NT, 8], U32)
        i2 = sb("i2", [P, NT, 2])
        ls = sb("ls", [P, NT, EXPERTS])
        el = sb("el", [P, NT, EXPERTS])
        se = sb("se", [P, NT])
        re = sb("re", [P, NT])
        pr = sb("pr", [P, NT, EXPERTS])
        mk = sb("mk", [P, 2, NT, EXPERTS])
        mk2 = sb("mk2", [P, NT, EXPERTS])
        comb = sb("comb", [P, NT, ALL])
        combt = sb("combt", [ALL, TC])
        w13s = sb("w13s", [P, HRING, 2, KD, P])
        w13_hi = sb("w13_hi", [P, HRING, 2, KD, P])
        w13_lo = sb("w13_lo", [P, HRING, 2, KD, P])
        w2s = sb("w2s", [P, WRING, KD * DM])
        cbc = sb("cbc", [P, CRING, TC])
        carrier = sb("carrier", [1, 8])
        stat, mv, ve, rstd = ({k: sb(f"{name}_{k}", [P, NT * n]) for k in ("x1", "xl", "x2", "xo")}
                              for name, n in (("stat", 6), ("mv", 2), ("ve", 1), ("rstd", 1)))

        row_v = yacc[0:1, 0, :]
        ctxt = work[:, 0:KD * P].rearrange("p (k n) -> p k n", k=KD)
        ropek = work[:, 256:512].rearrange("p (a n) -> p a n", a=2)
        krot = work[:, 512:1536].rearrange("p (a b n) -> p a b n", a=2, b=HB)
        ksum = work[:, 1536:2048].rearrange("p (b n) -> p b n", b=HB)
        wk = work[:, 2048:3072].rearrange("p (k n) -> p k n", k=KD)
        wks = work[:, 3072:4096].rearrange("p (k n) -> p k n", k=KD)
        wv = work[:, 4096:5120].rearrange("p (k n) -> p k n", k=KD)

        brow_dram = nc.dram_tensor("brow_dram", (NS, TC), F32, kind="Internal").ap()
        comb_dram = nc.dram_tensor("comb_dram", (ALL, TC), F32, kind="Internal").ap()

        def rope_part(s):
            return rope[:, s, :].rearrange("p (o t) -> p o t", o=1).to_broadcast([P, 2, TC])

        def col(name, i=0, n=1):
            a = VEC[name][0] + i
            return vec[:, a:a + n]

        one = lambda name: signal(name, 0)
        w_vec, w_win, w_mix, w_setup, w_att = (one(n) for n in ("w_vec", "w_win", "w_mix", "w_setup", "w_att"))
        consts, ident_set, zeroed, iota_set = one("consts"), one("ident_set"), one("zeroed"), one("iota_set")
        setup_act, setup_dve, setup_pe = one("setup_act"), one("setup_dve"), one("setup_pe")
        kv_zeroed, kv_done, gate_split = one("kv_zeroed"), one("kv_done"), one("gate_split")

        x_in = signal("x_in", 16)
        xt_in = signal("xt_in", 16)
        sq_done = signal("sq_done", 1)
        ms_done = signal("ms_done", 1)
        rms_done = signal("rms_done", 1)
        xn_done = signal("xn_done", 1)
        xnt_ps = signal("xnt_ps", KD)
        xnt_done = signal("xnt_done", KD)
        xz_ps = signal("xz_ps", 2 * Q)
        hist_in = signal("hist_in", 1)
        xi_done = signal("xi_done", Q)
        sz_done = signal("sz_done", Q)
        tap_done = signal("tap_done", Q)
        conv_done = signal("conv_done", (TAPS - 1) * Q)
        hist_out = signal("hist_out", 1)
        u_done = signal("u_done", Q)
        xp_ps = signal("xp_ps", 1)
        rows_done = signal("rows_done", 1)
        ct_ps = signal("ct_ps", 1)
        ctok_done = signal("ctok_done", 1)
        brow_out = signal("brow_out", 16)
        bbc_in = [signal(f"bbc_in{s}", 16 * NS // 4) for s in range(2)]
        dp_ps = signal("dp_ps", Q)
        ymin_done = signal("ymin_done", Q)
        exp_done = signal("exp_done", Q)
        ln_done = signal("ln_done", Q)
        delta_done = signal("delta_done", Q)
        v_done = signal("v_done", Q)
        carry_kept = signal("carry_kept", 1)
        carry_done = signal("carry_done", NS)
        da_done = signal("da_done", NS * Q)
        dbu_done = signal("dbu_done", 2 * NS)
        scan_done = signal("scan_done", NS * Q)
        ht_ps = signal("ht_ps", NS * NT)
        y_done = signal("y_done", NS * NT)
        yt_ps = signal("yt_ps", Q)
        yd_done = signal("yd_done", Q)
        yg_done = signal("yg_done", Q)
        out_ps = signal("out_ps", NT)
        res_done = signal("res_done", NT)
        x1_done = signal("x1_done", NT)

        norm = {k: {s: signal(f"{k}_{s}", n) for s, n in (("stats", NT), ("held", 1), ("aggr", NT), ("ve", 1), ("rstd", 1))}
                for k in ("x1", "xl", "x2", "xo")}

        x1t_ps = signal("x1t_ps", KD)
        x1t_done = signal("x1t_done", KD)
        rope_in = signal("rope_in", 16)
        q_ps = signal("q_ps", HB)
        q_rows = signal("q_rows", HB)
        qs_in = [signal(f"qs_in{s}", 32) for s in range(2)]
        cos_done = signal("cos_done", 2)
        sin_done = signal("sin_done", 2)
        q_done = signal("q_done", 2)
        s_ps = signal("s_ps", NT)
        mx_done = signal("mx_done", NT)
        top_score_done = signal("top_score_done", NT)
        p_done = signal("p_done", NT)
        pt_ps = signal("pt_ps", NT)
        pt_done = signal("pt_done", NT)
        av_ps = signal("av_ps", NT)
        rec_done = signal("rec_done", NT)
        on_done = signal("on_done", NT)
        ont_ps = signal("ont_ps", NT)
        ont_done = signal("ont_done", NT)
        ao_ps = signal("ao_ps", NT)
        xa_done = signal("xa_done", NT)
        xl_done = signal("xl_done", NT)
        xlt_ps = signal("xlt_ps", KD)
        xlt_done = signal("xlt_done", KD)
        f_ps = signal("f_ps", NT)
        f_done = signal("f_done", NT)
        x2_done = signal("x2_done", NT)
        x2t_ps = signal("x2t_ps", KD)
        x2hi_done = signal("x2hi_done", KD)
        x2lo_done = signal("x2lo_done", KD)
        lg_ps = signal("lg_ps", 1)
        lg_low_done = signal("lg_low_done", 1)
        lg_done = signal("lg_done", 1)
        m8_done = signal("m8_done", 2)
        i8_done = signal("i8_done", 1)
        ls_done = signal("ls_done", 1)
        el_done = signal("el_done", 1)
        top_done = signal("top_done", 7)
        comb_done = signal("comb_done", 1)
        combt_ps = signal("combt_ps", 1)
        combt_done = signal("combt_done", 1)
        comb_out = signal("comb_out", 16)
        cbc_in = [signal(f"cbc_in{s}", 16 * len(range(s, EXPERTS, CRING))) for s in range(CRING)]
        w13_in = [signal(f"w13_in{s}", 16 * len(range(s, 2 * ALL, HRING))) for s in range(HRING)]
        hi_done = signal("hi_done", 2 * ALL)
        lo_done = signal("lo_done", 2 * ALL)
        w2_in = [signal(f"w2_in{s}", 16 * len(range(s, ALL, WRING))) for s in range(WRING)]
        a_ps = signal("a_ps", 2 * ALL)
        b_ps = signal("b_ps", 2 * ALL)
        th_done = signal("th_done", 2 * ALL)
        ga_done = signal("ga_done", 2 * ALL)
        gac_done = signal("gac_done", 2 * EXPERTS)
        gm_done = signal("gm_done", 2 * ALL)
        hh_done = signal("hh_done", 2 * ALL)
        o_ps = signal("o_ps", 2 * ALL)
        xo_done = signal("xo_done", NT)
        fin_done = signal("fin_done", NT)
        out_store = signal("out_store", 16)

        block = ctx.enter_context(nc.Block())

        def streams(eng, mixer, second):
            def body(i, first, last):
                for kind, step in SCHEDULE:
                    if kind in ("early", "mid", "late"):
                        if not first:
                            second(i - 1, step, kind)
                    elif kind == "post" and step >= 3:
                        if not first:
                            mixer(i - 1, kind, step)
                    elif kind == "setup":
                        if first:
                            mixer(i, kind, step)
                    elif kind == "fetch" and not last:
                        mixer(i + 1, kind, step)
                    elif not last:
                        mixer(i, kind, step)

            for step in range(4):
                mixer(0, "fetch", step)
            body(0, True, False)
            with eng.Fori(1, CHUNKS, 1) as i:
                body(i, False, False)
            body(CHUNKS, False, True)

        @block.sync
        def _(sp):
            def load_bbc(j, pair):
                if pair >= 2:
                    sp.wait_ge(*dbu_done.at(j, 2 * (2 * pair - 2)))
                sp.dma_start(bbc[:, pair % 2, :, :].rearrange("p a t -> p (a t)"),
                             brow_dram[2 * pair:2 * pair + 2, :].rearrange("a t -> (a t)").partition_broadcast(P)
                             ).then_inc(bbc_in[pair % 2].sem, 16)

            def mixer(j, kind, n):
                if kind == "fetch" and n == 0:
                    sp.wait_ge(*(xnt_ps.at(j, 0)))
                    sp.dma_start(xn[:, :, :], x[bass.ds(j % CHUNKS, 1)].rearrange("a t p d -> p (a t) d")
                                 ).then_inc(x_in.sem, 16)
                if kind == "setup" and n == 0:
                    sp.dma_start(wxp[:, :, :], w_xp.rearrange("(k p) n -> p k n", p=P)).then_inc(w_mix.sem, 16)
                    sp.dma_start(wdt[:, :], w_dt).then_inc(w_mix.sem, 16)
                    sp.dma_start(wout[:, :, :], w_out.rearrange("(k p) n -> p k n", p=P)).then_inc(w_mix.sem, 16)
                    for dst, src in ((ctxt, ctx_t), (wk, w_k), (wks, w_ks), (wv, w_v)):
                        sp.dma_start(dst, src.rearrange("(k p) n -> p k n", p=P)).then_inc(w_setup.sem, 16)
                    sp.dma_start(ropek, rope_k.rearrange("a p n -> p a n")).then_inc(w_setup.sem, 16)
                    sp.dma_start(row_v, rows[:, 0:2 * DM]).then_inc(w_setup.sem, 16)
                    sp.dma_start(row[:, :, :].rearrange("o a n -> o (a n)"), rows[:, 2 * DM:4 * DM]).then_inc(w_setup.sem, 16)
                    for dst, src in ((wq, w_q), (wo, w_o), (wf, w_f), (wgate, w_gate)):
                        sp.dma_start(dst[:, :, :], src.rearrange("(k p) n -> p k n", p=P)).then_inc(w_att.sem, 16)
                    sp.dma_start(b2s[:, :], b2).then_inc(w_att.sem, 16)
                if kind == "pre" and n == 3:
                    sp.wait_ge(*res_done.at(j, 0))
                    sp.dma_start(xt[:, :, :], x[bass.ds(j, 1)].rearrange("a t p d -> p (a t) d")
                                 ).then_inc(xt_in.sem, 16)
                if kind == "pre" and n == 4:
                    sp.wait_ge(*rows_done.at(j, 1))
                    sp.dma_start(brow_dram, brow).then_inc(brow_out.sem, 16)
                    sp.wait_ge(*brow_out.at(j, 16))
                    load_bbc(j, 0)
                    load_bbc(j, 1)
                if kind == "scan" and n % 4 == 3 and (n + 5) // 4 < NS // 2:
                    load_bbc(j, (n + 5) // 4)

            def load_half(j, c):
                if c >= HRING:
                    sp.wait_ge(*lo_done.at(j, c - HRING + 1))
                else:
                    sp.wait_ge(*lo_done.at(j, 0))
                sp.dma_start(w13s[:, c % HRING, :, :, :].rearrange("p s k n -> p (s k n)"), w13[c]
                             ).then_inc(w13_in[c % HRING].sem, 16)

            def load_second(j, e):
                if e >= WRING:
                    sp.wait_ge(*o_ps.at(j, 2 * (e - WRING) + 2))
                else:
                    sp.wait_ge(*o_ps.at(j, 0))
                sp.dma_start(w2s[:, e % WRING, :], w2[e]).then_inc(w2_in[e % WRING].sem, 16)

            def load_comb(j, e):
                g = e - 1
                if g >= CRING:
                    sp.wait_ge(*gac_done.at(j, 2 * (g - CRING) + 2))
                sp.dma_start(cbc[:, g % CRING, :], comb_dram[e, :].partition_broadcast(P)
                             ).then_inc(cbc_in[g % CRING].sem, 16)

            def second(j, t, part):
                if part != "late":
                    return
                if t == 0:
                    sp.wait_ge(*sq_done.at(j + 1, 1))
                    sp.dma_start(rope[:, :, :], rope_q[bass.ds(j, 1)].rearrange("c a p t -> p (c a) t")
                                 ).then_inc(rope_in.sem, 16)
                if t == T_Q:
                    for s in range(2):
                        b = slice(2 * s, 2 * s + 2)
                        sp.wait_ge(*q_rows.at(j, 2 * s + 2))
                        sp.dma_start(qs[0:P:2, b, :], qr[1:P:2, b, :]).then_inc(qs_in[s].sem, 16)
                        sp.dma_start(qs[1:P:2, b, :], qr[0:P:2, b, :]).then_inc(qs_in[s].sem, 16)
                if t == T_LNT:
                    for c in range(HRING):
                        load_half(j, c)
                    for e in range(WRING):
                        load_second(j, e)
                if t == T_TOP:
                    sp.wait_ge(*combt_done.at(j, 1))
                    sp.dma_start(comb_dram, combt[0:ALL, :]).then_inc(comb_out.sem, 16)
                    sp.wait_ge(*comb_out.at(j, 16))
                    for e in range(1, CRING + 1):
                        load_comb(j, e)
                c = t - T_EXP + 1 + HRING
                if HRING <= c < 2 * ALL:
                    load_half(j, c)
                e, odd = divmod(t - T_EXP - 2, 2)
                if 0 <= e < ALL and odd == 0:
                    if 1 <= e and e + CRING < ALL:
                        load_comb(j, e + CRING)
                if 0 <= e < ALL and odd == 1 and e + WRING < ALL:
                    load_second(j, e + WRING)
                if t == T_OUT:
                    sp.wait_ge(*fin_done.at(j, NT))
                    sp.dma_start(out[bass.ds(j, 1)].rearrange("a t p d -> p (a t) d"), xa[:, :, :]
                                 ).then_inc(out_store.sem, 16)

            sp.dma_start(vec[:, :], vecs).then_inc(w_vec.sem, 16)
            sp.dma_start(win[:, :, :], w_in.rearrange("(k p) n -> p k n", p=P)).then_inc(w_win.sem, 16)
            streams(sp, mixer, second)
            sp.wait_ge(*out_store.at(CHUNKS, 0))

        @block.gpsimd
        def _(pool):
            for s in signals.values():
                if s.per:
                    pool.sem_inc(s.sem, 1)
            pool.memset(ident[:, :], 0.0).then_inc(zeroed.sem, 1)
            pool.memset(ones[:, :], 1.0).then_inc(consts.sem, 1)
            pool.memset(power[:, :], -0.5).then_inc(consts.sem, 1)
            for c in range(CHUNKS):
                pool.memset(keep[:, c:c + 1], 0.0 if c % CPS == 0 else 1.0).then_inc(consts.sem, 1)
            pool.memset(carry[:, :, :], 0.0).then_inc(consts.sem, 1)
            pool.memset(hist[:, :, :], 0.0).then_inc(consts.sem, 1)
            pool.memset(comb[:, :, :], 1.0).then_inc(consts.sem, 1)
            pool.iota(iota_i[:, :], pattern=[[1, EXPERTS]], base=0, channel_multiplier=0).then_inc(iota_set.sem, 1)
            pool.wait_ge(zeroed.sem, 1)
            pool.affine_select(out=ident[:, :], in_=ident[:, :], compare_op=ALU.not_equal, fill=1.0,
                               base=0, pattern=[[-1, P]], channel_multiplier=1).then_inc(ident_set.sem, 1)

            def mixer(j, kind, n):
                if kind == "setup" and n == 0:
                    pool.memset(kblk[:, :, :], 0.0).then_inc(kv_zeroed.sem, 1)
                    pool.memset(vx[:, :, :], 1.0).then_inc(kv_zeroed.sem, 1)
                if kind == "fetch" and n == 2:
                    pool.wait_ge(*ms_done.at(j, 1))
                    if is_first(j):
                        pool.wait_ge(consts.sem, 5 + CHUNKS)
                    pool.tensor_tensor(rms[:, :], ms[:, :], power[:, :], ALU.pow).then_inc(rms_done.sem, 1)
                if kind == "pre" and n == 6:
                    inputs(j, 0)
                    inputs(j, 1)
                if kind == "scan" and 1 <= n < 2 * NS - 1:
                    inputs(j, n + 1)
                if kind == "post" and n == 4:
                    rstd_of(j, "x1")

            def inputs(j, i):
                n, h = divmod(i, 2)
                pool.wait_ge(*bbc_in[n // 2 % 2].at(j, 16 * (n // 4 + 1)))
                if i < 2:
                    pool.wait_ge(*v_done.at(j, 2 * i + 2))
                pool.wait_ge(*scan_done.at(j, max(0, 2 * (i - DRING) + 2)))
                pool.tensor_tensor(dbu[:, i % DRING, :, :], v[:, 2 * h:2 * h + 2, :],
                                   bbc[:, n // 2 % 2, n % 2, :].rearrange("p (o t) -> p o t", o=1)
                                   .to_broadcast([P, 2, TC]), ALU.mult).then_inc(dbu_done.sem, 1)

            def rstd_of(j, k):
                pool.wait_ge(*norm[k]["ve"].at(j, 1))
                pool.tensor_tensor(rstd[k][:, :], ve[k][:, :], power[:, :], ALU.pow
                                   ).then_inc(norm[k]["rstd"].sem, 1)

            def second(j, t, part):
                if part == "mid":
                    return
                if part == "early":
                    if t == T_ROT:
                        for s in range(2):
                            b = slice(2 * s, 2 * s + 2)
                            pool.wait_ge(*qs_in[s].at(j, 32))
                            pool.tensor_tensor(qs[:, b, :], qs[:, b, :], rope_part(1), ALU.mult
                                               ).then_inc(sin_done.sem, 1)
                    if t == T_RES:
                        rstd_of(j, "xl")
                    c = t - T_EXP + 1
                    if 0 <= c < 2 * ALL:
                        pool.wait_ge(*hi_done.at(j, c + 1))
                        pool.tensor_tensor(w13_lo[:, c % HRING, :, :, :].bitcast(F32R), w13s[:, c % HRING, :, :, :],
                                           w13_hi[:, c % HRING, :, :, :], ALU.subtract).then_inc(lo_done.sem, 1)
                    c = t - T_EXP - 1
                    if 2 <= c < 2 * ALL:
                        g, ib = divmod(c - 2, 2)
                        pool.wait_ge(*ga_done.at(j, c + 1))
                        pool.wait_ge(*cbc_in[g % CRING].at(j, 16 * (g // CRING + 1)))
                        pool.wait_ge(*gm_done.at(j, c - 1))
                        pool.tensor_tensor(gac[:, ib, :], ga[:, ib, :], cbc[:, g % CRING, :], ALU.mult
                                           ).then_inc(gac_done.sem, 1)
                    return
                if t == T_X2:
                    rstd_of(j, "x2")
                if t == T_OUT:
                    rstd_of(j, "xo")

            streams(pool, mixer, second)

        @block.scalar
        def _(act):
            act.preload_act_table(ACT.Exp)
            act.wait_ge(w_vec.sem, 16)
            act.activation(neg_a[:, :], col("A_log", 0, Q * NS), ACT.Exp).then_inc(setup_act.sem, 1)
            act.activation(ratio[:, 0:1], col("gate"), ACT.Exp, scale=-1.0).then_inc(setup_act.sem, 1)

            def mixer(j, kind, n):
                if kind == "fetch" and n == 1:
                    act.wait_ge(*x_in.at(j, 16))
                    act.wait_ge(*q_done.at(j, 0) if is_first(j) else q_done.at(j - 1, 0))
                    for t in range(NT):
                        last = act.activation(rope[:, t // 2, t % 2 * DM:(t % 2 + 1) * DM], xn[:, t, :], ACT.Square,
                                              accum_out=ssq[:, t:t + 1])
                    last.then_inc(sq_done.sem, 1)
                if kind == "pre" and n == 1:
                    for k in range(KD):
                        act.wait_ge(*xnt_ps.at(j, k + 1))
                        act.activation(xnt[:, k, :], ps[:, k, :], ACT.Copy, scale=col("norm_w", k)
                                       ).then_inc(xnt_done.sem, 1)
                if kind == "pre" and n == 2:
                    act.wait_ge(*yd_done.at(j, 0))
                    for q in range(Q):
                        convolution_start(j, q)
                if kind == "pre" and n == 3:
                    act.wait_ge(*yg_done.at(j, 0))
                    for pair in range(Q // 2):
                        for q in (2 * pair, 2 * pair + 1):
                            act.wait_ge(*xz_ps.at(j, Q + q + 1))
                            act.activation(sz[:, q, :], ps[:, q, :], ACT.Silu).then_inc(sz_done.sem, 1)
                        for q in (2 * pair, 2 * pair + 1):
                            act.wait_ge(*conv_done.at(j, pair * 2 * (TAPS - 1) + 2 * (TAPS - 2) + q % 2 + 1))
                            act.activation(u[:, q, :], u[:, q, :], ACT.Silu).then_inc(u_done.sem, 1)
                if kind == "pre" and n == 4:
                    act.wait_ge(*xp_ps.at(j, 1))
                    act.wait_ge(*brow_out.at(j, 0))
                    act.activation(rows_t[:, :], ps[:, 6, :], ACT.Copy).then_inc(rows_done.sem, 1)
                if kind == "pre" and n == 5:
                    act.preload_act_table(ACT.Exp)
                if kind == "pre" and n == 6:
                    for q in range(Q):
                        act.wait_ge(*ymin_done.at(j, q + 1))
                        act.activation(delta[:, q, :], delta[:, q, :], ACT.Exp).then_inc(exp_done.sem, 1)
                    for q in range(Q):
                        act.wait_ge(*exp_done.at(j, q + 1))
                        act.activation(delta[:, q, :], delta[:, q, :], ACT.Ln, bias=1.0).then_inc(ln_done.sem, 1)
                if kind == "scan":
                    for unit in range(2 * n + 2 if n else 0, min(2 * n + 4, NS * Q)):
                        if unit < Q:
                            act.wait_ge(*delta_done.at(j, unit + 1))
                        m, q = divmod(unit, Q)
                        act.wait_ge(*scan_done.at(j, max(0, unit - 1)))
                        act.activation(ps[:, unit % 2, :], delta[:, q, :], ACT.Exp,
                                       scale=neg_a[:, q * NS + m:q * NS + m + 1]).then_inc(da_done.sem, 1)
                    m = n // 2 - 1
                    if n % 2 == 0 and 0 <= m < NS:
                        act.wait_ge(*scan_done.at(j, Q * (m + 1)))
                        act.activation(carry[:, m, :], hs[:, m % 2, :, TC - 1], ACT.Copy).then_inc(carry_done.sem, 1)

            def convolution_start(j, q):
                act.wait_ge(*xz_ps.at(j, q + 1))
                act.activation(xi[:, q, TAPS - 1:TAPS - 1 + TC], ps[:, q, :], ACT.Copy).then_inc(xi_done.sem, 1)
                act.activation(u[:, q, :], ps[:, q, :], ACT.Identity, scale=col("conv_w", q * TAPS + TAPS - 1),
                               bias=col("conv_b", q)).then_inc(tap_done.sem, 1)

            def second(j, t, part):
                if part == "mid":
                    gate_halves(j, t)
                    return
                if part == "late":
                    if t == T_Q:
                        act.wait_ge(*o_ps.at(j, 0))
                        for b in range(HB):
                            act.wait_ge(*q_ps.at(j, b + 1))
                            act.activation(qr[:, b, :], ps[:, 4 + b, :], ACT.Identity, bias=col("bq", b)
                                           ).then_inc(q_rows.sem, 1)
                    if t == T_X1T:
                        for k in range(KD):
                            act.wait_ge(*x1t_ps.at(j, k + 1))
                            act.activation(x1t[:, k, :], ps[:, 4 + k, :], ACT.Copy).then_inc(x1t_done.sem, 1)
                    if t == T_TOP:
                        act.wait_ge(*combt_ps.at(j, 1))
                        act.wait_ge(*comb_out.at(j, 0))
                        act.activation(combt[:, :], ps[0:ALL, 7, :], ACT.Copy).then_inc(combt_done.sem, 1)
                    return
                for tile in range(NT):
                    if t == T_PT + 2 * tile:
                        act.wait_ge(*top_score_done.at(j, tile + 1))
                        act.wait_ge(*pt_ps.at(j, tile))
                        for h in range(HEADS):
                            last = act.activation(prob[:, h * KEYS:(h + 1) * KEYS],
                                                  ps[:, 4 + h // 4, h % 4 * KEYS:(h % 4 + 1) * KEYS], ACT.Exp,
                                                  scale=HD ** -0.5, bias=top[:, h:h + 1])
                        last.then_inc(p_done.sem, 1)
                    if t == T_PT + 2 * tile + 1:
                        act.wait_ge(*pt_ps.at(j, tile + 1))
                        act.wait_ge(*av_ps.at(j, tile))
                        act.activation(probt.rearrange("p (a n) -> p a n", a=2), ps[:, 6:8, :], ACT.Copy
                                       ).then_inc(pt_done.sem, 1)
                    if t == T_PT + 2 * tile + 3:
                        act.wait_ge(*ont_ps.at(j, tile + 1))
                        act.wait_ge(*ao_ps.at(j, tile))
                        act.activation(ont[:, :, :], ps[:, 5, 0:DM].rearrange("p (k n) -> p k n", k=KD), ACT.Copy
                                       ).then_inc(ont_done.sem, 1)
                if t == T_FFN:
                    for k in range(KD):
                        act.wait_ge(*xlt_ps.at(j, k + 1))
                        act.activation(x1t[:, k, :], ps[:, 4 + k, :], ACT.Identity, scale=col("gamma", k),
                                       bias=col("beta", k)).then_inc(xlt_done.sem, 1)
                if t == T_GATE:
                    for k in range(KD):
                        act.wait_ge(*x2t_ps.at(j, k + 1))
                        act.activation(x2_hi[:, k, :].bitcast(F32R), ps[:, 4 + k, :], ACT.Copy).then_inc(x2hi_done.sem, 1)
                c = t - T_EXP + 1
                if 0 <= c < 2 * ALL:
                    act.wait_ge(*w13_in[c % HRING].at(j, 16 * (c // HRING + 1)))
                    act.wait_ge(*b_ps.at(j, max(0, c - HRING + 1)))
                    act.activation(w13_hi[:, c % HRING, :, :, :].bitcast(F32R), w13s[:, c % HRING, :, :, :], ACT.Copy
                                   ).then_inc(hi_done.sem, 1)
            def gate_halves(j, t):
                if t == T_TOP:
                    act.wait_ge(*ls_done.at(j, 1))
                    act.activation(el[:, :, :], ls[:, :, :], ACT.Exp).then_inc(el_done.sem, 1)
                c = t - T_EXP
                if 0 <= c < 2 * ALL:
                    ib = c % 2
                    bias = half_b1[:, c:c + 1]
                    act.wait_ge(*a_ps.at(j, c + 1))
                    act.wait_ge(*gm_done.at(j, max(0, c - 1)))
                    act.activation(ga[:, ib, :], ps[:, 4, :], ACT.Identity, scale=0.5, bias=bias
                                   ).then_inc(ga_done.sem, 1)
                    act.activation(th[:, ib, :], ps[:, 4, :], ACT.Tanh, scale=0.5, bias=bias
                                   ).then_inc(th_done.sem, 1)

            streams(act, mixer, second)

        @block.tensor
        def _(pe):
            def transposes(bank, src, tiles, sig):
                for t in range(tiles):
                    last = pe.transpose(ps[:, bank, t * P:(t + 1) * P], src(t), ident[:, :])
                last.then_inc(sig.sem, 1)

            def mixer(j, kind, n):
                if kind == "setup" and n == 1:
                    pe.wait_ge(w_setup.sem, 7 * 16)
                    for s, w in enumerate((wk, wks)):
                        for b in range(HB):
                            for k in range(KD):
                                last = pe.matmul(ps[:, 4 + s, b * P:(b + 1) * P], w[:, k, b * P:(b + 1) * P], ctxt[:, k, :],
                                                 start=(k == 0), stop=(k == KD - 1))
                    last.then_inc(setup_pe.sem, 1)
                    pe.wait_ge(consts.sem, 5 + CHUNKS)
                    for s in range(SEQS):
                        for a in range(2):
                            o = ps[a * CTX:(a + 1) * CTX, 6, s * DM:(s + 1) * DM]
                            for k in range(KD):
                                pe.matmul(o, ctxt[:, k, s * CTX:(s + 1) * CTX], wv[:, k, a * DM:(a + 1) * DM],
                                          start=(k == 0), stop=False)
                            last = pe.matmul(o, ones[0:1, 0:CTX], row_v[:, a * DM:(a + 1) * DM], start=False, stop=True)
                    last.then_inc(setup_pe.sem, 1)
                if kind == "scan" and n == SCAN_TICKS - 1 and is_first(j):
                    pe.wait_ge(w_att.sem, 5 * 16)
                    pe.wait_ge(kv_done.sem, 2)
                    pe.wait_ge(gate_split.sem, 2)
                if kind == "pre" and n == 1:
                    if is_first(j):
                        pe.wait_ge(ident_set.sem, 1)
                        pe.wait_ge(w_win.sem, 16)
                    pe.wait_ge(*xn_done.at(j, 1))
                    pe.wait_ge(*yd_done.at(j, 0))
                    for k in range(KD):
                        transposes(k, lambda t: xn[:, t, k * P:(k + 1) * P], NT, xnt_ps)
                if kind == "pre" and n == 2:
                    pe.wait_ge(*xnt_done.at(j, KD))
                    for m in range(Q):
                        if m == 2:
                            pe.wait_ge(*res_done.at(j, 0))
                        input_block(j, m)
                if kind == "pre" and n == 3:
                    for m in range(Q, 2 * Q):
                        pe.wait_ge(*tap_done.at(j, m - Q + 1))
                        input_block(j, m)
                if kind == "pre" and n == 4:
                    if is_first(j):
                        pe.wait_ge(w_mix.sem, 3 * 16)
                    for q in range(Q):
                        pe.wait_ge(*u_done.at(j, q + 1))
                        last = pe.matmul(ps[:, 6, :], wxp[:, q, :], u[:, q, :], start=(q == 0), stop=(q == Q - 1))
                    last.then_inc(xp_ps.sem, 1)
                if kind == "pre" and n == 5:
                    pe.wait_ge(*rows_done.at(j, 1))
                    transposes(7, lambda t: rows_t[:, t * P:(t + 1) * P], NT, ct_ps)
                    for q in range(Q):
                        pe.wait_ge(*sz_done.at(j, q + 1))
                        pe.matmul(ps[:, q, :], wdt[:, q * P:(q + 1) * P], dtr,
                                  start=True, stop=True).then_inc(dp_ps.sem, 1)
                    pe.wait_ge(*ctok_done.at(j, 1))
                if kind == "scan" and 2 <= n < 2 * NS + 2:
                    state_rows(j, *divmod(n - 2, 2))
                if kind == "post" and n == 0:
                    for t in range(NT):
                        pe.wait_ge(*y_done.at(j, (NS - 1) * NT + t + 1))
                    for q in range(Q):
                        transposes(q, lambda t: yacc[:, t, q * P:(q + 1) * P], NT, yt_ps)
                if kind == "post" and n == 3:
                    for t in range(NT):
                        for q in range(Q):
                            if t == 0:
                                pe.wait_ge(*yg_done.at(j, q + 1))
                            last = pe.matmul(ps[:, 2 + t // 2, t % 2 * DM:(t % 2 + 1) * DM], v[:, q, t * P:(t + 1) * P],
                                             wout[:, q, :], start=(q == 0), stop=(q == Q - 1))
                        last.then_inc(out_ps.sem, 1)

            def input_block(j, m):
                for k in range(KD):
                    last = pe.matmul(ps[:, m % Q, :], win[:, k, m * P:(m + 1) * P], xnt[:, k, :],
                                     start=(k == 0), stop=(k == KD - 1))
                last.then_inc(xz_ps.sem, 1)

            def state_rows(j, n, half):
                for t in range(2 * half, 2 * half + 2):
                    pe.wait_ge(*scan_done.at(j, Q * (n + 1)))
                    pe.wait_ge(*y_done.at(j, max(0, n * NT + t - 1)))
                    transposes(2 + t % 2, lambda q: hs[:, n % 2, q, t * P:(t + 1) * P], Q, ht_ps)

            def second(j, t, part):
                if part == "early":
                    second_early(j, t)
                if part == "late":
                    second_late(j, t)

            def second_early(j, t):
                if t == T_X1T:
                    pe.wait_ge(*x1_done.at(j, NT))
                    pe.wait_ge(*xo_done.at(j, 0))
                    pe.wait_ge(*hh_done.at(j, 0))
                    for k in range(KD):
                        transposes(4 + k, lambda t: x1[:, t, k * P:(k + 1) * P], NT, x1t_ps)
                if t == T_Q:
                    pe.wait_ge(*x1t_done.at(j, KD))
                    for b in range(HB):
                        for k in range(KD):
                            last = pe.matmul(ps[:, 4 + b, :], wq[:, k, b * P:(b + 1) * P], x1t[:, k, :],
                                             start=(k == 0), stop=(k == KD - 1))
                        last.then_inc(q_ps.sem, 1)
                for tile in range(NT):
                    if t == T_S + 2 * tile:
                        pe.wait_ge(*q_done.at(j, 2))
                        if tile:
                            pe.wait_ge(*p_done.at(j, tile))
                        if tile >= 2:
                            pe.wait_ge(*ont_done.at(j, tile - 1))
                        for b in range(HB):
                            last = pe.matmul(ps[:, 4 + b // 2, b % 2 * 2 * KEYS:(b % 2 + 1) * 2 * KEYS],
                                             qr[:, b, tile * P:(tile + 1) * P],
                                             kblk[:, bass.ds(j // CPS, 1), b * 2 * KEYS:(b + 1) * 2 * KEYS]
                                             .rearrange("p a n -> p (a n)"), start=True, stop=True)
                        last.then_inc(s_ps.sem, 1)
                c = t - T_EXP
                if 0 <= c < 2 * ALL:
                    e, ib = divmod(c, 2)
                    pe.wait_ge(*lo_done.at(j, c + 1))
                    pe.wait_ge(*th_done.at(j, c))
                    gate_rows(j, c, 0, a_ps)
                if 0 <= c - 1 < 2 * ALL:
                    pe.wait_ge(*hh_done.at(j, c - 1))
                    gate_rows(j, c - 1, 1, b_ps)

            def gate_rows(j, c, s, sig):
                products(ps[:, 4 + s, :], lambda w, k: w[:, c % HRING, s, k, :], (w13_hi, w13_lo),
                         lambda x, k: x[:, k, :], (x2_hi, x2_lo)).then_inc(sig.sem, 1)

            def products(o, left, ls, right, rs):
                terms = [(ls[0], rs[0]), (ls[1], rs[0]), (ls[0], rs[1])]
                for i, (l, r) in enumerate(terms):
                    for k in range(KD):
                        last = pe.matmul(o, left(l, k).bitcast(F32R), right(r, k).bitcast(F32R),
                                         start=(i == 0 and k == 0), stop=(i == len(terms) - 1 and k == KD - 1))
                return last

            def second_late(j, t):
                for tile in range(NT):
                    if t == T_PT + 2 * tile:
                        pe.wait_ge(*p_done.at(j, tile + 1))
                        pe.wait_ge(*on_done.at(j, tile))
                        if tile >= 2:
                            pe.wait_ge(*xa_done.at(j, tile - 1))
                        for h in range(HEADS):
                            last = pe.transpose(ps[:, 6 + h // 4, h % 4 * P:(h % 4 + 1) * P],
                                                prob[:, h * KEYS:(h + 1) * KEYS], ident[:, :])
                        last.then_inc(pt_ps.sem, 1)
                    if t == T_PT + 2 * tile + 1:
                        pe.wait_ge(*pt_done.at(j, tile + 1))
                        for h in range(HEADS):
                            c = slice(h * (HD + 1), (h + 1) * (HD + 1))
                            last = pe.matmul(ps[:, 6, c], probt[:, h * P:(h + 1) * P],
                                             vx[:, bass.ds(j // CPS, 1), c].rearrange("p a n -> p (a n)"),
                                             start=True, stop=True)
                        last.then_inc(av_ps.sem, 1)
                    if t == T_PT + 2 * tile + 3:
                        pe.wait_ge(*ont_done.at(j, tile + 1))
                        pe.wait_ge(*pt_done.at(j, min(tile + 2, NT)))
                        for k in range(KD):
                            pe.matmul(ps[:, 7, 0:DM], ont[:, k, :], wo[:, k, :], start=(k == 0), stop=False)
                        pe.matmul(ps[:, 7, 0:DM], ones[0:1, :], row[0:1, 0, :], start=False, stop=True
                                  ).then_inc(ao_ps.sem, 1)
                for tile in range(NT):
                    if t == T_PT + 2 * tile + 2:
                        pe.wait_ge(*on_done.at(j, tile + 1))
                        pe.wait_ge(*p_done.at(j, min(tile + 2, NT)))
                        transposes(5, lambda k: on[:, k * P:(k + 1) * P], KD, ont_ps)
                if t == T_LNT:
                    pe.wait_ge(*xl_done.at(j, NT))
                    for k in range(KD):
                        transposes(4 + k, lambda t: xa[:, t, k * P:(k + 1) * P], NT, xlt_ps)
                if t == T_FFN:
                    pe.wait_ge(*xlt_done.at(j, KD))
                    for tile in range(NT):
                        o = ps[:, 6 + tile // 2, tile % 2 * DM:(tile % 2 + 1) * DM]
                        for k in range(KD):
                            pe.matmul(o, x1t[:, k, tile * P:(tile + 1) * P], wf[:, k, :], start=(k == 0), stop=False)
                        pe.matmul(o, ones[0:1, :], row[0:1, 1, :], start=False, stop=True).then_inc(f_ps.sem, 1)
                if t == T_X2T:
                    pe.wait_ge(*x2_done.at(j, NT))
                    for k in range(KD):
                        transposes(4 + k, lambda t: x2[:, t, k * P:(k + 1) * P], NT, x2t_ps)
                if t == T_GATE:
                    pe.wait_ge(*x2lo_done.at(j, KD))
                    for tile in range(NT):
                        for i, (x, n) in enumerate(((x2_hi, 2 * EXPERTS), (x2_lo, EXPERTS))):
                            for k in range(KD):
                                last = pe.matmul(ps[:, 6, tile * 2 * EXPERTS:tile * 2 * EXPERTS + n],
                                                 x[:, k, tile * P:(tile + 1) * P].bitcast(F32R),
                                                 wgate_parts[:, k, 0:n].bitcast(F32R), start=(i == 0 and k == 0),
                                                 stop=(i == 1 and k == KD - 1), skip_group_check=True)
                    last.then_inc(lg_ps.sem, 1)
                if t == T_TOP:
                    pe.wait_ge(*comb_done.at(j, 1))
                    for tile in range(NT):
                        last = pe.transpose(ps[0:ALL, 7, tile * P:(tile + 1) * P], comb[:, tile, :], ident[:, :])
                    last.then_inc(combt_ps.sem, 1)
                if t == T_TOP + 1:
                    pe.wait_ge(*combt_done.at(j, 1))
                    for tile in range(NT):
                        pe.matmul(out_cols(tile), combt[:, tile * P:(tile + 1) * P], b2s[:, :],
                                  start=(tile % 2 == 0), stop=False, skip_group_check=True)
                c = t - T_EXP - 2
                if 0 <= c < 2 * ALL:
                    e, ib = divmod(c, 2)
                    if ib == 0:
                        pe.wait_ge(*w2_in[e % WRING].at(j, 16 * (e // WRING + 1)))
                    pe.wait_ge(*hh_done.at(j, c + 1))
                    for tile in range(NT):
                        last = pe.matmul(out_cols(tile), hh[:, ib, tile * P:(tile + 1) * P],
                                         w2s[:, e % WRING, ib * DM:(ib + 1) * DM],
                                         start=False, stop=(c == 2 * ALL - 1), skip_group_check=True)
                    last.then_inc(o_ps.sem, 1)

            def out_cols(tile):
                return ps[:, 6 + tile // 2, tile % 2 * DM:(tile % 2 + 1) * DM]

            streams(pe, mixer, second)
            pe.wait_ge(*xn_done.at(CHUNKS, 1))

        @block.vector
        def _(dve):
            dve.wait_ge(w_vec.sem, 16)
            dve.wait_ge(iota_set.sem, 1)
            dve.tensor_copy(iota8[:, :], iota_i[:, :]).then_inc(setup_dve.sem, 1)
            dve.tensor_scalar(half_b1[:, :], col("b1", 0, ALL * KD), 0.5, None, ALU.mult).then_inc(setup_dve.sem, 1)
            dve.wait_ge(setup_act.sem, 2)
            dve.tensor_scalar(neg_a[:, :], neg_a[:, :], -1.0, None, ALU.mult).then_inc(setup_dve.sem, 1)
            dve.tensor_scalar(ratio[:, 1:2], ratio[:, 0:1], 1.0, None, ALU.add).then_inc(setup_dve.sem, 1)
            dve.wait_ge(setup_dve.sem, 4)
            dve.reciprocal(ratio[:, 2:3], ratio[:, 1:2]).then_inc(setup_dve.sem, 1)
            def mixer(j, kind, n):
                if kind == "setup" and n == 1:
                    dve.wait_ge(w_setup.sem, 7 * 16)
                    dve.wait_ge(setup_pe.sem, 1)
                    for s, bias in enumerate(("bk", "bk_swap")):
                        for b in range(HB):
                            last = dve.scalar_tensor_tensor(out=krot[:, s, b, :], in0=ps[:, 4 + s, b * P:(b + 1) * P],
                                                            scalar=col(bias, b), in1=ropek[:, s, :], op0=ALU.add, op1=ALU.mult)
                    last.then_inc(setup_dve.sem, 1)
                    dve.wait_ge(setup_dve.sem, 6)
                    dve.tensor_tensor(ksum, krot[:, 0, :, :], krot[:, 1, :, :], ALU.add).then_inc(setup_dve.sem, 1)
                    dve.wait_ge(setup_dve.sem, 7)
                    dve.wait_ge(kv_zeroed.sem, 2)
                    for s in range(SEQS):
                        for g in range(4):
                            r = slice(32 * g, 32 * g + 32)
                            o = kblk[r, s, :].rearrange("p (b n) -> p b n", b=HB)[:, :, g * CTX:(g + 1) * CTX]
                            i = ksum[r, :, s * CTX:(s + 1) * CTX]
                            if g % 2:
                                last = dve.tensor_scalar(o, i, ratio[r, 2:3], None, ALU.mult)
                            else:
                                last = dve.tensor_copy(o, i)
                    last.then_inc(kv_done.sem, 1)
                    dve.wait_ge(setup_pe.sem, 2)
                    for s in range(SEQS):
                        last = dve.tensor_copy(vx[:, s, :].rearrange("p (h d) -> p h d", h=HEADS)[:, :, 0:HD],
                                               ps[:, 6, s * DM:(s + 1) * DM].rearrange("p (h d) -> p h d", h=HEADS))
                    last.then_inc(kv_done.sem, 1)

                    dve.wait_ge(w_att.sem, 5 * 16)
                    dve.tensor_copy(wgate_parts[:, :, 0:EXPERTS].bitcast(F32R), wgate[:, :, :]).then_inc(gate_split.sem, 1)
                    dve.wait_ge(gate_split.sem, 1)
                    dve.tensor_tensor(wgate_parts[:, :, EXPERTS:2 * EXPERTS].bitcast(F32R), wgate[:, :, :], wgate_parts[:, :, 0:EXPERTS], ALU.subtract
                                      ).then_inc(gate_split.sem, 1)
                if kind == "fetch" and n == 2:
                    dve.wait_ge(*sq_done.at(j, 1))
                    dve.tensor_scalar(ms[:, :], ssq[:, :], 1.0 / DM, EPS, ALU.mult, ALU.add).then_inc(ms_done.sem, 1)
                if kind == "pre" and n == 1:
                    dve.wait_ge(*hist_out.at(j, 0))
                    dve.wait_ge(*ht_ps.at(j, 0))
                    dve.wait_ge(*carry_done.at(j, 0))
                    dve.tensor_scalar(xi[:, :, 0:TAPS - 1], hist[:, :, :], keep[:, bass.ds(j, 1)], None, ALU.mult
                                      ).then_inc(hist_in.sem, 1)
                    dve.tensor_scalar(carry[:, :, :], carry[:, :, :], keep[:, bass.ds(j, 1)], None, ALU.mult
                                      ).then_inc(carry_kept.sem, 1)
                if kind == "fetch" and n == 3:
                    if is_first(j):
                        dve.wait_ge(consts.sem, 5 + CHUNKS)
                    dve.wait_ge(*rms_done.at(j, 1))
                    for t in range(NT):
                        last = dve.tensor_scalar(xn[:, t, :], xn[:, t, :], rms[:, t:t + 1], None, ALU.mult)
                    last.then_inc(xn_done.sem, 1)
                if kind == "pre" and n == 2:
                    convolution(j, 0)
                    convolution(j, 1)
                    dve.tensor_copy(hist[:, :, :], xi[:, :, TC:TC + TAPS - 1]).then_inc(hist_out.sem, 1)
                if kind == "pre" and n == 5:
                    dve.wait_ge(*ct_ps.at(j, 1))
                    dve.tensor_copy(ctok[:, :, :], ps[:, 7, :].rearrange("p (t n) -> p t n", t=NT)[:, :, 64:64 + NS]
                                    ).then_inc(ctok_done.sem, 1)
                    for q in range(Q):
                        dve.wait_ge(*dp_ps.at(j, q + 1))
                        dve.tensor_scalar(delta[:, q, :], ps[:, q, :], col("dt_b", q), LINEAR,
                                          ALU.add, ALU.min).then_inc(ymin_done.sem, 1)
                if kind == "pre" and n == 6:
                    for q in range(Q):
                        dve.wait_ge(*ln_done.at(j, q + 1))
                        dve.scalar_tensor_tensor(out=delta[:, q, :], in0=ps[:, q, :], scalar=col("dt_b", q),
                                                 in1=delta[:, q, :], op0=ALU.add, op1=ALU.max
                                                 ).then_inc(delta_done.sem, 1)
                        if q % 2 == 1:
                            for r in (q - 1, q):
                                dve.wait_ge(*delta_done.at(j, r + 1))
                                dve.tensor_tensor(v[:, r, :], delta[:, r, :], u[:, r, :], ALU.mult
                                                  ).then_inc(v_done.sem, 1)
                if kind == "sum" and 3 <= n < 2 * NS + 3:
                    sum_states(j, *divmod(n - 3, 2))
                if kind == "scan":
                    for unit in range(2 * n, min(2 * n + 2, NS * Q)):
                        m, q = divmod(unit, Q)
                        if unit == 0:
                            dve.wait_ge(*carry_kept.at(j, 1))
                        dve.wait_ge(*da_done.at(j, unit + 1))
                        dve.wait_ge(*dbu_done.at(j, n + 1))
                        if m >= 2 and q == 0:
                            dve.wait_ge(*ht_ps.at(j, (m - 1) * NT))
                            dve.wait_ge(*carry_done.at(j, m - 1))
                        dve.tensor_tensor_scan(hs[:, m % 2, q, 0:TC], ps[:, unit % 2, :], dbu[:, n % DRING, q % 2, :],
                                               carry[:, m, q:q + 1], ALU.mult, ALU.add).then_inc(scan_done.sem, 1)
                if kind == "post" and n == 1:
                    for q in range(Q):
                        dve.wait_ge(*yt_ps.at(j, q + 1))
                        dve.wait_ge(*dbu_done.at(j, 2 * NS))
                        dve.scalar_tensor_tensor(out=v[:, q, :], in0=u[:, q, :], scalar=col("skip", q),
                                                 in1=ps[:, q, :], op0=ALU.mult, op1=ALU.add).then_inc(yd_done.sem, 1)
                if kind == "post" and n == 2:
                    for q in range(Q):
                        dve.wait_ge(*yd_done.at(j, q + 1))
                        dve.tensor_tensor(v[:, q, :], v[:, q, :], sz[:, q, :], ALU.mult).then_inc(yg_done.sem, 1)
                if kind == "post" and n == 4:
                    for t in range(NT):
                        dve.wait_ge(*out_ps.at(j, t // 2 * 2 + 2))
                        if t == 0:
                            dve.wait_ge(*xt_in.at(j, 16))
                        dve.scalar_tensor_tensor(out=x1[:, t, :], in0=xt[:, t, :], scalar=2.0,
                                                 in1=ps[:, 2 + t // 2, t % 2 * DM:(t % 2 + 1) * DM],
                                                 op0=ALU.mult, op1=ALU.add).then_inc(res_done.sem, 1)
                    for t in range(NT):
                        row_stats(j, "x1", x1, t, res_done)
                    deviations(j, "x1")
                if kind == "post" and n == 5:
                    normalise(j, "x1", x1, x1, x1_done)

            def convolution(j, pair):
                done = pair * 2 * (TAPS - 1)
                for k in range(TAPS - 1):
                    for q in (2 * pair, 2 * pair + 1):
                        if k == 0:
                            dve.wait_ge(*hist_in.at(j, 1))
                            dve.wait_ge(*xi_done.at(j, q + 1))
                            dve.wait_ge(*tap_done.at(j, q + 1))
                        else:
                            dve.wait_ge(*conv_done.at(j, done - 1))
                        dve.scalar_tensor_tensor(out=u[:, q, :], in0=xi[:, q, k:k + TC], scalar=col("conv_w", q * TAPS + k),
                                                 in1=u[:, q, :], op0=ALU.mult, op1=ALU.add).then_inc(conv_done.sem, 1)
                        done += 1

            def sum_states(j, n, half):
                for t in range(2 * half, 2 * half + 2):
                    c = ctok[:, t, n:n + 1]
                    dve.wait_ge(*ht_ps.at(j, n * NT + t + 1))
                    if n == 0:
                        dve.wait_ge(*ctok_done.at(j, 1))
                        dve.wait_ge(*xz_ps.at(j, 2 * Q))
                        dve.tensor_scalar(yacc[:, t, :], ps[:, 2 + t % 2, :], c, None, ALU.mult).then_inc(y_done.sem, 1)
                    else:
                        dve.wait_ge(*y_done.at(j, (n - 1) * NT + t + 1))
                        dve.scalar_tensor_tensor(out=yacc[:, t, :], in0=ps[:, 2 + t % 2, :], scalar=c,
                                                 in1=yacc[:, t, :], op0=ALU.mult, op1=ALU.add).then_inc(y_done.sem, 1)

            def row_stats(j, k, src, t, before):
                dve.wait_ge(*before.at(j, t + 1))
                dve.bn_stats(stat[k][:, 6 * t:6 * t + 6], src[:, t, :]).then_inc(norm[k]["stats"].sem, 1)

            def deviations(j, k):
                st = stat[k][:, :].rearrange("p (t n) -> p t n", t=NT)
                mean = mv[k][:, :].rearrange("p (t n) -> p t n", t=NT)
                dve.wait_ge(*norm[k]["stats"].at(j, NT))
                spot = ("x1", "xl", "x2", "xo").index(k)
                dve.wait_ge(*norm[k]["held"].at(j, 0))
                dve.memset(carrier[0:1, spot:spot + 1], 0.0).then_inc(norm[k]["held"].sem, 1)
                for t in range(NT):
                    last = dve.bn_aggr(mean[:, t, :], st[:, t, :])
                last.then_inc(norm[k]["aggr"].sem, NT)
                dve.wait_ge(*norm[k]["aggr"].at(j, NT))
                dve.tensor_scalar(ve[k][:, :], mean[:, :, 1], EPS, None, ALU.add).then_inc(norm[k]["ve"].sem, 1)

            def normalise(j, k, src, dst, after):
                mean = mv[k][:, :].rearrange("p (t n) -> p t n", t=NT)
                dve.wait_ge(*norm[k]["rstd"].at(j, 1))
                for t in range(NT):
                    dve.tensor_scalar(dst[:, t, :], src[:, t, :], mean[:, t, 0:1], rstd[k][:, t:t + 1],
                                      ALU.subtract, ALU.mult).then_inc(after.sem, 1)

            def second(j, t, part):
                if part == "mid":
                    second_mid(j, t)
                if part == "late":
                    second_late(j, t)

            def second_mid(j, t):
                for tile in range(NT):
                    if t == T_PT + 2 * tile + 2:
                        heads = ps[:, 6, 0:HEADS * (HD + 1)].rearrange("p (h d) -> p h d", h=HEADS)
                        dve.wait_ge(*av_ps.at(j, tile + 1))
                        dve.wait_ge(*on_done.at(j, tile))
                        dve.reciprocal(rec[:, :], heads[:, :, HD]).then_inc(rec_done.sem, 1)
                        dve.wait_ge(*rec_done.at(j, tile + 1))
                        dve.wait_ge(*ont_ps.at(j, tile))
                        dve.tensor_tensor(on[:, :].rearrange("p (h d) -> p h d", h=HEADS), heads[:, :, 0:HD],
                                          rec[:, :].rearrange("p (h o) -> p h o", o=1).to_broadcast([P, HEADS, HD]),
                                          ALU.mult).then_inc(on_done.sem, 1)
                    if t == T_PT + 2 * tile + 4:
                        dve.wait_ge(*ao_ps.at(j, tile + 1))
                        if tile == 0:
                            dve.wait_ge(*out_store.at(j, 0))
                        dve.tensor_tensor(xa[:, tile, :], ps[:, 7, 0:DM], x1[:, tile, :], ALU.add
                                          ).then_inc(xa_done.sem, 1)
                        row_stats(j, "xl", xa, tile, xa_done)
                if t == T_RES:
                    deviations(j, "xl")
                if t == T_LNT:
                    normalise(j, "xl", xa, xa, xl_done)
                if t == T_X2:
                    relu_rows(j, 0)
                if t == T_X2T:
                    normalise(j, "x2", x2, x2, x2_done)
                if t == T_TOP:
                    top_two(j)
                if t == T_GATE:
                    for k in range(KD):
                        dve.wait_ge(*x2hi_done.at(j, k + 1))
                        dve.tensor_tensor(x2_lo[:, k, :].bitcast(F32R), ps[:, 4 + k, :], x2_hi[:, k, :], ALU.subtract
                                          ).then_inc(x2lo_done.sem, 1)

            def relu_rows(j, half):
                for tile in (2 * half, 2 * half + 1):
                    dve.wait_ge(*f_ps.at(j, 2 * half + 2))
                    dve.scalar_tensor_tensor(out=x2[:, tile, :], in0=ps[:, 6 + half, tile % 2 * DM:(tile % 2 + 1) * DM],
                                             scalar=0.0, in1=x1[:, tile, :], op0=ALU.max, op1=ALU.add
                                             ).then_inc(f_done.sem, 1)

            def second_late(j, t):
                if t == T_X2:
                    relu_rows(j, 1)
                    for tile in range(NT):
                        row_stats(j, "x2", x2, tile, f_done)
                    deviations(j, "x2")
                if t == T_ROT:
                    for s in range(2):
                        b = slice(2 * s, 2 * s + 2)
                        if s == 0:
                            dve.wait_ge(*rope_in.at(j, 16))
                        dve.wait_ge(*qs_in[s].at(j, 32))
                        dve.tensor_tensor(qr[:, b, :], qr[:, b, :], rope_part(0), ALU.mult).then_inc(cos_done.sem, 1)
                    for s in range(2):
                        b = slice(2 * s, 2 * s + 2)
                        dve.wait_ge(*cos_done.at(j, s + 1))
                        dve.wait_ge(*sin_done.at(j, s + 1))
                        dve.tensor_tensor(qr[:, b, :], qr[:, b, :], qs[:, b, :], ALU.add).then_inc(q_done.sem, 1)
                for tile in range(NT):
                    if t == T_S + 2 * tile:
                        s8 = ps[:, 4:6, :].rearrange("p a (h n) -> p (a h) n", n=KEYS)
                        dve.wait_ge(*s_ps.at(j, tile + 1))
                        dve.tensor_reduce(mx[:, :], s8, AX.X, ALU.max).then_inc(mx_done.sem, 1)
                        dve.wait_ge(*mx_done.at(j, tile + 1))
                        dve.wait_ge(*p_done.at(j, tile))
                        dve.tensor_scalar(top[:, :], mx[:, :], -HD ** -0.5, None, ALU.mult
                                          ).then_inc(top_score_done.sem, 1)
                if t == T_TOP:
                    combine_weights(j)
                c = t - T_EXP - 1
                if 0 <= c < 2 * ALL:
                    ib = c % 2
                    dve.wait_ge(*th_done.at(j, c + 1))
                    if c < 2:
                        dve.wait_ge(*ga_done.at(j, c + 1))
                    else:
                        dve.wait_ge(*gac_done.at(j, c - 1))
                    dve.wait_ge(*hh_done.at(j, max(0, c - 1)))
                    dve.scalar_tensor_tensor(out=gm[:, ib, :], in0=th[:, ib, :], scalar=1.0,
                                             in1=(gac if c >= 2 else ga)[:, ib, :],
                                             op0=ALU.add, op1=ALU.mult).then_inc(gm_done.sem, 1)
                    dve.wait_ge(*gm_done.at(j, c + 1))
                    dve.wait_ge(*b_ps.at(j, c + 1))
                    dve.wait_ge(*o_ps.at(j, max(0, c - 1)))
                    dve.scalar_tensor_tensor(out=hh[:, ib, :], in0=ps[:, 5, :], scalar=col("b3", c),
                                             in1=gm[:, ib, :], op0=ALU.add, op1=ALU.mult).then_inc(hh_done.sem, 1)
                if t == T_OUT:
                    for tile in range(NT):
                        dve.wait_ge(*o_ps.at(j, 2 * ALL))
                        dve.tensor_tensor(xa[:, tile, :], ps[:, 6 + tile // 2, tile % 2 * DM:(tile % 2 + 1) * DM],
                                          x2[:, tile, :], ALU.add).then_inc(xo_done.sem, 1)
                    for tile in range(NT):
                        row_stats(j, "xo", xa, tile, xo_done)
                    deviations(j, "xo")
                    normalise(j, "xo", xa, xa, fin_done)

            def wide(a):
                return a.to_broadcast([P, NT, EXPERTS])

            def top_two(j):
                dve.wait_ge(*lg_ps.at(j, 1))
                sums = ps[:, 6, 0:NT * 2 * EXPERTS].rearrange("p (t a e) -> p t a e", t=NT, a=2)
                dve.tensor_copy(lg_low[:, :, :], sums[:, :, 1, :]).then_inc(lg_low_done.sem, 1)
                dve.wait_ge(*lg_low_done.at(j, 1))
                dve.tensor_tensor(lg[:, :, :], sums[:, :, 0, :], lg_low[:, :, :], ALU.add).then_inc(lg_done.sem, 1)
                dve.wait_ge(*lg_done.at(j, 1))
                dve.memset(carrier[0:1, 4:5], 0.0).then_inc(m8_done.sem, 1)
                for t in range(NT):
                    last = dve.max(m8[:, t, :], lg[:, t, :])
                last.then_inc(m8_done.sem, 1)
                dve.wait_ge(*m8_done.at(j, 2))
                dve.tensor_tensor(ls[:, :, :], lg[:, :, :], wide(m8[:, :, 0:1]), ALU.subtract).then_inc(ls_done.sem, 1)
                for t in range(NT):
                    last = dve.max_index(i8[:, t, :], m8[:, t, :], lg[:, t, :])
                last.then_inc(i8_done.sem, 1)
                dve.wait_ge(*i8_done.at(j, 1))
                dve.tensor_copy(i2[:, :, :], i8[:, :, 0:2]).then_inc(top_done.sem, 1)
                dve.wait_ge(*top_done.at(j, 1))
                for s in range(2):
                    last = dve.tensor_tensor(mk[:, s, :, :],
                                             iota8[:, :].rearrange("p (o e) -> p o e", o=1).to_broadcast([P, NT, EXPERTS]),
                                             wide(i2[:, :, s:s + 1]), ALU.is_equal)
                last.then_inc(top_done.sem, 1)
                dve.wait_ge(*top_done.at(j, 2))
                dve.tensor_tensor(mk2[:, :, :], mk[:, 0, :, :], mk[:, 1, :, :], ALU.add).then_inc(top_done.sem, 1)

            def combine_weights(j):
                dve.wait_ge(*el_done.at(j, 1))
                dve.tensor_reduce(se[:, :], el[:, :, :], AX.X, ALU.add).then_inc(top_done.sem, 1)
                dve.wait_ge(*top_done.at(j, 4))
                dve.reciprocal(re[:, :], se[:, :]).then_inc(top_done.sem, 1)
                dve.wait_ge(*top_done.at(j, 5))
                dve.tensor_tensor(pr[:, :, :], el[:, :, :], wide(re[:, :].rearrange("p (t o) -> p t o", o=1)), ALU.mult
                                  ).then_inc(top_done.sem, 2)
                dve.wait_ge(*top_done.at(j, 7))
                dve.tensor_tensor(comb[:, :, 1:ALL], pr[:, :, :], mk2[:, :, :], ALU.mult).then_inc(comb_done.sem, 1)

            streams(dve, mixer, second)
        return signals


def _swap(a):
    return a.reshape(*a.shape[:-1], -1, 2)[..., ::-1].reshape(a.shape)


def _pairs(a, t):
    n = a.shape[0]
    return np.concatenate([a.reshape(n, HEADS, HD), t.reshape(n, HEADS, HD)], axis=2).reshape(n, 2 * DM)


def _rope_tables(positions):
    inv = (1.0 / 10000.0 ** (np.arange(0, HD, 2, dtype=np.float32) / np.float32(HD))).astype(np.float32)
    freqs = positions.astype(np.float32)[:, None] * inv[None, :]
    emb = np.concatenate([freqs, freqs], axis=-1).T
    sign = np.where(np.arange(HD) % 2 == 0, -1.0, 1.0).astype(np.float32)[:, None]
    cos, sin = np.cos(emb).astype(np.float32), (np.sin(emb) * sign).astype(np.float32)
    return np.stack([np.tile(cos, (P // HD, 1)), np.tile(sin, (P // HD, 1))])


def _layout(I):
    A = {k: np.asarray(v) for k, v in I.items()}
    a = lambda k: A["L0_attn_" + k]
    c = lambda k: A["L0_xattn_" + k][3]
    f = lambda k: A["L0_ffn_" + k]
    by_row = lambda w: np.ascontiguousarray(w.reshape(-1, P, *w.shape[1:]).swapaxes(0, 1)).reshape(P, -1)
    pair_w = lambda m, n: _pairs(c(m).T, c(n).T)
    pair_b = lambda m, n: _pairs(c(m)[None], c(n)[None])[0]
    bq, bk = pair_b("b_qa", "b_qt"), pair_b("b_ka", "b_kt")
    parts = {
        "norm_w": by_row(a("norm_w")), "conv_w": by_row(a("conv_w")), "conv_b": by_row(a("conv_b")),
        "dt_b": by_row(a("dt_proj_b")), "skip": by_row(a("D")), "A_log": by_row(a("A_log")),
        "bq": by_row(bq), "bk": by_row(bk), "bk_swap": by_row(_swap(bk)),
        "gamma": by_row(c("gamma")), "beta": by_row(c("beta")),
        "b1": by_row(np.concatenate([f("sb1"), f("b1").reshape(-1)])),
        "b3": by_row(np.concatenate([f("sb3"), f("b3").reshape(-1)])),
        "gate": np.broadcast_to(c("gating_factor").reshape(1, 1), (P, 1)),
    }
    wq, wk = pair_w("W_qa", "W_qt"), pair_w("W_ka", "W_kt")
    stack = lambda w, s: np.concatenate([f(s)[None], f(w)]).reshape(ALL, KD, P, DM).swapaxes(1, 2)
    w13 = np.stack([stack("w1", "sw1"), stack("w3", "sw3")], axis=2).reshape(ALL, P, 2, KD, KD, P)
    w13 = w13.transpose(0, 4, 1, 2, 3, 5).reshape(2 * ALL, P, 2 * KD * P)
    pos = np.arange(SEQ).reshape(CPS, TC)
    arrays = {
        "x": A["x"].reshape(CHUNKS, NT, P, DM),
        "w_in": a("in_proj_w").T, "w_out": a("out_proj_w").T, "w_xp": np.concatenate([m for w, n in zip(np.split(a("x_proj_w").T, (RANK, RANK + NS), axis=1), (32, 32, 64))
                                for m in (w, np.zeros((DI, n - w.shape[1]), w.dtype))], axis=1), "w_dt": a("dt_proj_w").T,
        "w_q": wq, "w_k": wk, "w_ks": _swap(wk),
        "w_v": np.concatenate([c("W_va").T, c("W_vt").T], axis=1),
        "w_o": c("W_o").T, "w_f": c("W_ffn").T, "w_gate": f("gate_w").T,
        "w13": w13, "w2": stack("w2", "sw2").reshape(ALL, P, KD * DM), "b2": np.concatenate([f("sb2")[None], f("b2")]),
        "vecs": np.concatenate([parts[k] for k in VEC], axis=1),
        "rows": np.stack([c("b_va"), c("b_vt"), c("b_o"), c("b_ffn")]).reshape(1, -1),
        "ctx_t": A["ctx_1024"].reshape(SEQS * CTX, DM).T,
        "rope_q": np.stack([_rope_tables(pos[k % CPS]) for k in range(CHUNKS)]),
        "rope_k": _rope_tables(np.tile(np.arange(CTX), SEQS)),
    }
    return {k: np.ascontiguousarray(v) for k, v in arrays.items()}


def kernel(**inputs):
    import concourse.bacc as bacc
    from concourse.bass_utils import run_bass_kernel_spmd

    nc = bacc.Bacc("TRN2", target_bir_lowering=False, num_devices=1)
    arrays = _layout(inputs)
    args = [nc.dram_tensor(f"in_{n}", a.shape, mybir.dt.from_np(a.dtype), kind="ExternalInput").ap()
            for n, a in arrays.items()]
    out = nc.dram_tensor("out", (CHUNKS, NT, P, DM), F32, kind="ExternalOutput").ap()
    block_kernel(nc, *args, out)
    r = run_bass_kernel_spmd(nc, [{f"in_{n}": a for n, a in arrays.items()}], core_ids=[0])
    return r.results[0]["out"].reshape(SEQS, SEQ, DM)
```
